# Optimizing a Trainium2 kernel written in Bass

```python
import numpy as np
import jax
import jax.numpy as jnp

def _softmax(x, axis=-1):
    return jax.nn.softmax(x, axis=axis)

def _gelu(x):
    return jax.nn.gelu(x, approximate=True)

def _silu(x):
    return jax.nn.silu(x)

def _sigmoid(x):
    return jax.nn.sigmoid(x)

def _layernorm(x, axis=-1, eps=1e-05):
    m = jnp.mean(x, axis=axis, keepdims=True)
    v = jnp.var(x, axis=axis, keepdims=True)
    return (x - m) / jnp.sqrt(v + eps)

def _scatter_add(tgt, idx, src, axis=0):
    return tgt.at[idx].add(src)

def _segment_sum(src, seg, n):
    return jax.ops.segment_sum(src, seg, n)
kernel_name = 'mk_decoder_preln_d1_seqx_r4_4030d6'

def setup_inputs(seed: int=0):
    np.random.seed(seed)
    _w = jnp.asarray

    def _rec_inputs():
        import jax
        import jax.numpy as jnp
        _rk = jax.random.key(seed)
        x = -0.0002928 + 1 * jax.random.normal(jax.random.fold_in(_rk, 1), (8, 512, 256), jnp.float32)
        _lenS = 512 - jax.random.randint(jax.random.fold_in(_rk, 7), (8,), 0, max(1, 512 // 4) + 1, jnp.int32)
        _lenS2 = 64 - jax.random.randint(jax.random.fold_in(_rk, 8), (8,), 0, max(1, 64 // 4) + 1, jnp.int32)
        _ctx_1024P = jax.random.normal(jax.random.fold_in(_rk, 11), (8, 16, 256), jnp.float32)
        _ctx_1024c = jax.random.dirichlet(jax.random.fold_in(_rk, 511), 0.3 * jnp.ones((16,), jnp.float32), (8, 64))
        _ctx_1024t = jnp.einsum('bsk,bkd->bsd', _ctx_1024c, _ctx_1024P)
        _ctx_1024t = _ctx_1024t * jax.lax.rsqrt(jnp.mean(jnp.square(_ctx_1024t)) + 1e-12) * 0.953939
        ctx_1024 = -1.39393e-06 + 0.999914 * (_ctx_1024t + 0.3 * jax.random.normal(jax.random.fold_in(_rk, 611), (8, 64, 256), jnp.float32))
        return (x, ctx_1024)
    x, ctx_1024 = _rec_inputs()

    def _L0_attn_setup():
        import jax, jax.numpy as jnp
        import numpy as np
        D_CONV = 4

        def _mamba_fwd(x, W_in, conv_w, conv_b, W_x, W_dt, b_dt, A_log, D_skip, W_out):
            Bsz, L, _ = x.shape
            d_inner, d_state = A_log.shape
            dt_rank = W_dt.shape[1]
            xz = x @ W_in.T
            xc, z = jnp.split(xz, 2, axis=-1)
            xt = xc.transpose(0, 2, 1)
            xt = jax.lax.conv_general_dilated(xt, conv_w, window_strides=(1,), padding=[(D_CONV - 1, 0)], feature_group_count=d_inner, dimension_numbers=('NCH', 'OIH', 'NCH'))
            xc = xt.transpose(0, 2, 1) + conv_b
            xc = jax.nn.silu(xc)
            xc = xc * 0 + 1
            dBC = xc @ W_x.T
            dlt = dBC[..., :dt_rank]
            Bm = dBC[..., dt_rank:dt_rank + d_state]
            Cm = dBC[..., dt_rank + d_state:]
            delta = jax.nn.softplus(dlt @ W_dt.T + b_dt)
            A = -jnp.exp(A_log)

            def step(h, inp):
                x_t, d_t, B_t, C_t = inp
                dA = jnp.exp(d_t[:, :, None] * A)
                dBx = d_t[:, :, None] * B_t[:, None, :] * x_t[:, :, None]
                h = dA * h + dBx
                y_t = jnp.einsum('ben,bn->be', h, C_t)
                return (h, y_t)
            h0 = jnp.zeros((Bsz, d_inner, d_state), x.dtype)
            xs = (xc.transpose(1, 0, 2), delta.transpose(1, 0, 2), Bm.transpose(1, 0, 2), Cm.transpose(1, 0, 2))
            _, ys = jax.lax.scan(step, h0, xs)
            y = ys.transpose(1, 0, 2) + D_skip * xc
            out = y * jax.nn.silu(z) @ W_out.T
            return out
        key = jax.random.key(seed)
        ks = jax.random.split(key, 10)
        d_model, d_inner, d_state, dt_rank = (256, 512, 16, 64)
        B, L = (2, 512)
        s = 0.02
        return {'x': jax.random.normal(ks[0], (B, L, d_model), jnp.float32), 'W_in': jax.random.normal(ks[1], (2 * d_inner, d_model), jnp.float32) * s, 'conv_w': jax.random.normal(ks[2], (d_inner, 1, D_CONV), jnp.float32) * s, 'conv_b': jax.random.normal(ks[3], (d_inner,), jnp.float32) * s, 'W_x': jax.random.normal(ks[4], (dt_rank + 2 * d_state, d_inner), jnp.float32) * s, 'W_dt': jax.random.normal(ks[5], (d_inner, dt_rank), jnp.float32) * s, 'b_dt': jax.random.normal(ks[6], (d_inner,), jnp.float32) * s, 'A_log': jnp.log(jnp.tile(jnp.arange(1, d_state + 1, dtype=jnp.float32), (d_inner, 1))), 'D_skip': jax.random.normal(ks[7], (d_inner,), jnp.float32), 'W_out': jax.random.normal(ks[8], (d_model, d_inner), jnp.float32) * s}
    _L0_attn_all = _L0_attn_setup()
    _L0_attn_in = {k: v for k, v in _L0_attn_all.items() if k in ('W_in', 'conv_w', 'conv_b', 'W_x', 'W_dt', 'b_dt', 'A_log', 'D_skip', 'W_out')}
    del _L0_attn_all

    def _L0_xattn_setup():
        import jax, jax.numpy as jnp
        import numpy as np
        from math import sqrt
        D_MODEL = 256
        N_HEADS = 16
        DK = D_MODEL // N_HEADS
        key = jax.random.key(seed)
        ks = jax.random.split(key, 11)
        B, L, S = (2, 512, 512)
        inp = {'queries': jax.random.normal(ks[0], (B, L, D_MODEL), jnp.float32), 'keys': jax.random.normal(ks[1], (B, S, D_MODEL), jnp.float32), 'values': jax.random.normal(ks[2], (B, S, D_MODEL), jnp.float32), 'Wq': jax.random.normal(ks[3], (D_MODEL, D_MODEL), jnp.float32) * 0.02, 'bq': jnp.zeros((D_MODEL,), jnp.float32), 'Wk': jax.random.normal(ks[4], (D_MODEL, D_MODEL), jnp.float32) * 0.02, 'bk': jnp.zeros((D_MODEL,), jnp.float32), 'Wv': jax.random.normal(ks[5], (D_MODEL, D_MODEL), jnp.float32) * 0.02, 'bv': jnp.zeros((D_MODEL,), jnp.float32), 'Wo': jax.random.normal(ks[6], (D_MODEL, D_MODEL), jnp.float32) * 0.02, 'bo': jnp.zeros((D_MODEL,), jnp.float32)}
        return inp
    _L0_xattn_all = _L0_xattn_setup()
    _L0_xattn_in = {k: v for k, v in _L0_xattn_all.items() if k in ('Wq', 'bq', 'Wk', 'bk', 'Wv', 'bv', 'Wo', 'bo')}
    del _L0_xattn_all

    def _L0_ffn_setup():
        import jax, jax.numpy as jnp
        import numpy as np
        import math
        N_EMBD = 256
        HIDDEN = 4 * N_EMBD
        N_EXPERTS = 8
        TOP_K = 2
        B, T = (4, 512)

        def new_gelu(x):
            c = math.sqrt(2.0 / math.pi)
            return 0.5 * x * (1.0 + jnp.tanh(c * (x + 0.044715 * x * x * x)))

        def _moe_forward(x, Wfc_s, bfc_s, Wproj_s, bproj_s, Wr, Wfc, bfc, Wproj, bproj):
            Bb, Tt, C = x.shape
            xf = x.reshape(Bb * Tt, C)
            N = Bb * Tt
            shared = new_gelu(xf @ Wfc_s + bfc_s) @ Wproj_s + bproj_s
            logits = xf @ Wr
            probs = jax.nn.softmax(logits, axis=-1)
            topk_p, topk_i = jax.lax.top_k(probs, TOP_K)
            topk_p = topk_p / jnp.sum(topk_p, axis=-1, keepdims=True)
            gate = jnp.zeros((N, N_EXPERTS), dtype=xf.dtype)
            gate = gate.at[jnp.arange(N)[:, None], topk_i].add(topk_p)
            routed = jnp.zeros_like(xf)
            for e in range(N_EXPERTS):
                h = new_gelu(xf @ Wfc[e] + bfc[e]) @ Wproj[e] + bproj[e]
                routed = routed + h * gate[:, e:e + 1]
            return (shared + routed).reshape(Bb, Tt, C)
        key = jax.random.key(seed)
        ks = jax.random.split(key, 10)
        s = 0.02
        return {'x': jax.random.normal(ks[0], (B, T, N_EMBD), dtype=jnp.float32), 'Wfc_s': jax.random.normal(ks[1], (N_EMBD, HIDDEN), dtype=jnp.float32) * s, 'bfc_s': jnp.zeros((HIDDEN,), dtype=jnp.float32), 'Wproj_s': jax.random.normal(ks[2], (HIDDEN, N_EMBD), dtype=jnp.float32) * s, 'bproj_s': jnp.zeros((N_EMBD,), dtype=jnp.float32), 'Wr': jax.random.normal(ks[3], (N_EMBD, N_EXPERTS), dtype=jnp.float32) * s, 'Wfc': jax.random.normal(ks[4], (N_EXPERTS, N_EMBD, HIDDEN), dtype=jnp.float32) * s, 'bfc': jnp.zeros((N_EXPERTS, HIDDEN), dtype=jnp.float32), 'Wproj': jax.random.normal(ks[5], (N_EXPERTS, HIDDEN, N_EMBD), dtype=jnp.float32) * s, 'bproj': jnp.zeros((N_EXPERTS, N_EMBD), dtype=jnp.float32)}
    _L0_ffn_all = _L0_ffn_setup()
    _L0_ffn_in = {k: v for k, v in _L0_ffn_all.items() if k in ('Wfc_s', 'bfc_s', 'Wproj_s', 'bproj_s', 'Wr', 'Wfc', 'bfc', 'Wproj', 'bproj')}
    del _L0_ffn_all
    return {'x': x, 'ctx_1024': ctx_1024, 'L0_attn_W_in': _L0_attn_in['W_in'], 'L0_attn_conv_w': _L0_attn_in['conv_w'], 'L0_attn_conv_b': _L0_attn_in['conv_b'], 'L0_attn_W_x': _L0_attn_in['W_x'], 'L0_attn_W_dt': _L0_attn_in['W_dt'], 'L0_attn_b_dt': _L0_attn_in['b_dt'], 'L0_attn_A_log': _L0_attn_in['A_log'], 'L0_attn_D_skip': _L0_attn_in['D_skip'], 'L0_attn_W_out': _L0_attn_in['W_out'], 'L0_xattn_Wq': _L0_xattn_in['Wq'], 'L0_xattn_bq': _L0_xattn_in['bq'], 'L0_xattn_Wk': _L0_xattn_in['Wk'], 'L0_xattn_bk': _L0_xattn_in['bk'], 'L0_xattn_Wv': _L0_xattn_in['Wv'], 'L0_xattn_bv': _L0_xattn_in['bv'], 'L0_xattn_Wo': _L0_xattn_in['Wo'], 'L0_xattn_bo': _L0_xattn_in['bo'], 'L0_ffn_Wfc_s': _L0_ffn_in['Wfc_s'], 'L0_ffn_bfc_s': _L0_ffn_in['bfc_s'], 'L0_ffn_Wproj_s': _L0_ffn_in['Wproj_s'], 'L0_ffn_bproj_s': _L0_ffn_in['bproj_s'], 'L0_ffn_Wr': _L0_ffn_in['Wr'], 'L0_ffn_Wfc': _L0_ffn_in['Wfc'], 'L0_ffn_bfc': _L0_ffn_in['bfc'], 'L0_ffn_Wproj': _L0_ffn_in['Wproj'], 'L0_ffn_bproj': _L0_ffn_in['bproj']}

def reference(x, ctx_1024, L0_attn_W_in, L0_attn_conv_w, L0_attn_conv_b, L0_attn_W_x, L0_attn_W_dt, L0_attn_b_dt, L0_attn_A_log, L0_attn_D_skip, L0_attn_W_out, L0_xattn_Wq, L0_xattn_bq, L0_xattn_Wk, L0_xattn_bk, L0_xattn_Wv, L0_xattn_bv, L0_xattn_Wo, L0_xattn_bo, L0_ffn_Wfc_s, L0_ffn_bfc_s, L0_ffn_Wproj_s, L0_ffn_bproj_s, L0_ffn_Wr, L0_ffn_Wfc, L0_ffn_bfc, L0_ffn_Wproj, L0_ffn_bproj):
    import jax
    import jax.numpy as jnp

    def _L0_attn_ref(x, W_in, conv_w, conv_b, W_x, W_dt, b_dt, A_log, D_skip, W_out):
        import jax, jax.numpy as jnp
        import numpy as np
        D_CONV = 4

        def _mamba_fwd(x, W_in, conv_w, conv_b, W_x, W_dt, b_dt, A_log, D_skip, W_out):
            Bsz, L, _ = x.shape
            d_inner, d_state = A_log.shape
            dt_rank = W_dt.shape[1]
            xz = x @ W_in.T
            xc, z = jnp.split(xz, 2, axis=-1)
            xt = xc.transpose(0, 2, 1)
            xt = jax.lax.conv_general_dilated(xt, conv_w, window_strides=(1,), padding=[(D_CONV - 1, 0)], feature_group_count=d_inner, dimension_numbers=('NCH', 'OIH', 'NCH'))
            xc = xt.transpose(0, 2, 1) + conv_b
            xc = jax.nn.silu(xc)
            xc = xc * 0 + 1
            dBC = xc @ W_x.T
            dlt = dBC[..., :dt_rank]
            Bm = dBC[..., dt_rank:dt_rank + d_state]
            Cm = dBC[..., dt_rank + d_state:]
            delta = jax.nn.softplus(dlt @ W_dt.T + b_dt)
            A = -jnp.exp(A_log)

            def step(h, inp):
                x_t, d_t, B_t, C_t = inp
                dA = jnp.exp(d_t[:, :, None] * A)
                dBx = d_t[:, :, None] * B_t[:, None, :] * x_t[:, :, None]
                h = dA * h + dBx
                y_t = jnp.einsum('ben,bn->be', h, C_t)
                return (h, y_t)
            h0 = jnp.zeros((Bsz, d_inner, d_state), x.dtype)
            xs = (xc.transpose(1, 0, 2), delta.transpose(1, 0, 2), Bm.transpose(1, 0, 2), Cm.transpose(1, 0, 2))
            _, ys = jax.lax.scan(step, h0, xs)
            y = ys.transpose(1, 0, 2) + D_skip * xc
            out = y * jax.nn.silu(z) @ W_out.T
            return out
        return _mamba_fwd(x, W_in, conv_w, conv_b, W_x, W_dt, b_dt, A_log, D_skip, W_out)

    def _L0_xattn_ref(queries, keys, values, Wq, bq, Wk, bk, Wv, bv, Wo, bo):
        import jax, jax.numpy as jnp
        import numpy as np
        from math import sqrt
        D_MODEL = 256
        N_HEADS = 16
        DK = D_MODEL // N_HEADS
        B, L, _ = queries.shape
        S = values.shape[1]
        H, dk = (N_HEADS, DK)
        q = (queries @ Wq + bq).reshape(B, L, H, dk)
        k = (keys @ Wk + bk).reshape(B, S, H, dk)
        v = (values @ Wv + bv).reshape(B, S, H, dk)
        scale = 1.0 / sqrt(dk)
        scores = jnp.einsum('blhd,bshd->bhls', q, k)
        causal = jnp.triu(jnp.ones((L, S), dtype=bool), k=1)
        scores = jnp.where(causal[None, None], -jnp.inf, scores)
        attn = jax.nn.softmax(scores * scale, axis=-1)
        out = jnp.einsum('bhls,bshd->blhd', attn, v).reshape(B, L, H * dk)
        out = out @ Wo + bo
        return out

    def _L0_ffn_ref(x, Wfc_s, bfc_s, Wproj_s, bproj_s, Wr, Wfc, bfc, Wproj, bproj):
        import jax, jax.numpy as jnp
        import numpy as np
        import math
        N_EMBD = 256
        HIDDEN = 4 * N_EMBD
        N_EXPERTS = 8
        TOP_K = 2
        B, T = (4, 512)

        def new_gelu(x):
            c = math.sqrt(2.0 / math.pi)
            return 0.5 * x * (1.0 + jnp.tanh(c * (x + 0.044715 * x * x * x)))

        def _moe_forward(x, Wfc_s, bfc_s, Wproj_s, bproj_s, Wr, Wfc, bfc, Wproj, bproj):
            Bb, Tt, C = x.shape
            xf = x.reshape(Bb * Tt, C)
            N = Bb * Tt
            shared = new_gelu(xf @ Wfc_s + bfc_s) @ Wproj_s + bproj_s
            logits = xf @ Wr
            probs = jax.nn.softmax(logits, axis=-1)
            topk_p, topk_i = jax.lax.top_k(probs, TOP_K)
            topk_p = topk_p / jnp.sum(topk_p, axis=-1, keepdims=True)
            gate = jnp.zeros((N, N_EXPERTS), dtype=xf.dtype)
            gate = gate.at[jnp.arange(N)[:, None], topk_i].add(topk_p)
            routed = jnp.zeros_like(xf)
            for e in range(N_EXPERTS):
                h = new_gelu(xf @ Wfc[e] + bfc[e]) @ Wproj[e] + bproj[e]
                routed = routed + h * gate[:, e:e + 1]
            return (shared + routed).reshape(Bb, Tt, C)
        return _moe_forward(x, Wfc_s, bfc_s, Wproj_s, bproj_s, Wr, Wfc, bfc, Wproj, bproj)
    x = x + _L0_attn_ref(_layernorm(x, axis=-1), L0_attn_W_in, L0_attn_conv_w, L0_attn_conv_b, L0_attn_W_x, L0_attn_W_dt, L0_attn_b_dt, L0_attn_A_log, L0_attn_D_skip, L0_attn_W_out)
    x = x + _L0_xattn_ref(_layernorm(x, axis=-1), ctx_1024, ctx_1024, L0_xattn_Wq, L0_xattn_bq, L0_xattn_Wk, L0_xattn_bk, L0_xattn_Wv, L0_xattn_bv, L0_xattn_Wo, L0_xattn_bo)
    x = x + _L0_ffn_ref(_layernorm(x, axis=-1), L0_ffn_Wfc_s, L0_ffn_bfc_s, L0_ffn_Wproj_s, L0_ffn_bproj_s, L0_ffn_Wr, L0_ffn_Wfc, L0_ffn_bfc, L0_ffn_Wproj, L0_ffn_bproj)
    return x

_drawn_inputs = setup_inputs


def setup_inputs(seed=0):
    import zlib

    import numpy as np

    out = dict(_drawn_inputs(seed))
    spreads = {'L0_xattn_bq': (0.0, 0.8),
     'L0_xattn_bk': (0.0, 2.0),
     'L0_xattn_bv': (0.0, 0.1),
     'L0_xattn_bo': (0.0, 0.1),
     'L0_ffn_bfc_s': (0.0, 0.1),
     'L0_ffn_bproj_s': (0.0, 0.1),
     'L0_ffn_bfc': (0.0, 0.325),
     'L0_ffn_bproj': (0.0, 0.1)}
    factors = {'L0_attn_W_dt': 27.752,
     'L0_attn_b_dt': 62.784,
     'L0_attn_A_log': 64.0,
     'L0_xattn_Wq': 8.0,
     'L0_xattn_Wk': 8.0}
    for name, (base, spread) in spreads.items():
        noise = np.random.default_rng([zlib.crc32(name.encode()), seed]).standard_normal(out[name].shape)
        drawn = base * np.exp(spread * noise) if base else spread * noise
        out[name] = jnp.asarray(drawn.astype(out[name].dtype))
    for name, factor in factors.items():
        out[name] = (out[name] * factor).astype(out[name].dtype)
    return out
```

```python
def build(nc, d, stop=9):
    import concourse.bass as bass
    from concourse import mybir
    from contextlib import ExitStack

    F32, I32 = mybir.dt.float32, mybir.dt.int32
    ALU = mybir.AluOpType
    ACT = mybir.ActivationFunctionType
    AX = mybir.AxisListType.X

    P = 128
    B, L, D = d["x"].shape
    N = B * L
    TILES, TB = N // P, L // P
    KD = D // P
    S = d["ctxT"].shape[2] // B
    EI, NS = d["A_log"].shape
    KE = EI // P
    R = d["W_dtT"].shape[0]
    H = 16
    DK = D // H
    HH = H // KD
    NP = H // 2
    PW = 2 * DK + 2
    E = d["Wfc"].shape[0]
    HID = d["Wfc"].shape[2]
    KH = HID // P
    BLK = 2 * P
    ROOM = N + BLK
    NBR = ROOM // BLK
    ROW = 272
    GATE, TOK = D, D + E
    SCALE = DK ** -0.5
    BIG = 1e30

    out = d["out"]

    ctx = ExitStack()
    with ctx:
        def sb(name, shape, dt=F32):
            return ctx.enter_context(nc.sbuf_tensor(name, shape, dt))

        X = sb("X", [P, TILES, D])
        ident = sb("ident", [P, P])
        tri = sb("tri", [P, P])
        ones = sb("ones", [P, P])
        small = sb("small", [P, 64])
        headmask = small[:, 0:HH]
        tiew = small[:, 8:8 + E]
        rowno = small[:, 16:18]
        ebase = small[:, 24:24 + E]
        eps4, half4 = small[:, 32:32 + TB], small[:, 40:40 + TB]
        causal = sb("causal", [P, HH * S])
        yD = sb("yD", [P, KE, L])
        stats = sb("stats", [P, TB, 6])
        mv = sb("mv", [P, TB, 2])
        vare = sb("vare", [P, TB])
        rstd = sb("rstd", [P, TB])
        hn = sb("hn", [P, TB, D])
        hT = sb("hT", [P, KD, L])
        PS = ctx.enter_context(nc.psum_tensor("PS", [P, 8, 512], F32))

        RG = nc.dram_tensor("routed_rows", [E * ROOM, ROW], F32, kind="Internal").ap()

        class Count:
            def __init__(self, sem):
                self.sem, self.n = sem, 0

            def inc(self, ins, by=1):
                ins.then_inc(self.sem, by)
                self.n += by
                return self.n

        def phase_sems(c, names):
            return [c.enter_context(nc.semaphore(n)) for n in names.split()]

        pool_waits = ctx.enter_context(nc.semaphore("pool_waits"))
        sp_waits = ctx.enter_context(nc.semaphore("sp_waits"))
        bn_waits = ctx.enter_context(nc.semaphore("bn_waits"))

        def pool_wait(pool, sem, value):
            pool.wait_ge(sem, value)
            pool.sem_inc(pool_waits, 1)

        def norm_stats(link, tiles):
            for t, src in enumerate(tiles):
                last = nc.vector.bn_stats(stats[:, t, :], src)
            link(last)
            nc.vector.sem_inc(bn_waits, 1)
            for t in range(len(tiles)):
                last = nc.vector.bn_aggr(mv[:, t, :], stats[:, t, :])
            return last

        def norm_rstd(pool, done, before):
            nc.gpsimd.tensor_tensor(vare[:], mv[:, :, 1], eps4, ALU.add).then_inc(done, 1)
            pool_wait(pool, done, before + 1)
            nc.gpsimd.tensor_tensor(rstd[:], vare[:], half4, ALU.pow).then_inc(done, 1)

        def norm_apply(tiles, dsts):
            for t, src in enumerate(tiles):
                last = nc.vector.tensor_scalar(dsts[t], src, mv[:, t, 0:1], rstd[:, t:t + 1],
                                               ALU.subtract, ALU.mult)
            return last

        with ExitStack() as c:
            def tmp(name, shape, dt=F32):
                return c.enter_context(nc.sbuf_tensor(name, shape, dt))
            wx = tmp("wx", [P, KE, R + 2 * NS])
            wdt = tmp("wdt", [R, EI])
            bdt = tmp("bdt", [P, KE])
            dsk = tmp("dsk", [P, KE])
            alog = tmp("alog", [P, KE, NS])
            steps = tmp("steps", [P, L - 1])
            onesrow = tmp("onesrow", [P, L])
            dlt = tmp("dlt", [R, 1])
            bc = tmp("bc", [P, 2 * NS])
            dl = tmp("dl", [P, 8, KE])
            rate = tmp("rate", [P, KE, NS])
            coef = tmp("coef", [P, KE, NS])
            pw = tmp("pw", [P, 2, L - 1])
            kern = tmp("kern", [P, KE, L])
            (consts_in, x_in, w_in, small_mm, dve_done, act_done, pw_ready, pw_used,
             s_chain) = phase_sems(c, "consts_in x_in w_in small_mm dve_done act_done pw_ready pw_used s_chain")
            with nc.Block() as block:
                @block.sync
                def _(sp):
                    for dst, src in ((wx[:], d["W_xT"].rearrange("(k p) r -> p k r", p=P)),
                                     (wdt[:], d["W_dtT"]), (bdt[:], d["b_dt"]), (dsk[:], d["D_skip"]),
                                     (alog[:], d["A_log"].rearrange("(k p) n -> p k n", p=P)),
                                     (steps[:], d["steps"])):
                        sp.dma_start(dst, src).then_inc(w_in, 16)
                    for dst, src in ((ident[:], d["ident"]), (tri[:], d["tri"]),
                                     (small[:], d["small"]), (causal[:], d["causal"])):
                        sp.dma_start(dst, src).then_inc(consts_in, 16)
                    for b in range(B):
                        sp.dma_start(X[:, b * TB:(b + 1) * TB, :],
                                     d["x"][b].rearrange("(t p) d -> p t d", p=P)).then_inc(x_in, 16)
                    sp.wait_ge(consts_in, 64)
                    sp.wait_ge(x_in, 16 * B)

                @block.tensor
                def _(pe):
                    pe.wait_ge(w_in, 96)
                    pe.wait_ge(dve_done, 1)
                    for k in range(KE):
                        nc.tensor.matmul(PS[0:R, 0, 0:1], wx[:, k, 0:R], ones[:, 0:1],
                                         start=k == 0, stop=k == KE - 1)
                    for k in range(KE):
                        last = nc.tensor.matmul(PS[:, 1, 0:2 * NS], ones[:, :], wx[:, k, R:R + 2 * NS],
                                                start=k == 0, stop=k == KE - 1)
                    last.then_inc(small_mm, 1)
                    pe.wait_ge(dve_done, 2)
                    for k in range(KE):
                        last = nc.tensor.matmul(PS[:, 2, k:k + 1], wdt[:, k * P:(k + 1) * P], dlt[:],
                                                start=True, stop=True)
                    last.then_inc(small_mm, 1)

                @block.vector
                def _(dve):
                    n = [0]
                    def link(ins):
                        n[0] += 1
                        ins.then_inc(s_chain, 1)
                        dve.wait_ge(s_chain, n[0])
                    nc.vector.memset(onesrow[:], 1.0)
                    link(nc.vector.memset(kern[:], 0.0))
                    nc.vector.memset(ones[:], 1.0).then_inc(dve_done, 1)
                    dve.wait_ge(small_mm, 1)
                    nc.vector.tensor_copy(dlt[:], PS[0:R, 0, 0:1]).then_inc(dve_done, 1)
                    link(nc.vector.tensor_copy(bc[:], PS[:, 1, 0:2 * NS]))
                    dve.wait_ge(small_mm, 2)
                    t_, na, ex, u, ln, dlt_ = (dl[:, i, :] for i in range(6))
                    link(nc.vector.tensor_tensor(t_, PS[:, 2, 0:KE], bdt[:], ALU.add))
                    link(nc.vector.tensor_scalar(na, t_, -1.0, None, ALU.mult))
                    link(nc.vector.tensor_tensor(na, na, t_, ALU.min))
                    nc.vector.tensor_scalar(dl[:, 6, :], t_, 0.0, None, ALU.max).then_inc(dve_done, 1)
                    dve.wait_ge(act_done, 1)
                    nc.vector.tensor_scalar(u, ex, 1.0, None, ALU.add).then_inc(dve_done, 1)
                    dve.wait_ge(act_done, 2)
                    nc.vector.tensor_scalar(alog[:], alog[:], 88.7, None, ALU.min).then_inc(dve_done, 1)
                    link(nc.vector.tensor_tensor(ln, ln, ex, ALU.mult))
                    link(nc.vector.tensor_scalar(dl[:, 7, :], u, -1.0, 1e-30, ALU.add, ALU.max))
                    link(nc.vector.reciprocal(dl[:, 7, :], dl[:, 7, :]))
                    link(nc.vector.tensor_tensor(ln, ln, dl[:, 7, :], ALU.mult))
                    link(nc.vector.tensor_scalar(na, u, 1.0, None, ALU.is_equal))
                    link(nc.vector.tensor_tensor(na, na, ex, ALU.mult))
                    link(nc.vector.tensor_tensor(ln, ln, na, ALU.add))
                    link(nc.vector.tensor_tensor(dlt_, ln, dl[:, 6, :], ALU.add))
                    dve.wait_ge(act_done, 3)
                    link(nc.vector.tensor_scalar(rate[:], rate[:], -2.0 ** -40, None, ALU.mult))
                    for k in range(KE):
                        last = nc.vector.tensor_scalar(rate[:, k, :], rate[:, k, :], dlt_[:, k:k + 1],
                                                       None, ALU.mult)
                    link(last)
                    nc.vector.tensor_scalar(rate[:], rate[:], -1e4 * 2.0 ** -40, 2.0 ** 40, ALU.max,
                                            ALU.mult).then_inc(dve_done, 1)
                    link(nc.vector.tensor_tensor(bc[:, 0:NS], bc[:, 0:NS], bc[:, NS:2 * NS], ALU.mult))
                    for k in range(KE):
                        last = nc.vector.tensor_scalar(coef[:, k, :], bc[:, 0:NS], dlt_[:, k:k + 1],
                                                       None, ALU.mult)
                    link(last)
                    link(nc.vector.reduce_sum(kern[:, :, 0], coef[:], axis=AX))
                    for k in range(KE):
                        for m in range(NS):
                            i = k * NS + m
                            dve.wait_ge(pw_ready, i + 1)
                            nc.vector.scalar_tensor_tensor(
                                kern[:, k, 1:L], pw[:, i % 2, :], coef[:, k, m:m + 1], kern[:, k, 1:L],
                                ALU.mult, ALU.add).then_inc(pw_used, 1)
                            dve.wait_ge(pw_used, i + 1)
                    for k in range(KE):
                        last = nc.vector.tensor_tensor_scan(yD[:, k, :], onesrow[:], kern[:, k, :],
                                                            dsk[:, k:k + 1], ALU.mult, ALU.add)
                    link(last)

                @block.scalar
                def _(act):
                    act.wait_ge(dve_done, 3)
                    nc.scalar.activation(dl[:, 2, :], dl[:, 1, :], ACT.Exp).then_inc(act_done, 1)
                    act.wait_ge(dve_done, 4)
                    nc.scalar.activation(dl[:, 4, :], dl[:, 3, :], ACT.Ln).then_inc(act_done, 1)
                    act.wait_ge(dve_done, 5)
                    nc.scalar.activation(rate[:], alog[:], ACT.Exp).then_inc(act_done, 1)
                    act.wait_ge(dve_done, 6)
                    for k in range(KE):
                        for m in range(NS):
                            i = k * NS + m
                            if i >= 2:
                                act.wait_ge(pw_used, i - 1)
                            nc.scalar.activation(pw[:, i % 2, :], steps[:], ACT.Exp,
                                                 scale=rate[:, k, m:m + 1]).then_inc(pw_ready, 1)

        with ExitStack() as c:
            def tmp(name, shape, dt=F32):
                return c.enter_context(nc.sbuf_tensor(name, shape, dt))
            win = tmp("win", [P, KD, EI])
            wout = tmp("wout", [P, KE, D])
            sz = tmp("sz", [P, KE, L])
            g = tmp("g", [P, KE, L])
            (w_in, hn_var, hn_rstd, hn_ready, hT_psum, hT_ready, z_psum, sz_ready, g_ready, o_psum, x1_ready,
             s_chain) = phase_sems(c, "a_w_in a_hn_var a_hn_rstd a_hn_ready a_hT_psum a_hT_ready a_z_psum a_sz_ready a_g_ready a_o_psum a_x1_ready a_chain")
            with nc.Block() as block:
                @block.sync
                def _(sp):
                    sp.dma_start(win[:], d["W_inT"].rearrange("(k p) e -> p k e", p=P)).then_inc(w_in, 16)
                    sp.dma_start(wout[:], d["W_outT"].rearrange("(k p) e -> p k e", p=P)).then_inc(w_in, 16)

                @block.tensor
                def _(pe):
                    def transposes(b):
                        pe.wait_ge(hn_ready, b + 1)
                        for t in range(TB):
                            for k in range(KD):
                                last = nc.tensor.transpose(PS[:, 4 + k, t * P:(t + 1) * P],
                                                           hn[:, t, k * P:(k + 1) * P], ident[:])
                        last.then_inc(hT_psum, 1)

                    def z_part(b):
                        pe.wait_ge(hT_ready, KD * b + KD)
                        for e in range(KE):
                            for k in range(KD):
                                last = nc.tensor.matmul(PS[:, e, :], win[:, k, e * P:(e + 1) * P], hT[:, k, :],
                                                        start=k == 0, stop=k == KD - 1)
                            last.then_inc(z_psum, 1)

                    def out_part(b):
                        pe.wait_ge(g_ready, KE * b + KE)
                        pe.wait_ge(x1_ready, 2 * b + 2)
                        for t in range(TB):
                            for e in range(KE):
                                last = nc.tensor.matmul(PS[:, 6 + t // 2, (t % 2) * D:(t % 2 + 1) * D],
                                                        g[:, e, t * P:(t + 1) * P], wout[:, e, :],
                                                        start=e == 0, stop=e == KE - 1)
                            if t % 2:
                                last.then_inc(o_psum, 1)

                    pe.wait_ge(w_in, 32)
                    transposes(0)
                    with pe.Fori(0, B - 1) as b:
                        z_part(b)
                        transposes(b + 1)
                        out_part(b)
                    z_part(B - 1)
                    out_part(B - 1)

                @block.scalar
                def _(act):
                    def evac(b):
                        act.wait_ge(hT_psum, b + 1)
                        for k in range(KD):
                            nc.scalar.activation(hT[:, k, :], PS[:, 4 + k, :], ACT.Copy).then_inc(hT_ready, 1)

                    def silu(b):
                        for e in range(KE):
                            act.wait_ge(z_psum, KE * b + e + 1)
                            if not isinstance(b, int) or b:
                                act.wait_ge(g_ready, KE * (b - 1) + e + 1)
                            nc.scalar.activation(sz[:, e, :], PS[:, e, :], ACT.Silu).then_inc(sz_ready, 1)

                    evac(0)
                    silu(0)
                    with act.Fori(1, B) as b:
                        evac(b)
                        silu(b)

                @block.vector
                def _(dve):
                    base = [0]
                    n = [0]
                    def link(ins):
                        n[0] += 1
                        ins.then_inc(s_chain, 1)
                        dve.wait_ge(s_chain, base[0] + n[0])

                    def tiles(b):
                        return [X[:, TB * b + t, :] for t in range(TB)]

                    def stats_part(b):
                        norm_stats(link, tiles(b)).then_inc(hn_var, 1)

                    def apply_part(b):
                        if not isinstance(b, int) or b:
                            dve.wait_ge(hT_psum, b)
                        dve.wait_ge(hn_rstd, 2 * b + 2)
                        norm_apply(tiles(b), [hn[:, t, :] for t in range(TB)]).then_inc(hn_ready, 1)

                    def gate(b, e):
                        dve.wait_ge(sz_ready, KE * b + e + 1)
                        nc.vector.tensor_tensor(g[:, e, :], sz[:, e, :], yD[:, e, :],
                                                ALU.mult).then_inc(g_ready, 1)

                    def residual(b):
                        for i in range(2):
                            dve.wait_ge(o_psum, 2 * b + i + 1)
                            xs = X[:, bass.ds(TB * b + 2 * i, 2), :].rearrange("p t d -> p (t d)")
                            nc.vector.tensor_tensor(xs, xs, PS[:, 6 + i, :], ALU.add).then_inc(x1_ready, 1)

                    dve.sem_inc(x1_ready, 2)
                    stats_part(0)
                    apply_part(0)
                    with dve.Fori(0, B - 1) as b:
                        n[0] = 0
                        base[0] = b + 1
                        stats_part(b + 1)
                        gate(b, 0)
                        apply_part(b + 1)
                        for e in range(1, KE):
                            gate(b, e)
                        residual(b)
                    for e in range(KE):
                        gate(B - 1, e)
                    residual(B - 1)
                    dve.wait_ge(x1_ready, 2 * B + 2)

                @block.gpsimd
                def _(pool):
                    with pool.Fori(0, B) as b:
                        pool_wait(pool, hn_var, b + 1)
                        norm_rstd(pool, hn_rstd, 2 * b)

        if stop == 1:
            dump(nc, ctx, X, out, B, TB, P)
            return

        with ExitStack() as c:
            def tmp(name, shape, dt=F32):
                return c.enter_context(nc.sbuf_tensor(name, shape, dt))
            wq, wk, wv, wo = (tmp(n, [P, KD, D]) for n in ("wq", "wk", "wv", "wo"))
            bq, bk = tmp("bq", [P, KD]), tmp("bk", [P, KD])
            bv = tmp("bv", [1, D])
            bo = tmp("bo", [P, D])
            ctx2 = tmp("ctx2", [P, KD, B, 2, S])
            kT = tmp("kT", [P, KD, B, S])
            kbd = tmp("kbd", [P, B, KD, HH * S])
            vbd = tmp("vbd", [P, B, NP * PW])
            qT = tmp("qT", [P, KD, L])
            pr = tmp("pr", [P, 2, H * S])
            prT = tmp("prT", [P, NP, P])
            mx = tmp("mx", [P, 2, H])
            den = tmp("den", [P, H])
            o = tmp("o", [P, D])
            oT = tmp("oT", [P, KD, P])
            (w_in, k_psum, kT_ready, k_ready, v_psum, v_ready, vz,
             hn_var, hn_rstd, hn_ready, hT_psum, hT_ready, q_psum, qT_ready, bo_added,
             s_psum, s_max, s_shift, p_ready, pT_psum, pT_ready, o_psum, o_den, o_ready, oT_psum, oT_ready,
             y_psum, x2_ready, s_chain) = phase_sems(c, """b_w_in b_k_psum b_kT_ready b_k_ready
                b_v_psum b_v_ready b_vz b_hn_var b_hn_rstd b_hn_ready b_hT_psum b_hT_ready b_q_psum b_qT_ready
                b_bo_added b_s_psum b_s_max b_s_shift b_p_ready b_pT_psum b_pT_ready b_o_psum b_o_den b_o_ready
                b_oT_psum b_oT_ready b_y_psum b_x2_ready b_chain""")
            with nc.Block() as block:
                @block.sync
                def _(sp):
                    for w, n in ((wk, "Wk"), (wv, "Wv"), (wq, "Wq"), (wo, "Wo")):
                        sp.dma_start(w[:], d[n].rearrange("(k p) e -> p k e", p=P)).then_inc(w_in, 16)
                    for j in range(2):
                        for k in range(KD):
                            sp.dma_start(ctx2[:, k, :, j, :],
                                         d["ctxT"][k].rearrange("p (b s) -> p b s", s=S)).then_inc(w_in, 16)
                    sp.dma_start(bq[:], d["bq"]).then_inc(w_in, 16)
                    sp.dma_start(bk[:], d["bk"]).then_inc(w_in, 16)
                    sp.dma_start(bv[:], d["bv"]).then_inc(w_in, 16)
                    sp.dma_start(bo[:], d["bo"].to_broadcast([P, D])).then_inc(w_in, 16)
                W_IN = 16 * 12

                @block.tensor
                def _(pe):
                    pe.wait_ge(w_in, W_IN)
                    for m in range(KD):
                        for k in range(KD):
                            last = nc.tensor.matmul(PS[:, m, :], wk[:, k, m * P:(m + 1) * P],
                                                    ctx2[:, k, :, 0, :], start=k == 0, stop=k == KD - 1)
                        last.then_inc(k_psum, 1)
                    for b in range(B):
                        if b >= 2:
                            pe.wait_ge(v_ready, 2 * (b - 1))
                        for k in range(KD):
                            nc.tensor.matmul(PS[:, 2 + b % 2, 0:D], ctx2[:, k, b, :, :], wv[:, k, :],
                                             start=k == 0, stop=False)
                        nc.tensor.matmul(PS[:, 2 + b % 2, 0:D], ones[0:1, :], bv[:], start=False,
                                         stop=True).then_inc(v_psum, 1)

                    def transpose_x(j, t):
                        pe.wait_ge(hn_ready, j + 1)
                        if not isinstance(j, int) or j:
                            pe.wait_ge(hT_ready, j)
                        for k in range(KD):
                            last = nc.tensor.transpose(PS[:, 6, k * P:(k + 1) * P],
                                                       hn[:, t, k * P:(k + 1) * P], ident[:])
                        last.then_inc(hT_psum, 1)

                    def project_q(b):
                        pe.wait_ge(hT_ready, TB * b + TB)
                        if not isinstance(b, int) or b:
                            pe.wait_ge(s_shift, KD * TB * b)
                        for m in range(KD):
                            for k in range(KD):
                                last = nc.tensor.matmul(PS[:, m, :], wq[:, k, m * P:(m + 1) * P], hT[:, k, :],
                                                        start=k == 0, stop=k == KD - 1)
                            last.then_inc(q_psum, 1)

                    def scores(b, t):
                        i = TB * b + t
                        pe.wait_ge(qT_ready, KD * b + KD)
                        for m in range(KD):
                            if not isinstance(i, int) or i:
                                pe.wait_ge(s_shift, KD * (i - 1) + m + 1)
                            last = nc.tensor.matmul(PS[:, m, :], qT[:, m, t * P:(t + 1) * P],
                                                    kbd[:, bass.ds(b, 1), m, :].rearrange("p a n -> p (a n)"),
                                                    start=True, stop=t > 0)
                            if t == 0:
                                last = nc.tensor.matmul(PS[:, m, :], ident[:], causal[:], start=False,
                                                        stop=True)
                            last.then_inc(s_psum, 1)

                    def transpose_p(i, par):
                        pe.wait_ge(p_ready, i + 1)
                        if not isinstance(i, int) or i:
                            pe.wait_ge(pT_ready, i)
                        for j in range(NP):
                            last = nc.tensor.transpose(PS[:, 2 + j // 4, (j % 4) * P:(j % 4 + 1) * P],
                                                       pr[:, par, j * P:(j + 1) * P], ident[:])
                        last.then_inc(pT_psum, 1)

                    def weigh_values(i, b):
                        pe.wait_ge(pT_ready, i + 1)
                        if not isinstance(i, int) or i:
                            pe.wait_ge(o_ready, i)
                        for j in range(NP):
                            last = nc.tensor.matmul(
                                PS[:, 4, j * PW:(j + 1) * PW], prT[:, j, :],
                                vbd[:, bass.ds(b, 1), j * PW:(j + 1) * PW].rearrange("p a n -> p (a n)"),
                                start=True, stop=True)
                        last.then_inc(o_psum, 1)

                    def transpose_o(i):
                        pe.wait_ge(o_ready, i + 1)
                        if not isinstance(i, int) or i:
                            pe.wait_ge(oT_ready, i)
                        for k in range(KD):
                            last = nc.tensor.transpose(PS[:, 7, k * P:(k + 1) * P],
                                                       o[:, k * P:(k + 1) * P], ident[:])
                        last.then_inc(oT_psum, 1)

                    def project_o(i):
                        pe.wait_ge(oT_ready, i + 1)
                        if not isinstance(i, int) or i:
                            pe.wait_ge(x2_ready, i)
                        for k in range(KD):
                            last = nc.tensor.matmul(PS[:, 5, 0:D], oT[:, k, :], wo[:, k, :],
                                                    start=k == 0, stop=k == KD - 1)
                        last.then_inc(y_psum, 1)

                    def step(b, t, scored=True, following=True, lag2=True, lag3=True):
                        i = TB * b + t
                        if lag2:
                            transpose_p(i - 2, t % 2)
                        if scored:
                            scores(b, t)
                        if lag3:
                            transpose_o(i - 3)
                        if following:
                            transpose_x(i + TB, t)
                        if lag2:
                            weigh_values(i - 2, b if t >= 2 else b - 1)
                        if lag3:
                            project_o(i - 3)
                        if following and t == TB - 1:
                            project_q(b + 1)

                    pe.wait_ge(k_ready, 1)
                    pe.wait_ge(kT_ready, KD)
                    pe.wait_ge(vz, 3)
                    pe.wait_ge(v_ready, 2 * B)
                    for t in range(TB):
                        transpose_x(t, t)
                    project_q(0)
                    for t in range(TB):
                        step(0, t, lag2=t >= 2, lag3=t >= 3)
                    with pe.Fori(1, B - 1) as b:
                        for t in range(TB):
                            step(b, t)
                    for t in range(TB):
                        step(B - 1, t, following=False)
                    for t in range(3):
                        step(B, t, scored=False, following=False, lag2=t < 2)

                @block.scalar
                def _(act):
                    for b in range(B):
                        act.wait_ge(v_psum, b + 1)
                        if b == 0:
                            act.wait_ge(vz, 1)
                        for h in range(2):
                            rows = slice(h * S, (h + 1) * S)
                            dst = vbd[rows, b, :].rearrange("p (j c) -> p j c", c=PW)[:, :, h * DK:(h + 1) * DK]
                            src = PS[rows, 2 + b % 2, 0:D].rearrange("p (j c) -> p j c", c=2 * DK)
                            nc.scalar.activation(dst, src[:, :, h * DK:(h + 1) * DK],
                                                 ACT.Copy).then_inc(v_ready, 1)

                    def evac_x(j, t):
                        act.wait_ge(hT_psum, j + 1)
                        nc.scalar.activation(hT[:, :, t * P:(t + 1) * P],
                                             PS[:, 6, 0:D].rearrange("p (k n) -> p k n", k=KD),
                                             ACT.Copy).then_inc(hT_ready, 1)

                    def evac_q(b):
                        for m in range(KD):
                            act.wait_ge(q_psum, KD * b + m + 1)
                            nc.scalar.activation(qT[:, m, :], PS[:, m, :], ACT.Identity,
                                                 bias=bq[:, m:m + 1]).then_inc(qT_ready, 1)

                    def evac_p(i):
                        act.wait_ge(pT_psum, i + 1)
                        nc.scalar.activation(prT[:].rearrange("p j n -> p (j n)"),
                                             PS[:, 2:4, :].rearrange("p a n -> p (a n)"),
                                             ACT.Copy).then_inc(pT_ready, 1)

                    def evac_o(i):
                        act.wait_ge(oT_psum, i + 1)
                        nc.scalar.activation(oT[:].rearrange("p k n -> p (k n)"), PS[:, 7, 0:D],
                                             ACT.Copy).then_inc(oT_ready, 1)

                    def exps(i, par):
                        act.wait_ge(s_shift, KD * i + KD)
                        nc.scalar.activation(pr[:, par, :], pr[:, par, :], ACT.Exp,
                                             scale=SCALE).then_inc(p_ready, 1)

                    def step(b, t, scored=True, following=True, lag2=True, lag3=True):
                        i = TB * b + t
                        if lag2:
                            evac_p(i - 2)
                        if lag3:
                            evac_o(i - 3)
                        if following:
                            evac_x(i + TB, t)
                        if scored:
                            exps(i, t % 2)
                        if following and t == TB - 1:
                            evac_q(b + 1)

                    act.wait_ge(w_in, W_IN)
                    for t in range(TB):
                        evac_x(t, t)
                    evac_q(0)
                    for t in range(TB):
                        step(0, t, lag2=t >= 2, lag3=t >= 3)
                    with act.Fori(1, B - 1) as b:
                        for t in range(TB):
                            step(b, t)
                    for t in range(TB):
                        step(B - 1, t, following=False)
                    for t in range(3):
                        step(B, t, scored=False, following=False, lag2=t < 2)

                @block.gpsimd
                def _(pool):
                    nc.gpsimd.memset(vbd[:], 0.0).then_inc(vz, 1)
                    pool_wait(pool, vz, 1)
                    for h in range(2):
                        v = vbd[h * S:(h + 1) * S, :, :].rearrange("p b (j c) -> p b j c", c=PW)
                        nc.gpsimd.memset(v[:, :, :, 2 * DK + h:2 * DK + h + 1], 1.0).then_inc(vz, 1)
                        pool_wait(pool, vz, 2 + h)

                    def rstds(i):
                        pool_wait(pool, hn_var, i + 1)
                        norm_rstd(pool, hn_rstd, 2 * i)

                    pool_wait(pool, w_in, W_IN)
                    rstds(0)
                    pool_wait(pool, kT_ready, KD)
                    for b in range(B):
                        for m in range(KD):
                            dst = kbd[:, b, m, :].rearrange("p (h s) -> p h s", s=S)
                            last = nc.gpsimd.tensor_tensor(
                                dst, kT[:, m, b, :].unsqueeze(1).to_broadcast([P, HH, S]),
                                headmask.unsqueeze(2).to_broadcast([P, HH, S]), ALU.mult)
                    last.then_inc(k_ready, 1)

                    def add_bo(b):
                        pool_wait(pool, hn_ready, TB * b + TB)
                        xs = X[:, bass.ds(TB * b, TB), :]
                        nc.gpsimd.tensor_tensor(xs, xs, bo[:].unsqueeze(1).to_broadcast([P, TB, D]),
                                                ALU.add).then_inc(bo_added, 1)
                    add_bo(0)
                    with pool.Fori(1, B) as b:
                        rstds(b)
                        add_bo(b)

                @block.vector
                def _(dve):
                    base = [0]
                    n = [0]
                    def link(ins):
                        n[0] += 1
                        ins.then_inc(s_chain, 1)
                        dve.wait_ge(s_chain, base[0] + n[0])

                    for m in range(KD):
                        dve.wait_ge(k_psum, m + 1)
                        nc.vector.tensor_scalar(kT[:, m, :, :].rearrange("p b s -> p (b s)"), PS[:, m, :],
                                                bk[:, m:m + 1], None, ALU.add).then_inc(kT_ready, 1)

                    def tile(j):
                        return X[:, bass.ds(j, 1), :].rearrange("p a d -> p (a d)")

                    def stats_part(b):
                        norm_stats(link, [tile(TB * b + t) for t in range(TB)]).then_inc(hn_var, 1)

                    def apply_part(b, t):
                        j = TB * b + t
                        if t == 0:
                            dve.wait_ge(hn_rstd, 2 * b + 2)
                        if not isinstance(j, int) or j >= TB:
                            dve.wait_ge(hT_psum, j - TB + 1)
                        nc.vector.tensor_scalar(hn[:, t, :], tile(j), mv[:, t, 0:1], rstd[:, t:t + 1],
                                                ALU.subtract, ALU.mult).then_inc(hn_ready, 1)

                    def shift(i, par):
                        for m in range(KD):
                            dve.wait_ge(s_psum, KD * i + m + 1)
                            nc.vector.tensor_reduce(mx[:, par, m * HH:(m + 1) * HH],
                                                    PS[:, m, :].rearrange("p (h s) -> p h s", s=S),
                                                    op=ALU.max, axis=AX).then_inc(s_max, 1)
                        if not isinstance(i, int) or i >= 2:
                            dve.wait_ge(pT_psum, i - 1)
                        for m in range(KD):
                            dve.wait_ge(s_max, KD * i + m + 1)
                            nc.vector.tensor_tensor(
                                pr[:, par, m * HH * S:(m + 1) * HH * S].rearrange("p (h s) -> p h s", s=S),
                                PS[:, m, :].rearrange("p (h s) -> p h s", s=S),
                                mx[:, par, m * HH:(m + 1) * HH].unsqueeze(2).to_broadcast([P, HH, S]),
                                ALU.subtract).then_inc(s_shift, 1)

                    def divide(i):
                        dve.wait_ge(o_psum, i + 1)
                        ps = PS[:, 4, 0:NP * PW].rearrange("p (j c) -> p j c", c=PW)
                        nc.vector.reciprocal(den[:].rearrange("p (j c) -> p j c", c=2),
                                             ps[:, :, 2 * DK:PW]).then_inc(o_den, 1)
                        dve.wait_ge(o_den, i + 1)
                        src = ps[:, :, 0:2 * DK].rearrange("p j (c e) -> p j c e", c=2)
                        nc.vector.tensor_tensor(
                            o[:].rearrange("p (j c e) -> p j c e", j=NP, c=2), src,
                            den[:].rearrange("p (j c) -> p j c", c=2).unsqueeze(3).to_broadcast([P, NP, 2, DK]),
                            ALU.mult).then_inc(o_ready, 1)

                    def residual(i, b):
                        dve.wait_ge(bo_added, b + 1)
                        dve.wait_ge(y_psum, i + 1)
                        nc.vector.tensor_tensor(tile(i), tile(i), PS[:, 5, 0:D], ALU.add).then_inc(x2_ready, 1)

                    def step(b, t, scored=True, following=True, lag3=True, lag4=True):
                        i = TB * b + t
                        if lag3:
                            divide(i - 3)
                        if lag4:
                            residual(i - 4, b - 1)
                        if following:
                            apply_part(b + 1, t)
                        if scored:
                            shift(i, t % 2)

                    dve.wait_ge(w_in, W_IN)
                    stats_part(0)
                    for t in range(TB):
                        apply_part(0, t)
                    dve.wait_ge(hn_ready, TB)
                    stats_part(1)
                    for t in range(TB):
                        step(0, t, lag3=t >= 3, lag4=False)
                    with dve.Fori(1, B - 1) as b:
                        n[0] = 0
                        base[0] = b + 1
                        dve.wait_ge(hn_ready, TB * b + TB)
                        stats_part(b + 1)
                        for t in range(TB):
                            step(b, t)
                    for t in range(TB):
                        step(B - 1, t, following=False)
                    for t in range(TB):
                        step(B, t, scored=False, following=False, lag3=t < 3)
                    dve.wait_ge(x2_ready, N // P)

        if stop == 2:
            dump(nc, ctx, X, out, B, TB, P)
            return

        with ExitStack() as c:
            def tmp(name, shape, dt=F32, c=c):
                return c.enter_context(nc.sbuf_tensor(name, shape, dt))
            wfc = tmp("wfc", [P, 2, KD, HID])
            wpr = tmp("wpr", [P, 2, KH, D])
            bpr = tmp("bpr", [P, 2, D])
            bfc = tmp("bfc", [P, E, KH])
            carry = tmp("carry", [P, E])
            (w_in, hn_var, hn_rstd, hn_ready, hT_psum, hT_ready, h_psum, h_ready, y_psum, x3_ready,
             l_psum, l_read, chosen, r_psum, r_read, gates_exp, slots_ready, rows_ready, hn_copied, scattered,
             bias_added, carry_ready, pads_scattered, stored, s_chain, pads_zeroed, *e_w_in) = phase_sems(
                ctx, """c_w_in c_hn_var c_hn_rstd c_hn_ready c_hT_psum c_hT_ready c_h_psum c_h_ready c_y_psum
                c_x3_ready c_l_psum c_l_read c_chosen c_r_psum c_r_read c_gates_exp c_slots_ready c_rows_ready
                c_hn_copied c_scattered c_bias_added c_carry_ready c_pads_scattered c_stored c_chain
                c_pads_zeroed c_even_w_in c_odd_w_in""")
            HELD = 4
            tbl = tmp("tbl", [P, 2 * E], I32)

            def weights(par, e):
                return ((wfc[:, par, :, :], d["Wfc"][bass.ds(e, 1)].rearrange("a (k p) n -> p (a k) n", p=P)),
                        (wpr[:, par, :, :], d["Wproj"][bass.ds(e, 1)].rearrange("a (k p) n -> p (a k) n", p=P)),
                        (bpr[:, par, :], d["bproj"][bass.ds(e, 1), :].to_broadcast([P, D])))

            cs = ExitStack()
            with cs:
                def tm(name, shape, dt=F32):
                    return cs.enter_context(nc.sbuf_tensor(name, shape, dt))
                wfs = tm("wfs", [P, KD, HID])
                wps = tm("wps", [P, KH, D])
                wr = tm("wr", [P, KD, E])
                bfs = tm("bfs", [P, KH])
                bps = tm("bps", [P, D])
                hid = tm("hid", [P, KH, L])
                rows = tm("rows", [P, TB, ROW])
                pads = tm("pads", [P, 2, ROW])
                tok = tm("tok", [P, TB])
                lg = tm("lg", [P, 8, TB, E])
                oh = tm("oh", [P, 3, TB, E])
                m4 = tm("m4", [P, 8, TB])
                meta = tm("meta", [P, TB, ROW - D])
                slot = tm("slot", [P, TB, 2], I32)
                slotc = tm("slotc", [P, TB, 2], I32)
                padslot = tm("padslot", [P, 2, E], I32)
                cnt = tm("cnt", [P, 4, E])
                cmp_ = tm("cmp", [P, E, NBR - 1])
                W_IN = 16 * 6
                with nc.Block() as block:
                    @block.sync
                    def _(sp):
                        for dst, src in ((wfs[:], d["Wfc_s"].rearrange("(k p) e -> p k e", p=P)),
                                         (wps[:], d["Wproj_s"].rearrange("(k p) e -> p k e", p=P)),
                                         (wr[:], d["Wr"].rearrange("(k p) e -> p k e", p=P)),
                                         (bfs[:], d["bfc_s"]), (bps[:], d["bproj_s"].to_broadcast([P, D])),
                                         (bfc[:], d["bfc"])):
                            sp.dma_start(dst, src).then_inc(w_in, 16)
                        for e in range(2):
                            for dst, src in weights(e, e):
                                sp.dma_start(dst, src).then_inc(e_w_in[e], 16)
                        ov = out.rearrange("(t p) d -> p t d", p=P)
                        with sp.Fori(0, B) as b:
                            sp.wait_ge(x3_ready, TB * b + 2 * TB)
                            sp.dma_start(ov[:, bass.ds(TB * b, TB), :], X[:, bass.ds(TB * b, TB), :]).then_inc(stored, 16)
                        sp.wait_ge(pads_zeroed, 1)
                        sp.dma_start(out[N:N + BLK, :].rearrange("(h p) d -> p h d", p=P),
                                     pads[:, :, 0:D]).then_inc(stored, 16)
                        sp.wait_ge(stored, 16 * B + 16)

                    @block.tensor
                    def _(pe):
                        def transposes(b):
                            pe.wait_ge(hn_ready, b + 1)
                            if not isinstance(b, int) or b:
                                pe.wait_ge(r_read, b)
                            for t in range(TB):
                                for k in range(KD):
                                    last = nc.tensor.transpose(PS[:, 4 + k, t * P:(t + 1) * P],
                                                               hn[:, t, k * P:(k + 1) * P], ident[:])
                            last.then_inc(hT_psum, 1)

                        def up(b):
                            pe.wait_ge(hT_ready, KD * b + KD)
                            for j in range(KH):
                                pe.wait_ge(h_ready, KH * b + j + 1)
                                for k in range(KD):
                                    last = nc.tensor.matmul(PS[:, j % 4, :], wfs[:, k, j * P:(j + 1) * P], hT[:, k, :],
                                                            start=k == 0, stop=k == KD - 1)
                                last.then_inc(h_psum, 1)

                        def logits(b):
                            pe.wait_ge(hT_ready, KD * b + KD)
                            for t in range(TB):
                                for k in range(KD):
                                    last = nc.tensor.matmul(PS[:, 4, t * E:(t + 1) * E], hT[:, k, t * P:(t + 1) * P],
                                                            wr[:, k, :], start=k == 0, stop=k == KD - 1)
                            last.then_inc(l_psum, 1)

                        def ranks(b):
                            pe.wait_ge(chosen, b + 1)
                            for t in range(TB):
                                for s in range(t + 1):
                                    last = nc.tensor.matmul(PS[:, 5, t * E:(t + 1) * E],
                                                            tri[:] if s == t else ones[:], oh[:, 2, s, :],
                                                            start=s == 0, stop=s == t)
                            for s in range(TB):
                                last = nc.tensor.matmul(PS[:, 5, TB * E:(TB + 1) * E], ones[:], oh[:, 2, s, :],
                                                        start=s == 0, stop=s == TB - 1)
                            last.then_inc(r_psum, 1)

                        def down(b):
                            pe.wait_ge(h_ready, KH * b + KH + HELD)
                            for t in range(TB):
                                if t % 2 == 0:
                                    pe.wait_ge(x3_ready, TB * b + t + 2)
                                for j in range(KH):
                                    last = nc.tensor.matmul(PS[:, 6 + t // 2, (t % 2) * D:(t % 2 + 1) * D],
                                                            hid[:, j, t * P:(t + 1) * P], wps[:, j, :],
                                                            start=j == 0, stop=j == KH - 1)
                                if t % 2:
                                    last.then_inc(y_psum, 1)

                        pe.wait_ge(w_in, W_IN)
                        transposes(0)
                        logits(0)
                        with pe.Fori(0, B - 1) as b:
                            up(b)
                            ranks(b)
                            transposes(b + 1)
                            down(b)
                            logits(b + 1)
                        up(B - 1)
                        ranks(B - 1)
                        down(B - 1)

                    @block.scalar
                    def _(act):
                        def evac(b):
                            act.wait_ge(hT_psum, b + 1)
                            for k in range(KD):
                                nc.scalar.activation(hT[:, k, :], PS[:, 4 + k, :], ACT.Copy).then_inc(hT_ready, 1)

                        def gelus(b):
                            for j in range(KH):
                                act.wait_ge(h_psum, KH * b + j + 1)
                                nc.scalar.activation(hid[:, j, :], PS[:, j % 4, :], ACT.Gelu_apprx_tanh,
                                                     bias=bfs[:, j:j + 1]).then_inc(h_ready, 1)
                                if j == 3:
                                    act.wait_ge(chosen, b + 1)
                                    nc.scalar.activation(m4[:, 3, :], m4[:, 2, :], ACT.Tanh,
                                                         scale=0.5).then_inc(gates_exp, 1)

                        act.wait_ge(w_in, W_IN)
                        act.sem_inc(h_ready, HELD)
                        evac(0)
                        with act.Fori(0, B - 1) as b:
                            gelus(b)
                            evac(b + 1)
                        gelus(B - 1)

                    @block.gpsimd
                    def _(pool):
                        def rstds(b):
                            pool_wait(pool, hn_var, b + 1)
                            norm_rstd(pool, hn_rstd, 2 * b)

                        def copy_rows(b):
                            pool_wait(pool, hn_ready, b + 1)
                            if not isinstance(b, int) or b:
                                pool_wait(pool, scattered, 16 * 2 * TB * b)
                            nc.gpsimd.tensor_copy(rows[:, :, 0:D], hn[:]).then_inc(hn_copied, 1)
                            xs = X[:, bass.ds(TB * b, TB), :]
                            nc.gpsimd.tensor_tensor(xs, xs, bps[:].unsqueeze(1).to_broadcast([P, TB, D]),
                                                    ALU.add).then_inc(bias_added, 1)

                        def send_rows(b):
                            pool_wait(pool, slots_ready, b + 1)
                            nc.gpsimd.tensor_copy(rows[:, :, D:ROW], meta[:]).then_inc(rows_ready, 1)
                            nc.gpsimd.tensor_copy(slotc[:], slot[:]).then_inc(rows_ready, 1)
                            pool_wait(pool, rows_ready, 2 * b + 4)
                            pool_wait(pool, hn_copied, b + 1)
                            for t in range(TB):
                                for m in range(2):
                                    nc.gpsimd.indirect_dma_start(
                                        out=RG, out_offset=bass.IndirectOffsetOnAxis(ap=slotc[:, t, m:m + 1], axis=0),
                                        in_=rows[:, t, :], in_offset=None).then_inc(scattered, 16)

                        pool_wait(pool, w_in, W_IN)
                        nc.gpsimd.memset(pads[:], 0.0).then_inc(pads_zeroed, 1)
                        pool.sem_inc(rows_ready, 2)
                        rstds(0)
                        copy_rows(0)
                        with pool.Fori(0, B - 1) as b:
                            rstds(b + 1)
                            send_rows(b)
                            copy_rows(b + 1)
                        send_rows(B - 1)
                        pool_wait(pool, carry_ready, 1)
                        for e in range(E):
                            for h in range(2):
                                nc.gpsimd.indirect_dma_start(
                                    out=RG, out_offset=bass.IndirectOffsetOnAxis(ap=padslot[:, h, e:e + 1], axis=0),
                                    in_=pads[:, h, :], in_offset=None).then_inc(pads_scattered, 16)
                        pool_wait(pool, scattered, 16 * 2 * TB * B)
                        pool_wait(pool, pads_scattered, 16 * 2 * E)

                    @block.vector
                    def _(dve):
                        base = [0]
                        n = [0]
                        def link(ins):
                            n[0] += 1
                            ins.then_inc(s_chain, 1)
                            dve.wait_ge(s_chain, base[0] + n[0])

                        def tiles(b):
                            return [X[:, TB * b + t, :] for t in range(TB)]

                        def stats_part(b):
                            norm_stats(link, tiles(b)).then_inc(hn_var, 1)

                        def apply_part(b):
                            if not isinstance(b, int) or b:
                                dve.wait_ge(hT_psum, b)
                                dve.wait_ge(hn_copied, b)
                            dve.wait_ge(hn_rstd, 2 * b + 2)
                            norm_apply(tiles(b), [hn[:, t, :] for t in range(TB)]).then_inc(hn_ready, 1)

                        def first_of(score, top, choice):
                            link(nc.vector.tensor_reduce(top, score, op=ALU.max, axis=AX))
                            link(nc.vector.tensor_tensor(lg[:, 2, :, :], score,
                                                         top.unsqueeze(2).to_broadcast([P, TB, E]), ALU.is_equal))
                            link(nc.vector.tensor_tensor(lg[:, 2, :, :], lg[:, 2, :, :],
                                                         tiew.unsqueeze(1).to_broadcast([P, TB, E]), ALU.mult))
                            link(nc.vector.tensor_reduce(m4[:, 4, :], lg[:, 2, :, :], op=ALU.max, axis=AX))
                            link(nc.vector.tensor_tensor(choice, lg[:, 2, :, :],
                                                         m4[:, 4, :].unsqueeze(2).to_broadcast([P, TB, E]),
                                                         ALU.is_equal))

                        def choose(b):
                            dve.wait_ge(l_psum, b + 1)
                            nc.vector.tensor_copy(lg[:, 0, :, :].rearrange("p t e -> p (t e)"),
                                                  PS[:, 4, 0:TB * E]).then_inc(l_read, 1)
                            dve.wait_ge(l_read, b + 1)
                            first_of(lg[:, 0, :, :], m4[:, 0, :], oh[:, 0, :, :])
                            link(nc.vector.scalar_tensor_tensor(lg[:, 1, :, :], oh[:, 0, :, :], -BIG, lg[:, 0, :, :],
                                                                ALU.mult, ALU.add))
                            first_of(lg[:, 1, :, :], m4[:, 1, :], oh[:, 1, :, :])
                            link(nc.vector.tensor_tensor(m4[:, 2, :], m4[:, 0, :], m4[:, 1, :], ALU.subtract))
                            nc.vector.tensor_tensor(oh[:, 2, :, :], oh[:, 0, :, :], oh[:, 1, :, :],
                                                    ALU.add).then_inc(chosen, 1)

                        CHOOSE = 12

                        def place(b):
                            dve.wait_ge(r_psum, b + 1)
                            dve.wait_ge(rows_ready, 2 * b + 2)
                            pos = lg[:, 3, :, :]
                            link(nc.vector.tensor_tensor(pos, PS[:, 5, 0:TB * E].rearrange("p (t e) -> p t e", e=E),
                                                         carry[:].unsqueeze(1).to_broadcast([P, TB, E]), ALU.add))
                            nc.vector.tensor_tensor(carry[:], carry[:], PS[:, 5, TB * E:(TB + 1) * E],
                                                    ALU.add).then_inc(r_read, 1)
                            for m in range(2):
                                link(nc.vector.tensor_tensor(lg[:, 4 + m, :, :], pos, oh[:, m, :, :], ALU.mult))
                                link(nc.vector.tensor_reduce(m4[:, 5 + m, :], lg[:, 4 + m, :, :], op=ALU.add, axis=AX))
                                link(nc.vector.tensor_copy(slot[:, :, m], m4[:, 5 + m, :]))
                            dve.wait_ge(gates_exp, b + 1)
                            for m, sign in enumerate((0.5, -0.5)):
                                link(nc.vector.tensor_scalar(m4[:, 7, :], m4[:, 3, :], sign, 0.5, ALU.mult, ALU.add))
                                link(nc.vector.tensor_tensor(lg[:, 4 + m, :, :], oh[:, m, :, :],
                                                             m4[:, 7, :].unsqueeze(2).to_broadcast([P, TB, E]),
                                                             ALU.mult))
                            link(nc.vector.tensor_tensor(meta[:, :, 0:E], lg[:, 4, :, :], lg[:, 5, :, :], ALU.add))
                            nc.vector.tensor_copy(meta[:, :, E], tok[:]).then_inc(slots_ready, 1)
                            dve.wait_ge(slots_ready, b + 1)
                            link(nc.vector.tensor_scalar(tok[:], tok[:], float(L), None, ALU.add))

                        PLACE = 13

                        def residual(b):
                            dve.wait_ge(bias_added, b + 1)
                            for i in range(2):
                                dve.wait_ge(y_psum, 2 * b + i + 1)
                                xs = X[:, bass.ds(TB * b + 2 * i, 2), :].rearrange("p t d -> p (t d)")
                                nc.vector.tensor_tensor(xs, xs, PS[:, 6 + i, :], ALU.add).then_inc(x3_ready, 2)

                        dve.sem_inc(x3_ready, TB)
                        nc.vector.tensor_copy(carry[:], ebase)
                        for t in range(TB):
                            nc.vector.tensor_scalar(tok[:, t:t + 1], rowno[:, 0:1], float(t * P), None, ALU.add)
                        link(nc.vector.memset(meta[:], 0.0))
                        stats_part(0)
                        apply_part(0)
                        choose(0)
                        with dve.Fori(0, B - 1) as b:
                            n[0] = 0
                            base[0] = (1 + CHOOSE + PLACE) * b + (2 + CHOOSE)
                            stats_part(b + 1)
                            apply_part(b + 1)
                            place(b)
                            residual(b)
                            choose(b + 1)
                            assert n[0] == 1 + CHOOSE + PLACE, n
                        n[0] = 0
                        base[0] = (1 + CHOOSE + PLACE) * (B - 1) + (2 + CHOOSE)
                        place(B - 1)
                        dve.wait_ge(pads_zeroed, 1)
                        for h in range(2):
                            link(nc.vector.tensor_scalar(cnt[:, 3, :], carry[:], rowno[:, h:h + 1], None, ALU.add))
                            link(nc.vector.tensor_copy(padslot[:, h, :], cnt[:, 3, :]))
                            nc.vector.tensor_scalar(pads[:, h, TOK:TOK + 1], rowno[:, h:h + 1], float(N), None, ALU.add)
                        link(nc.vector.tensor_tensor(cnt[:, 0, :], carry[:], ebase, ALU.subtract))
                        for j in range(1, NBR - 1):
                            nc.vector.tensor_scalar(cmp_[:, :, j - 1], cnt[:, 0, :], float(BLK * j), None,
                                                    ALU.is_gt)
                        link(nc.vector.memset(cmp_[:, :, NBR - 2], 1.0))
                        link(nc.vector.tensor_reduce(cnt[:, 1, :], cmp_[:], op=ALU.add, axis=AX))
                        link(nc.vector.tensor_tensor_scan(cnt[:, 2, :], ones[:, 0:E], cnt[:, 1, :], 0.0,
                                                          ALU.mult, ALU.add))
                        link(nc.vector.tensor_tensor(cnt[:, 2, :], cnt[:, 2, :], cnt[:, 1, :], ALU.subtract))
                        link(nc.vector.tensor_copy(tbl[:, 0:E], cnt[:, 1, :]))
                        nc.vector.tensor_copy(tbl[:, E:2 * E], cnt[:, 2, :]).then_inc(carry_ready, 1)
                        residual(B - 1)
                        dve.wait_ge(x3_ready, TB * B + TB)

            if stop == 3:
                dump(nc, ctx, X, out, B, TB, P)
                return

            def tm(name, shape, dt=F32):
                return c.enter_context(nc.sbuf_tensor(name, shape, dt))
            xr = tm("xr", [P, 2, ROW])
            xT = tm("xT", [P, KD, BLK])
            hid = tm("hide", [P, KH, BLK])
            meta = tm("metae", [P, 2, ROW - D])
            gate = tm("gate", [P, 2])
            toki = tm("toki", [P, 2], I32)
            y = tm("y", [P, 2, D])
            (x_in, x_psum, xT_ready, xr_free, h_psum, h_ready, y_psum, y_read, y_ready, gate_ready,
             added, y_sent, s_chain) = phase_sems(c, """d_x_in d_x_psum d_xT_ready d_xr_free d_h_psum
                d_h_ready d_y_psum d_y_read d_y_ready d_gate_ready d_added d_y_sent d_chain""")
            rg = RG.rearrange("(n h p) c -> n p h c", h=2, p=P)

            def blocks_of(eng, e):
                return (eng.value_load(tbl[0:1, bass.ds(e, 1)], min_val=1, max_val=NBR - 1),
                        eng.value_load(tbl[0:1, bass.ds(E + e, 1)], min_val=0, max_val=2 * N // BLK + E))

            def every_block(eng, body, head=None):
                with eng.Fori(0, E // 2) as pair:
                    for par in range(2):
                        e = pair * 2 + par
                        if head:
                            head(pair, e, par)
                        count, before = blocks_of(eng, e)
                        with eng.Fori(0, count) as i:
                            body(before + i, e, par, i)

            with nc.Block() as block:
                @block.sync
                def _(sp):
                    def load(g, e, par, i):
                        sp.wait_ge(xr_free, g + 1)
                        sp.dma_start(xr[:].rearrange("p (a h) c -> p a h c", a=1),
                                     rg[bass.ds(e * NBR + i, 1)].rearrange("a p h c -> p a h c")).then_inc(x_in, 16)
                    every_block(sp, load)
                    _, before = blocks_of(sp, E - 1)
                    count, _ = blocks_of(sp, E - 1)
                    load(before + count, E - 1, 1, 0)
                    sp.wait_ge(x_in, (before + count) * 16 + 16)
                    sp.sem_inc(sp_waits, 1)

                @block.tensor
                def _(pe):
                    def transposes(g):
                        pe.wait_ge(x_in, g * 16 + 16)
                        if not isinstance(g, int):
                            pe.wait_ge(xT_ready, g)
                        for k in range(KD):
                            for h in range(2):
                                last = nc.tensor.transpose(PS[:, 4, k * BLK + h * P:k * BLK + (h + 1) * P],
                                                           xr[:, h, k * P:(k + 1) * P], ident[:])
                        last.then_inc(x_psum, 1)

                    def one(g, e, par, i):
                        pe.wait_ge(xT_ready, g + 1)
                        for j in range(KH):
                            pe.wait_ge(h_ready, g * KH + j + 1)
                            for k in range(KD):
                                last = nc.tensor.matmul(PS[:, j % 4, 0:BLK], wfc[:, par, k, j * P:(j + 1) * P],
                                                        xT[:, k, :], start=k == 0, stop=k == KD - 1)
                            last.then_inc(h_psum, 1)
                        transposes(g + 1)
                        pe.wait_ge(h_ready, g * KH + KH + HELD)
                        for h in range(2):
                            pe.wait_ge(y_read, g * 2 + h + 1)
                            for j in range(KH):
                                last = nc.tensor.matmul(PS[:, 5 + h, 0:D], hid[:, j, h * P:(h + 1) * P],
                                                        wpr[:, par, j, :], start=j == 0, stop=j == KH - 1)
                            last.then_inc(y_psum, 1)

                    transposes(0)
                    every_block(pe, one, lambda pair, e, par: pe.wait_ge(e_w_in[par], pair * 48 + 48))

                @block.scalar
                def _(act):
                    act.sem_inc(h_ready, HELD)

                    def gelus(g, e, par, i):
                        for j in range(KH):
                            act.wait_ge(h_psum, g * KH + j + 1)
                            nc.scalar.activation(hid[:, j, :], PS[:, j % 4, 0:BLK], ACT.Gelu_apprx_tanh,
                                                 bias=bfc[:].rearrange("p e j -> p (e j)")[:, bass.ds(e * KH + j, 1)]
                                                 ).then_inc(h_ready, 1)

                    def pair_of(pair, reload):
                        for par in range(2):
                            e = pair * 2 + par
                            count, before = blocks_of(act, e)
                            with act.Fori(0, count) as i:
                                gelus(before + i, e, par, i)
                            if reload:
                                act.wait_ge(y_read, (before + count) * 2 + 2)
                                for dst, src in weights(par, e + 2):
                                    act.dma_start(dst, src).then_inc(e_w_in[par], 16)

                    with act.Fori(0, E // 2 - 1) as pair:
                        pair_of(pair, True)
                    pair_of(E // 2 - 1, False)

                @block.gpsimd
                def _(pool):
                    pool.sem_inc(y_sent, 1)

                    def send(g, e, par, i):
                        pool_wait(pool, y_ready, g * 2 + 2)
                        for h in range(2):
                            nc.gpsimd.indirect_dma_start(
                                out=out, out_offset=bass.IndirectOffsetOnAxis(ap=toki[:, h:h + 1], axis=0),
                                in_=y[:, h, :], in_offset=None, compute_op=ALU.add).then_inc(added, 16)
                        pool_wait(pool, added, g * 32 + 32)
                        pool.sem_inc(y_sent, 1)

                    every_block(pool, send)

                @block.vector
                def _(dve):
                    dve.sem_inc(y_read, 2)

                    def take(g):
                        dve.wait_ge(x_psum, g + 1)
                        nc.vector.tensor_copy(xT[:].rearrange("p k n -> p (k n)"), PS[:, 4, :]).then_inc(xT_ready, 1)
                        nc.vector.tensor_copy(meta[:], xr[:, :, D:ROW]).then_inc(xr_free, 1)

                    def one(g, e, par, i):
                        dve.wait_ge(xr_free, g + 2)
                        dve.wait_ge(y_sent, g + 1)
                        nc.vector.tensor_copy(gate[:], meta[:, :, bass.ds(e, 1)].rearrange("p h a -> p (h a)"))
                        nc.vector.tensor_copy(toki[:], meta[:, :, E]).then_inc(gate_ready, 1)
                        dve.wait_ge(gate_ready, g + 1)
                        take(g + 1)
                        for h in range(2):
                            dve.wait_ge(y_psum, g * 2 + h + 1)
                            nc.vector.tensor_tensor(y[:, h, :], PS[:, 5 + h, 0:D], bpr[:, par, :],
                                                    ALU.add).then_inc(y_read, 1)
                        for h in range(2):
                            dve.wait_ge(y_read, g * 2 + 3 + h)
                            nc.vector.tensor_scalar(y[:, h, :], y[:, h, :], gate[:, h:h + 1], None,
                                                    ALU.mult).then_inc(y_ready, 1)

                    dve.sem_inc(xr_free, 1)
                    take(0)
                    every_block(dve, one, lambda pair, e, par: dve.wait_ge(e_w_in[par], pair * 48 + 48))


def dump(nc, ctx, X, out, B, TB, P):
    s = ctx.enter_context(nc.semaphore("dumped"))
    with nc.Block() as block:
        @block.sync
        def _(sp):
            for b in range(B):
                sp.dma_start(out[b * TB * P:(b + 1) * TB * P, :].rearrange("(t p) d -> p t d", p=P),
                             X[:, b * TB:(b + 1) * TB, :]).then_inc(s, 16)
            sp.wait_ge(s, 16 * B)


def kernel(x, ctx_1024, L0_attn_W_in, L0_attn_conv_w, L0_attn_conv_b, L0_attn_W_x, L0_attn_W_dt, L0_attn_b_dt,
           L0_attn_A_log, L0_attn_D_skip, L0_attn_W_out, L0_xattn_Wq, L0_xattn_bq, L0_xattn_Wk, L0_xattn_bk,
           L0_xattn_Wv, L0_xattn_bv, L0_xattn_Wo, L0_xattn_bo, L0_ffn_Wfc_s, L0_ffn_bfc_s, L0_ffn_Wproj_s,
           L0_ffn_bproj_s, L0_ffn_Wr, L0_ffn_Wfc, L0_ffn_bfc, L0_ffn_Wproj, L0_ffn_bproj):
    import numpy as np
    import concourse.bacc as bacc
    from concourse import mybir
    from concourse.bass_utils import run_bass_kernel_spmd

    nd = np.asarray
    P = 128
    Bb, L, D = nd(x).shape
    S = nd(ctx_1024).shape[1]
    E, _, HID = nd(L0_ffn_Wfc).shape
    ROOM = Bb * L + 2 * P
    EI = nd(L0_attn_W_out).shape[1]
    HH = 8

    small = np.zeros((P, 64), np.float32)
    small[:, 0:HH] = np.arange(P)[:, None] // 16 == np.arange(HH)[None, :]
    small[:, 8:8 + E] = E - np.arange(E)
    small[:, 16] = np.arange(P)
    small[:, 17] = np.arange(P) + P
    small[:, 24:24 + E] = np.arange(E) * ROOM
    small[:, 32:40] = 1e-5
    small[:, 40:48] = -0.5
    causal = np.where(np.arange(S)[None, :] > np.arange(P)[:, None], np.float32(-1e30), np.float32(0))
    arrays = {
        "x": nd(x),
        "ctxT": np.ascontiguousarray(nd(ctx_1024).reshape(Bb * S, D).T).reshape(D // P, P, Bb * S),
        "W_inT": nd(L0_attn_W_in)[EI:].T, "W_xT": nd(L0_attn_W_x).T, "W_dtT": nd(L0_attn_W_dt).T,
        "b_dt": nd(L0_attn_b_dt).reshape(-1, P).T, "D_skip": nd(L0_attn_D_skip).reshape(-1, P).T,
        "A_log": nd(L0_attn_A_log), "W_outT": nd(L0_attn_W_out).T,
        "Wq": nd(L0_xattn_Wq), "Wk": nd(L0_xattn_Wk), "Wv": nd(L0_xattn_Wv), "Wo": nd(L0_xattn_Wo),
        "bq": nd(L0_xattn_bq).reshape(-1, P).T, "bk": nd(L0_xattn_bk).reshape(-1, P).T,
        "bv": nd(L0_xattn_bv).reshape(1, -1), "bo": nd(L0_xattn_bo).reshape(1, -1),
        "Wfc_s": nd(L0_ffn_Wfc_s), "bfc_s": nd(L0_ffn_bfc_s).reshape(-1, P).T,
        "Wproj_s": nd(L0_ffn_Wproj_s), "bproj_s": nd(L0_ffn_bproj_s).reshape(1, -1),
        "Wr": nd(L0_ffn_Wr), "Wfc": nd(L0_ffn_Wfc), "bfc": nd(L0_ffn_bfc).reshape(E, -1, P).transpose(2, 0, 1),
        "Wproj": nd(L0_ffn_Wproj), "bproj": nd(L0_ffn_bproj),
        "ident": np.eye(P, dtype=np.float32),
        "tri": np.triu(np.ones((P, P), np.float32), 1),
        "small": small, "causal": np.tile(causal, (1, HH)),
        "steps": np.tile(np.arange(1, L, dtype=np.float32), (P, 1)),
    }
    nc = bacc.Bacc("TRN2", target_bir_lowering=False, num_devices=1)
    feeds, aps = {}, {}
    for name, a in arrays.items():
        a = np.ascontiguousarray(a)
        feeds["in_" + name] = a
        aps[name] = nc.dram_tensor("in_" + name, a.shape, mybir.dt.from_np(a.dtype), kind="ExternalInput").ap()
    aps["out"] = nc.dram_tensor("out_rows", (ROOM, D), mybir.dt.float32, kind="ExternalOutput").ap()
    build(nc, aps, STOP)
    r = run_bass_kernel_spmd(nc, [feeds], core_ids=[0])
    return r.results[0]["out_rows"][:Bb * L].reshape(Bb, L, D)


STOP = 9
```

```python
def build(nc, d, stop=9):
    import concourse.bass as bass
    from concourse import mybir
    from contextlib import ExitStack

    BF16 = mybir.dt.bfloat16
    F32, F32R, I32 = mybir.dt.float32, mybir.dt.float32r, mybir.dt.int32
    ALU = mybir.AluOpType
    ACT = mybir.ActivationFunctionType
    AX = mybir.AxisListType.X

    P = 128
    B, L, D = d["x"].shape
    N = B * L
    TILES, TB = N // P, L // P
    KD = D // P
    S = d["ctxT"].shape[2] // B
    EI, NS = d["A_log"].shape
    KE = EI // P
    R = d["W_dtT"].shape[0]
    H = 16
    DK = D // H
    HH = H // KD
    NP = H // 2
    PW = 2 * DK + 2
    E = d["Wfc"].shape[0]
    HID = d["Wfc"].shape[2]
    KH = HID // P
    BLK = 2 * P
    ROOM = N + BLK
    NBR = ROOM // BLK
    ROW = 272
    GATE, TOK = D, D + E
    SCALE = DK ** -0.5
    BIG = 1e30

    out = d["out"]

    ctx = ExitStack()
    with ctx:
        class Place:
            def __init__(self, at):
                self.at = at

            def __call__(self, name, shape, dt=F32):
                held = 4
                for n in shape[1:]:
                    held *= n
                t = nc.alloc_sbuf_tensor_at(name, list(shape), dt, offset=self.at)
                self.at += -(-held // 64) * 64
                return t

        sb = Place(-(-nc.sbuf_base // 64) * 64)

        X = sb("X", [P, TILES, D])
        ident = sb("ident", [P, P])
        tri = sb("tri", [P, P])
        ones = sb("ones", [P, P])
        small = sb("small", [P, 64])
        headmask = small[:, 0:HH]
        tiew = small[:, 8:8 + E]
        rowno = small[:, 16:18]
        ebase = small[:, 24:24 + E]
        eps4, half4 = small[:, 32:32 + TB], small[:, 40:40 + TB]
        stats = sb("stats", [P, TB, 6])
        mv = sb("mv", [P, TB, 2])
        vare = sb("vare", [P, TB])
        rstd = sb("rstd", [P, TB])
        hn = sb("hn", [P, TB, D])
        PS = ctx.enter_context(nc.psum_tensor("PS", [P, 8, 512], F32))

        RG = nc.dram_tensor("routed_rows", [E * ROOM, ROW], F32, kind="Internal").ap()

        class Count:
            def __init__(self, sem):
                self.sem, self.n = sem, 0

            def inc(self, ins, by=1):
                ins.then_inc(self.sem, by)
                self.n += by
                return self.n

        def phase_sems(c, names):
            return [c.enter_context(nc.semaphore(n)) for n in names.split()]

        pool_waits = ctx.enter_context(nc.semaphore("pool_waits"))
        sp_waits = ctx.enter_context(nc.semaphore("sp_waits"))
        bn_waits = ctx.enter_context(nc.semaphore("bn_waits"))

        def pool_wait(pool, sem, value):
            pool.wait_ge(sem, value)
            pool.sem_inc(pool_waits, 1)

        def norm_stats(link, tiles):
            for t, src in enumerate(tiles):
                last = nc.vector.bn_stats(stats[:, t, :], src)
            link(last)
            nc.vector.sem_inc(bn_waits, 1)
            for t in range(len(tiles)):
                last = nc.vector.bn_aggr(mv[:, t, :], stats[:, t, :])
            return last

        def norm_rstd(pool, done, before):
            nc.gpsimd.tensor_tensor(vare[:], mv[:, :, 1], eps4, ALU.add).then_inc(done, 1)
            pool_wait(pool, done, before + 1)
            nc.gpsimd.tensor_tensor(rstd[:], vare[:], half4, ALU.pow).then_inc(done, 1)

        def norm_apply(tiles, dsts):
            for t, src in enumerate(tiles):
                last = nc.vector.tensor_scalar(dsts[t], src, mv[:, t, 0:1], rstd[:, t:t + 1],
                                               ALU.subtract, ALU.mult)
            return last

        def product(out, w, x, first=True, last=True):
            (wh, wl), (xh, xl) = w, x
            nc.tensor.matmul(out, wh, xh, start=first, stop=False)
            nc.tensor.matmul(out, wh, xl, start=False, stop=False)
            return nc.tensor.matmul(out, wl, xh, start=False, stop=last)

        fcraw = sb("fcraw", [P, KD, HID])
        prraw = sb("prraw", [P, KH, D])
        wfs = [sb("wfs" + n, [P, KD, HID], F32R) for n in "hl"]
        wps = [sb("wps" + n, [P, KH, D], F32R) for n in "hl"]
        mixer_and_attention = Place(sb.at)
        ab = mixer_and_attention
        causal = ab("causal", [P, HH * S])
        yD = ab("yD", [P, KE, L])
        hT = ab("hT", [P, KD, L])

        with ExitStack() as c:
            tmp = Place(ab.at)
            wx = tmp("wx", [P, KE, R + 2 * NS])
            wdt = tmp("wdt", [R, EI])
            bdt = tmp("bdt", [P, KE])
            dsk = tmp("dsk", [P, KE])
            alog = tmp("alog", [P, KE, NS])
            steps = tmp("steps", [P, L - 1])
            onesrow = tmp("onesrow", [P, L])
            dlt = tmp("dlt", [R, 1])
            bc = tmp("bc", [P, 2 * NS])
            dl = tmp("dl", [P, 8, KE])
            rate = tmp("rate", [P, KE, NS])
            coef = tmp("coef", [P, KE, NS])
            pw = tmp("pw", [P, 2, L - 1])
            kern = tmp("kern", [P, KE, L])
            (consts_in, x_in, w_in, small_mm, dve_done, act_done, pw_ready, pw_used,
             s_chain) = phase_sems(c, "consts_in x_in w_in small_mm dve_done act_done pw_ready pw_used s_chain")
            with nc.Block() as block:
                @block.sync
                def _(sp):
                    for dst, src in ((wx[:], d["W_xT"].rearrange("(k p) r -> p k r", p=P)),
                                     (wdt[:], d["W_dtT"]), (bdt[:], d["b_dt"]), (dsk[:], d["D_skip"]),
                                     (alog[:], d["A_log"].rearrange("(k p) n -> p k n", p=P)),
                                     (steps[:], d["steps"])):
                        sp.dma_start(dst, src).then_inc(w_in, 16)
                    for dst, src in ((ident[:], d["ident"]), (tri[:], d["tri"]),
                                     (small[:], d["small"]), (causal[:], d["causal"])):
                        sp.dma_start(dst, src).then_inc(consts_in, 16)
                    for b in range(B):
                        sp.dma_start(X[:, b * TB:(b + 1) * TB, :],
                                     d["x"][b].rearrange("(t p) d -> p t d", p=P)).then_inc(x_in, 16)
                    sp.wait_ge(consts_in, 64)
                    sp.wait_ge(x_in, 16 * B)

                @block.tensor
                def _(pe):
                    pe.wait_ge(w_in, 96)
                    pe.wait_ge(dve_done, 1)
                    for k in range(KE):
                        nc.tensor.matmul(PS[0:R, 0, 0:1], wx[:, k, 0:R], ones[:, 0:1],
                                         start=k == 0, stop=k == KE - 1)
                    for k in range(KE):
                        last = nc.tensor.matmul(PS[:, 1, 0:2 * NS], ones[:, :], wx[:, k, R:R + 2 * NS],
                                                start=k == 0, stop=k == KE - 1)
                    last.then_inc(small_mm, 1)
                    pe.wait_ge(dve_done, 2)
                    for k in range(KE):
                        last = nc.tensor.matmul(PS[:, 2, k:k + 1], wdt[:, k * P:(k + 1) * P], dlt[:],
                                                start=True, stop=True)
                    last.then_inc(small_mm, 1)

                @block.vector
                def _(dve):
                    n = [0]
                    def link(ins):
                        n[0] += 1
                        ins.then_inc(s_chain, 1)
                        dve.wait_ge(s_chain, n[0])
                    nc.vector.memset(onesrow[:], 1.0)
                    link(nc.vector.memset(kern[:], 0.0))
                    nc.vector.memset(ones[:], 1.0).then_inc(dve_done, 1)
                    dve.wait_ge(small_mm, 1)
                    nc.vector.tensor_copy(dlt[:], PS[0:R, 0, 0:1]).then_inc(dve_done, 1)
                    link(nc.vector.tensor_copy(bc[:], PS[:, 1, 0:2 * NS]))
                    dve.wait_ge(small_mm, 2)
                    t_, na, ex, u, ln, dlt_ = (dl[:, i, :] for i in range(6))
                    link(nc.vector.tensor_tensor(t_, PS[:, 2, 0:KE], bdt[:], ALU.add))
                    link(nc.vector.tensor_scalar(na, t_, -1.0, None, ALU.mult))
                    link(nc.vector.tensor_tensor(na, na, t_, ALU.min))
                    nc.vector.tensor_scalar(dl[:, 6, :], t_, 0.0, None, ALU.max).then_inc(dve_done, 1)
                    dve.wait_ge(act_done, 1)
                    nc.vector.tensor_scalar(u, ex, 1.0, None, ALU.add).then_inc(dve_done, 1)
                    dve.wait_ge(act_done, 2)
                    nc.vector.tensor_scalar(alog[:], alog[:], 88.7, None, ALU.min).then_inc(dve_done, 1)
                    link(nc.vector.tensor_tensor(ln, ln, ex, ALU.mult))
                    link(nc.vector.tensor_scalar(dl[:, 7, :], u, -1.0, 1e-30, ALU.add, ALU.max))
                    link(nc.vector.reciprocal(dl[:, 7, :], dl[:, 7, :]))
                    link(nc.vector.tensor_tensor(ln, ln, dl[:, 7, :], ALU.mult))
                    link(nc.vector.tensor_scalar(na, u, 1.0, None, ALU.is_equal))
                    link(nc.vector.tensor_tensor(na, na, ex, ALU.mult))
                    link(nc.vector.tensor_tensor(ln, ln, na, ALU.add))
                    link(nc.vector.tensor_tensor(dlt_, ln, dl[:, 6, :], ALU.add))
                    dve.wait_ge(act_done, 3)
                    link(nc.vector.tensor_scalar(rate[:], rate[:], -2.0 ** -40, None, ALU.mult))
                    for k in range(KE):
                        last = nc.vector.tensor_scalar(rate[:, k, :], rate[:, k, :], dlt_[:, k:k + 1],
                                                       None, ALU.mult)
                    link(last)
                    nc.vector.tensor_scalar(rate[:], rate[:], -1e4 * 2.0 ** -40, 2.0 ** 40, ALU.max,
                                            ALU.mult).then_inc(dve_done, 1)
                    link(nc.vector.tensor_tensor(bc[:, 0:NS], bc[:, 0:NS], bc[:, NS:2 * NS], ALU.mult))
                    for k in range(KE):
                        last = nc.vector.tensor_scalar(coef[:, k, :], bc[:, 0:NS], dlt_[:, k:k + 1],
                                                       None, ALU.mult)
                    link(last)
                    link(nc.vector.reduce_sum(kern[:, :, 0], coef[:], axis=AX))
                    for k in range(KE):
                        for m in range(NS):
                            i = k * NS + m
                            dve.wait_ge(pw_ready, i + 1)
                            nc.vector.scalar_tensor_tensor(
                                kern[:, k, 1:L], pw[:, i % 2, :], coef[:, k, m:m + 1], kern[:, k, 1:L],
                                ALU.mult, ALU.add).then_inc(pw_used, 1)
                            dve.wait_ge(pw_used, i + 1)
                    for k in range(KE):
                        last = nc.vector.tensor_tensor_scan(yD[:, k, :], onesrow[:], kern[:, k, :],
                                                            dsk[:, k:k + 1], ALU.mult, ALU.add)
                    link(last)

                @block.scalar
                def _(act):
                    act.wait_ge(dve_done, 3)
                    nc.scalar.activation(dl[:, 2, :], dl[:, 1, :], ACT.Exp).then_inc(act_done, 1)
                    act.wait_ge(dve_done, 4)
                    nc.scalar.activation(dl[:, 4, :], dl[:, 3, :], ACT.Ln).then_inc(act_done, 1)
                    act.wait_ge(dve_done, 5)
                    nc.scalar.activation(rate[:], alog[:], ACT.Exp).then_inc(act_done, 1)
                    act.wait_ge(dve_done, 6)
                    for k in range(KE):
                        for m in range(NS):
                            i = k * NS + m
                            if i >= 2:
                                act.wait_ge(pw_used, i - 1)
                            nc.scalar.activation(pw[:, i % 2, :], steps[:], ACT.Exp,
                                                 scale=rate[:, k, m:m + 1]).then_inc(pw_ready, 1)

        with ExitStack() as c:
            tmp = Place(ab.at)
            win = tmp("win", [P, KD, EI])
            wout = tmp("wout", [P, KE, D])
            sz = tmp("sz", [P, KE, L])
            g = tmp("g", [P, KE, L])
            (w_in, hn_var, hn_rstd, hn_ready, hT_psum, hT_ready, z_psum, sz_ready, g_ready, o_psum, x1_ready,
             s_chain) = phase_sems(c, "a_w_in a_hn_var a_hn_rstd a_hn_ready a_hT_psum a_hT_ready a_z_psum a_sz_ready a_g_ready a_o_psum a_x1_ready a_chain")
            with nc.Block() as block:
                @block.sync
                def _(sp):
                    sp.dma_start(win[:], d["W_inT"].rearrange("(k p) e -> p k e", p=P)).then_inc(w_in, 16)
                    sp.dma_start(wout[:], d["W_outT"].rearrange("(k p) e -> p k e", p=P)).then_inc(w_in, 16)

                @block.tensor
                def _(pe):
                    def transposes(b):
                        pe.wait_ge(hn_ready, b + 1)
                        for t in range(TB):
                            for k in range(KD):
                                last = nc.tensor.transpose(PS[:, 4 + k, t * P:(t + 1) * P],
                                                           hn[:, t, k * P:(k + 1) * P], ident[:])
                        last.then_inc(hT_psum, 1)

                    def z_part(b):
                        pe.wait_ge(hT_ready, KD * b + KD)
                        for e in range(KE):
                            for k in range(KD):
                                last = nc.tensor.matmul(PS[:, e, :], win[:, k, e * P:(e + 1) * P], hT[:, k, :],
                                                        start=k == 0, stop=k == KD - 1)
                            last.then_inc(z_psum, 1)

                    def out_part(b):
                        pe.wait_ge(g_ready, KE * b + KE)
                        pe.wait_ge(x1_ready, 2 * b + 2)
                        for t in range(TB):
                            for e in range(KE):
                                last = nc.tensor.matmul(PS[:, 6 + t // 2, (t % 2) * D:(t % 2 + 1) * D],
                                                        g[:, e, t * P:(t + 1) * P], wout[:, e, :],
                                                        start=e == 0, stop=e == KE - 1)
                            if t % 2:
                                last.then_inc(o_psum, 1)

                    pe.wait_ge(w_in, 32)
                    transposes(0)
                    with pe.Fori(0, B - 1) as b:
                        z_part(b)
                        transposes(b + 1)
                        out_part(b)
                    z_part(B - 1)
                    out_part(B - 1)

                @block.scalar
                def _(act):
                    def evac(b):
                        act.wait_ge(hT_psum, b + 1)
                        for k in range(KD):
                            nc.scalar.activation(hT[:, k, :], PS[:, 4 + k, :], ACT.Copy).then_inc(hT_ready, 1)

                    def silu(b):
                        for e in range(KE):
                            act.wait_ge(z_psum, KE * b + e + 1)
                            if not isinstance(b, int) or b:
                                act.wait_ge(g_ready, KE * (b - 1) + e + 1)
                            nc.scalar.activation(sz[:, e, :], PS[:, e, :], ACT.Silu).then_inc(sz_ready, 1)

                    evac(0)
                    silu(0)
                    with act.Fori(1, B) as b:
                        evac(b)
                        silu(b)

                @block.vector
                def _(dve):
                    base = [0]
                    n = [0]
                    def link(ins):
                        n[0] += 1
                        ins.then_inc(s_chain, 1)
                        dve.wait_ge(s_chain, base[0] + n[0])

                    def tiles(b):
                        return [X[:, TB * b + t, :] for t in range(TB)]

                    def stats_part(b):
                        norm_stats(link, tiles(b)).then_inc(hn_var, 1)

                    def apply_part(b):
                        if not isinstance(b, int) or b:
                            dve.wait_ge(hT_psum, b)
                        dve.wait_ge(hn_rstd, 2 * b + 2)
                        norm_apply(tiles(b), [hn[:, t, :] for t in range(TB)]).then_inc(hn_ready, 1)

                    def gate(b, e):
                        dve.wait_ge(sz_ready, KE * b + e + 1)
                        nc.vector.tensor_tensor(g[:, e, :], sz[:, e, :], yD[:, e, :],
                                                ALU.mult).then_inc(g_ready, 1)

                    def residual(b):
                        for i in range(2):
                            dve.wait_ge(o_psum, 2 * b + i + 1)
                            xs = X[:, bass.ds(TB * b + 2 * i, 2), :].rearrange("p t d -> p (t d)")
                            nc.vector.tensor_tensor(xs, xs, PS[:, 6 + i, :], ALU.add).then_inc(x1_ready, 1)

                    dve.sem_inc(x1_ready, 2)
                    stats_part(0)
                    apply_part(0)
                    with dve.Fori(0, B - 1) as b:
                        n[0] = 0
                        base[0] = b + 1
                        stats_part(b + 1)
                        gate(b, 0)
                        apply_part(b + 1)
                        for e in range(1, KE):
                            gate(b, e)
                        residual(b)
                    for e in range(KE):
                        gate(B - 1, e)
                    residual(B - 1)
                    dve.wait_ge(x1_ready, 2 * B + 2)

                @block.gpsimd
                def _(pool):
                    with pool.Fori(0, B) as b:
                        pool_wait(pool, hn_var, b + 1)
                        norm_rstd(pool, hn_rstd, 2 * b)

        if stop == 1:
            dump(nc, ctx, X, out, B, TB, P)
            return

        def low(eng, out, whole, high):
            return eng.tensor_tensor(out, whole, high.bitcast(F32), ALU.subtract)

        with ExitStack() as c:
            tmp = Place(ab.at)
            wq, wk, wv, wo = (tmp(n, [P, KD, D]) for n in ("wq", "wk", "wv", "wo"))
            bq, bk = tmp("bq", [P, KD]), tmp("bk", [P, KD])
            bv = tmp("bv", [1, D])
            bo = tmp("bo", [P, D])
            ctx2 = tmp("ctx2", [P, KD, B, 2, S])
            kT = tmp("kT", [P, KD, B, S])
            kbd = tmp("kbd", [P, B, KD, HH * S])
            vbd = tmp("vbd", [P, B, NP * PW])
            qT = tmp("qT", [P, KD, L])
            pr = tmp("pr", [P, 2, H * S])
            prT = tmp("prT", [P, NP, P])
            mx = tmp("mx", [P, 2, H])
            den = tmp("den", [P, H])
            o = tmp("o", [P, D])
            oT = tmp("oT", [P, KD, P])
            (w_in, k_psum, kT_ready, k_ready, v_psum, v_ready, vz,
             hn_var, hn_rstd, hn_ready, hT_psum, hT_ready, q_psum, qT_ready, bo_added,
             s_psum, s_max, s_shift, p_ready, pT_psum, pT_ready, o_psum, o_den, o_ready, oT_psum, oT_ready,
             y_psum, x2_ready, s_chain, ws_in, ws_high, ws_low) = phase_sems(c, """b_w_in b_k_psum b_kT_ready b_k_ready
                b_v_psum b_v_ready b_vz b_hn_var b_hn_rstd b_hn_ready b_hT_psum b_hT_ready b_q_psum b_qT_ready
                b_bo_added b_s_psum b_s_max b_s_shift b_p_ready b_pT_psum b_pT_ready b_o_psum b_o_den b_o_ready
                b_oT_psum b_oT_ready b_y_psum b_x2_ready b_chain b_ws_in b_ws_high
                b_ws_low""")
            with nc.Block() as block:
                @block.sync
                def _(sp):
                    for w, n in ((wk, "Wk"), (wv, "Wv"), (wq, "Wq"), (wo, "Wo")):
                        sp.dma_start(w[:], d[n].rearrange("(k p) e -> p k e", p=P)).then_inc(w_in, 16)
                    for j in range(2):
                        for k in range(KD):
                            sp.dma_start(ctx2[:, k, :, j, :],
                                         d["ctxT"][k].rearrange("p (b s) -> p b s", s=S)).then_inc(w_in, 16)
                    sp.dma_start(bq[:], d["bq"]).then_inc(w_in, 16)
                    sp.dma_start(bk[:], d["bk"]).then_inc(w_in, 16)
                    sp.dma_start(bv[:], d["bv"]).then_inc(w_in, 16)
                    sp.dma_start(bo[:], d["bo"].to_broadcast([P, D])).then_inc(w_in, 16)
                    sp.dma_start(fcraw[:], d["Wfc_s"].rearrange("(k p) e -> p k e", p=P)).then_inc(ws_in, 16)
                    sp.dma_start(prraw[:], d["Wproj_s"].rearrange("(k p) e -> p k e", p=P)).then_inc(ws_in, 16)
                W_IN = 16 * 12

                @block.tensor
                def _(pe):
                    pe.wait_ge(w_in, W_IN)
                    for m in range(KD):
                        for k in range(KD):
                            last = nc.tensor.matmul(PS[:, m, :], wk[:, k, m * P:(m + 1) * P],
                                                    ctx2[:, k, :, 0, :], start=k == 0, stop=k == KD - 1)
                        last.then_inc(k_psum, 1)
                    for b in range(B):
                        if b >= 2:
                            pe.wait_ge(v_ready, 2 * (b - 1))
                        for k in range(KD):
                            nc.tensor.matmul(PS[:, 2 + b % 2, 0:D], ctx2[:, k, b, :, :], wv[:, k, :],
                                             start=k == 0, stop=False)
                        nc.tensor.matmul(PS[:, 2 + b % 2, 0:D], ones[0:1, :], bv[:], start=False,
                                         stop=True).then_inc(v_psum, 1)

                    def transpose_x(j, t):
                        pe.wait_ge(hn_ready, j + 1)
                        if not isinstance(j, int) or j:
                            pe.wait_ge(hT_ready, j)
                        for k in range(KD):
                            last = nc.tensor.transpose(PS[:, 6, k * P:(k + 1) * P],
                                                       hn[:, t, k * P:(k + 1) * P], ident[:])
                        last.then_inc(hT_psum, 1)

                    def project_q(b):
                        pe.wait_ge(hT_ready, TB * b + TB)
                        if not isinstance(b, int) or b:
                            pe.wait_ge(s_shift, KD * TB * b)
                        for m in range(KD):
                            for k in range(KD):
                                last = nc.tensor.matmul(PS[:, m, :], wq[:, k, m * P:(m + 1) * P], hT[:, k, :],
                                                        start=k == 0, stop=k == KD - 1)
                            last.then_inc(q_psum, 1)

                    def scores(b, t):
                        i = TB * b + t
                        pe.wait_ge(qT_ready, KD * b + KD)
                        for m in range(KD):
                            if not isinstance(i, int) or i:
                                pe.wait_ge(s_shift, KD * (i - 1) + m + 1)
                            last = nc.tensor.matmul(PS[:, m, :], qT[:, m, t * P:(t + 1) * P],
                                                    kbd[:, bass.ds(b, 1), m, :].rearrange("p a n -> p (a n)"),
                                                    start=True, stop=t > 0)
                            if t == 0:
                                last = nc.tensor.matmul(PS[:, m, :], ident[:], causal[:], start=False,
                                                        stop=True)
                            last.then_inc(s_psum, 1)

                    def transpose_p(i, par):
                        pe.wait_ge(p_ready, i + 1)
                        if not isinstance(i, int) or i:
                            pe.wait_ge(pT_ready, i)
                        for j in range(NP):
                            last = nc.tensor.transpose(PS[:, 2 + j // 4, (j % 4) * P:(j % 4 + 1) * P],
                                                       pr[:, par, j * P:(j + 1) * P], ident[:])
                        last.then_inc(pT_psum, 1)

                    def weigh_values(i, b):
                        pe.wait_ge(pT_ready, i + 1)
                        if not isinstance(i, int) or i:
                            pe.wait_ge(o_ready, i)
                        for j in range(NP):
                            last = nc.tensor.matmul(
                                PS[:, 4, j * PW:(j + 1) * PW], prT[:, j, :],
                                vbd[:, bass.ds(b, 1), j * PW:(j + 1) * PW].rearrange("p a n -> p (a n)"),
                                start=True, stop=True)
                        last.then_inc(o_psum, 1)

                    def transpose_o(i):
                        pe.wait_ge(o_ready, i + 1)
                        if not isinstance(i, int) or i:
                            pe.wait_ge(oT_ready, i)
                        for k in range(KD):
                            last = nc.tensor.transpose(PS[:, 7, k * P:(k + 1) * P],
                                                       o[:, k * P:(k + 1) * P], ident[:])
                        last.then_inc(oT_psum, 1)

                    def project_o(i):
                        pe.wait_ge(oT_ready, i + 1)
                        if not isinstance(i, int) or i:
                            pe.wait_ge(x2_ready, i)
                        for k in range(KD):
                            last = nc.tensor.matmul(PS[:, 5, 0:D], oT[:, k, :], wo[:, k, :],
                                                    start=k == 0, stop=k == KD - 1)
                        last.then_inc(y_psum, 1)

                    def step(b, t, scored=True, following=True, lag2=True, lag3=True):
                        i = TB * b + t
                        if lag2:
                            transpose_p(i - 2, t % 2)
                        if scored:
                            scores(b, t)
                        if lag3:
                            transpose_o(i - 3)
                        if following:
                            transpose_x(i + TB, t)
                        if lag2:
                            weigh_values(i - 2, b if t >= 2 else b - 1)
                        if lag3:
                            project_o(i - 3)
                        if following and t == TB - 1:
                            project_q(b + 1)

                    pe.wait_ge(k_ready, 1)
                    pe.wait_ge(kT_ready, KD)
                    pe.wait_ge(vz, 3)
                    pe.wait_ge(v_ready, 2 * B)
                    for t in range(TB):
                        transpose_x(t, t)
                    project_q(0)
                    for t in range(TB):
                        step(0, t, lag2=t >= 2, lag3=t >= 3)
                    with pe.Fori(1, B - 1) as b:
                        for t in range(TB):
                            step(b, t)
                    for t in range(TB):
                        step(B - 1, t, following=False)
                    for t in range(3):
                        step(B, t, scored=False, following=False, lag2=t < 2)

                @block.scalar
                def _(act):
                    for b in range(B):
                        act.wait_ge(v_psum, b + 1)
                        if b == 0:
                            act.wait_ge(vz, 1)
                        for h in range(2):
                            rows = slice(h * S, (h + 1) * S)
                            dst = vbd[rows, b, :].rearrange("p (j c) -> p j c", c=PW)[:, :, h * DK:(h + 1) * DK]
                            src = PS[rows, 2 + b % 2, 0:D].rearrange("p (j c) -> p j c", c=2 * DK)
                            nc.scalar.activation(dst, src[:, :, h * DK:(h + 1) * DK],
                                                 ACT.Copy).then_inc(v_ready, 1)

                    def evac_x(j, t):
                        act.wait_ge(hT_psum, j + 1)
                        nc.scalar.activation(hT[:, :, t * P:(t + 1) * P],
                                             PS[:, 6, 0:D].rearrange("p (k n) -> p k n", k=KD),
                                             ACT.Copy).then_inc(hT_ready, 1)

                    def evac_q(b):
                        for m in range(KD):
                            act.wait_ge(q_psum, KD * b + m + 1)
                            nc.scalar.activation(qT[:, m, :], PS[:, m, :], ACT.Identity,
                                                 bias=bq[:, m:m + 1]).then_inc(qT_ready, 1)

                    def evac_p(i):
                        act.wait_ge(pT_psum, i + 1)
                        nc.scalar.activation(prT[:].rearrange("p j n -> p (j n)"),
                                             PS[:, 2:4, :].rearrange("p a n -> p (a n)"),
                                             ACT.Copy).then_inc(pT_ready, 1)

                    def evac_o(i):
                        act.wait_ge(oT_psum, i + 1)
                        nc.scalar.activation(oT[:].rearrange("p k n -> p (k n)"), PS[:, 7, 0:D],
                                             ACT.Copy).then_inc(oT_ready, 1)

                    def exps(i, par):
                        act.wait_ge(s_shift, KD * i + KD)
                        nc.scalar.activation(pr[:, par, :], pr[:, par, :], ACT.Exp,
                                             scale=SCALE).then_inc(p_ready, 1)

                    def step(b, t, scored=True, following=True, lag2=True, lag3=True):
                        i = TB * b + t
                        if lag2:
                            evac_p(i - 2)
                        if lag3:
                            evac_o(i - 3)
                        if following:
                            evac_x(i + TB, t)
                        if scored:
                            exps(i, t % 2)
                        if following and t == TB - 1:
                            evac_q(b + 1)

                    act.wait_ge(ws_in, 32)
                    nc.scalar.activation(wfs[0][:], fcraw[:], ACT.Copy).then_inc(ws_high, 1)
                    nc.scalar.activation(wps[0][:], prraw[:], ACT.Copy).then_inc(ws_high, 1)
                    act.wait_ge(w_in, W_IN)
                    for t in range(TB):
                        evac_x(t, t)
                    evac_q(0)
                    for t in range(TB):
                        step(0, t, lag2=t >= 2, lag3=t >= 3)
                    with act.Fori(1, B - 1) as b:
                        for t in range(TB):
                            step(b, t)
                    for t in range(TB):
                        step(B - 1, t, following=False)
                    for t in range(3):
                        step(B, t, scored=False, following=False, lag2=t < 2)

                @block.gpsimd
                def _(pool):
                    nc.gpsimd.memset(vbd[:], 0.0).then_inc(vz, 1)
                    pool_wait(pool, vz, 1)
                    for h in range(2):
                        v = vbd[h * S:(h + 1) * S, :, :].rearrange("p b (j c) -> p b j c", c=PW)
                        nc.gpsimd.memset(v[:, :, :, 2 * DK + h:2 * DK + h + 1], 1.0).then_inc(vz, 1)
                        pool_wait(pool, vz, 2 + h)

                    def rstds(i):
                        pool_wait(pool, hn_var, i + 1)
                        norm_rstd(pool, hn_rstd, 2 * i)

                    pool_wait(pool, w_in, W_IN)
                    rstds(0)
                    pool_wait(pool, kT_ready, KD)
                    for b in range(B):
                        for m in range(KD):
                            dst = kbd[:, b, m, :].rearrange("p (h s) -> p h s", s=S)
                            last = nc.gpsimd.tensor_tensor(
                                dst, kT[:, m, b, :].unsqueeze(1).to_broadcast([P, HH, S]),
                                headmask.unsqueeze(2).to_broadcast([P, HH, S]), ALU.mult)
                    last.then_inc(k_ready, 1)

                    def add_bo(b):
                        pool_wait(pool, hn_ready, TB * b + TB)
                        xs = X[:, bass.ds(TB * b, TB), :]
                        nc.gpsimd.tensor_tensor(xs, xs, bo[:].unsqueeze(1).to_broadcast([P, TB, D]),
                                                ALU.add).then_inc(bo_added, 1)
                    add_bo(0)
                    rstds(1)
                    add_bo(1)
                    pool_wait(pool, ws_high, 2)
                    low(nc.gpsimd, wfs[1][:], fcraw[:], wfs[0][:]).then_inc(ws_low, 1)
                    low(nc.gpsimd, wps[1][:], prraw[:], wps[0][:]).then_inc(ws_low, 1)
                    with pool.Fori(2, B) as b:
                        rstds(b)
                        add_bo(b)

                @block.vector
                def _(dve):
                    base = [0]
                    n = [0]
                    def link(ins):
                        n[0] += 1
                        ins.then_inc(s_chain, 1)
                        dve.wait_ge(s_chain, base[0] + n[0])

                    for m in range(KD):
                        dve.wait_ge(k_psum, m + 1)
                        nc.vector.tensor_scalar(kT[:, m, :, :].rearrange("p b s -> p (b s)"), PS[:, m, :],
                                                bk[:, m:m + 1], None, ALU.add).then_inc(kT_ready, 1)

                    def tile(j):
                        return X[:, bass.ds(j, 1), :].rearrange("p a d -> p (a d)")

                    def stats_part(b):
                        norm_stats(link, [tile(TB * b + t) for t in range(TB)]).then_inc(hn_var, 1)

                    def apply_part(b, t):
                        j = TB * b + t
                        if t == 0:
                            dve.wait_ge(hn_rstd, 2 * b + 2)
                        if not isinstance(j, int) or j >= TB:
                            dve.wait_ge(hT_psum, j - TB + 1)
                        nc.vector.tensor_scalar(hn[:, t, :], tile(j), mv[:, t, 0:1], rstd[:, t:t + 1],
                                                ALU.subtract, ALU.mult).then_inc(hn_ready, 1)

                    def shift(i, par):
                        for m in range(KD):
                            dve.wait_ge(s_psum, KD * i + m + 1)
                            nc.vector.tensor_reduce(mx[:, par, m * HH:(m + 1) * HH],
                                                    PS[:, m, :].rearrange("p (h s) -> p h s", s=S),
                                                    op=ALU.max, axis=AX).then_inc(s_max, 1)
                        if not isinstance(i, int) or i >= 2:
                            dve.wait_ge(pT_psum, i - 1)
                        for m in range(KD):
                            dve.wait_ge(s_max, KD * i + m + 1)
                            nc.vector.tensor_tensor(
                                pr[:, par, m * HH * S:(m + 1) * HH * S].rearrange("p (h s) -> p h s", s=S),
                                PS[:, m, :].rearrange("p (h s) -> p h s", s=S),
                                mx[:, par, m * HH:(m + 1) * HH].unsqueeze(2).to_broadcast([P, HH, S]),
                                ALU.subtract).then_inc(s_shift, 1)

                    def divide(i):
                        dve.wait_ge(o_psum, i + 1)
                        ps = PS[:, 4, 0:NP * PW].rearrange("p (j c) -> p j c", c=PW)
                        nc.vector.reciprocal(den[:].rearrange("p (j c) -> p j c", c=2),
                                             ps[:, :, 2 * DK:PW]).then_inc(o_den, 1)
                        dve.wait_ge(o_den, i + 1)
                        src = ps[:, :, 0:2 * DK].rearrange("p j (c e) -> p j c e", c=2)
                        nc.vector.tensor_tensor(
                            o[:].rearrange("p (j c e) -> p j c e", j=NP, c=2), src,
                            den[:].rearrange("p (j c) -> p j c", c=2).unsqueeze(3).to_broadcast([P, NP, 2, DK]),
                            ALU.mult).then_inc(o_ready, 1)

                    def residual(i, b):
                        dve.wait_ge(bo_added, b + 1)
                        dve.wait_ge(y_psum, i + 1)
                        nc.vector.tensor_tensor(tile(i), tile(i), PS[:, 5, 0:D], ALU.add).then_inc(x2_ready, 1)

                    def step(b, t, scored=True, following=True, lag3=True, lag4=True):
                        i = TB * b + t
                        if lag3:
                            divide(i - 3)
                        if lag4:
                            residual(i - 4, b - 1)
                        if following:
                            apply_part(b + 1, t)
                        if scored:
                            shift(i, t % 2)

                    dve.wait_ge(w_in, W_IN)
                    stats_part(0)
                    for t in range(TB):
                        apply_part(0, t)
                    dve.wait_ge(hn_ready, TB)
                    stats_part(1)
                    for t in range(TB):
                        step(0, t, lag3=t >= 3, lag4=False)
                    with dve.Fori(1, B - 1) as b:
                        n[0] = 0
                        base[0] = b + 1
                        dve.wait_ge(hn_ready, TB * b + TB)
                        stats_part(b + 1)
                        for t in range(TB):
                            step(b, t)
                    for t in range(TB):
                        step(B - 1, t, following=False)
                    for t in range(TB):
                        step(B, t, scored=False, following=False, lag3=t < 3)
                    dve.wait_ge(x2_ready, N // P)

        if stop == 2:
            dump(nc, ctx, X, out, B, TB, P)
            return

        with ExitStack() as c:
            tmp = Place(sb.at)
            wfc = [tmp("wfc" + n, [P, 2, KD, HID], F32R) for n in "hl"]
            wpr = [tmp("wpr" + n, [P, 2, KH, D], F32R) for n in "hl"]
            bfc = tmp("bfc", [P, E, KH])
            carry = tmp("carry", [P, E])
            (w_in, hn_var, hn_rstd, hn_ready, hT_psum, hT_ready, h_psum, h_ready, y_psum, x3_ready,
             l_psum, l_read, chosen, r_psum, r_read, gates_exp, slots_ready, rows_ready, hn_copied, scattered,
             bias_added, carry_ready, pads_stored, stored, s_chain, pads_zeroed, wr_split, hT_high,
             l_ready, raw_in, e_high, e_low) = phase_sems(
                ctx, """c_w_in c_hn_var c_hn_rstd c_hn_ready c_hT_psum c_hT_ready c_h_psum c_h_ready c_y_psum
                c_x3_ready c_l_psum c_l_read c_chosen c_r_psum c_r_read c_gates_exp c_slots_ready c_rows_ready
                c_hn_copied c_scattered c_bias_added c_carry_ready c_pads_stored c_stored c_chain
                c_pads_zeroed c_wr_split c_hT_high c_l_ready c_raw_in c_e_high c_e_low""")
            HELD = 4
            tbl = tmp("tbl", [P, 2 * E], I32)

            def load_weights(pool, e):
                pool.dma_start(fcraw[:], d["Wfc"][bass.ds(e, 1)].rearrange("a (k p) n -> p (a k) n", p=P)).then_inc(raw_in, 16)
                pool.dma_start(prraw[:], d["Wproj"][bass.ds(e, 1)].rearrange("a (k p) n -> p (a k) n", p=P)).then_inc(raw_in, 16)

            def split_high(par):
                nc.scalar.activation(wfc[0][:, par], fcraw[:], ACT.Copy).then_inc(e_high, 1)
                nc.scalar.activation(wpr[0][:, par], prraw[:], ACT.Copy).then_inc(e_high, 1)

            experts_at = tmp.at
            if True:
                tm = Place(experts_at)
                wr = tm("wr", [P, KD, E])
                wrp = [tm("wr" + n, [P, KD, E], F32R) for n in "hl"]
                xTp = [tm("xT" + n, [P, KD, L], F32R) for n in "hl"]
                bfs = tm("bfs", [P, KH])
                bps = tm("bps", [P, D])
                act32 = tm("act32", [P, 2, L])
                hid = [tm("hid" + n, [P, KH, L], F32R) for n in "hl"]
                rows = tm("rows", [P, TB, ROW])
                pads = tm("pads", [P, 2, ROW])
                tok = tm("tok", [P, TB])
                lg = tm("lg", [P, 8, TB, E])
                oh = tm("oh", [P, 2, TB, E])
                both = tm("both", [P, TB, E], BF16)
                triones = tm("triones", [P, 2, P], BF16)
                m4 = tm("m4", [P, 8, TB])
                meta = tm("meta", [P, TB, ROW - D])
                slot = tm("slot", [P, TB, 2], I32)
                slotc = tm("slotc", [P, TB, 2], I32)
                ends = tm("ends", [P, E], I32)
                cnt = tm("cnt", [P, 4, E])
                cmp_ = tm("cmp", [P, E, NBR - 1])
                W_IN = 16 * 4
                with nc.Block() as block:
                    @block.sync
                    def _(sp):
                        for dst, src in ((wr[:], d["Wr"].rearrange("(k p) e -> p k e", p=P)),
                                         (bfs[:], d["bfc_s"]), (bps[:], d["bproj_s"].to_broadcast([P, D])),
                                         (bfc[:], d["bfc"])):
                            sp.dma_start(dst, src).then_inc(w_in, 16)
                        ov = out.rearrange("(t p) d -> p t d", p=P)
                        with sp.Fori(0, B) as b:
                            sp.wait_ge(x3_ready, TB * b + 2 * TB)
                            sp.dma_start(ov[:, bass.ds(TB * b, TB), :], X[:, bass.ds(TB * b, TB), :]).then_inc(stored, 16)
                        sp.wait_ge(pads_zeroed, 1)
                        sp.dma_start(out[N:N + BLK, :].rearrange("(h p) d -> p h d", p=P),
                                     pads[:, :, 0:D]).then_inc(stored, 16)
                        sp.wait_ge(carry_ready, 1)
                        for e in range(E):
                            end = sp.value_load(ends[0:1, e:e + 1], min_val=e * ROOM, max_val=e * ROOM + N)
                            sp.dma_start(RG[bass.ds(end, BLK), :].rearrange("(h p) c -> p h c", p=P),
                                         pads[:]).then_inc(pads_stored, 16)
                        sp.wait_ge(stored, 16 * B + 16)
                        sp.wait_ge(pads_stored, 16 * E)

                    @block.tensor
                    def _(pe):
                        def transposes(b):
                            pe.wait_ge(hn_ready, b + 1)
                            if not isinstance(b, int) or b:
                                pe.wait_ge(r_read, b)
                            for t in range(TB):
                                for k in range(KD):
                                    last = nc.tensor.transpose(PS[:, 4 + k, t * P:(t + 1) * P],
                                                               hn[:, t, k * P:(k + 1) * P], ident[:])
                            last.then_inc(hT_psum, 1)

                        def up(b):
                            pe.wait_ge(hT_ready, KD * b + KD)
                            for j in range(KH):
                                pe.wait_ge(h_ready, KH * b + j + 1)
                                js = slice(j * P, (j + 1) * P)
                                for k in range(KD):
                                    last = product(PS[:, j % 4, :], [w[:, k, js] for w in wfs],
                                                   [x[:, k, :] for x in xTp], k == 0, k == KD - 1)
                                last.then_inc(h_psum, 1)

                        def logits(b):
                            pe.wait_ge(hT_ready, KD * b + KD)
                            for t in range(TB):
                                for k in range(KD):
                                    last = product(PS[:, 4, t * E:(t + 1) * E],
                                                   [x[:, k, t * P:(t + 1) * P] for x in xTp],
                                                   [w[:, k, :] for w in wrp], k == 0, k == KD - 1)
                            last.then_inc(l_psum, 1)

                        def ranks(b):
                            pe.wait_ge(chosen, b + 1)
                            for t in range(TB):
                                for s in range(t + 1):
                                    last = nc.tensor.matmul(PS[:, 5, t * E:(t + 1) * E],
                                                            triones[:, 0 if s == t else 1, :], both[:, s, :],
                                                            start=s == 0, stop=s == t)
                            for s in range(TB):
                                last = nc.tensor.matmul(PS[:, 5, TB * E:(TB + 1) * E], triones[:, 1, :], both[:, s, :],
                                                        start=s == 0, stop=s == TB - 1)
                            last.then_inc(r_psum, 1)

                        def down(b, tiles):
                            for t in tiles:
                                if t % 2 == 0:
                                    pe.wait_ge(x3_ready, TB * b + t + 2)
                                for j in range(KH):
                                    if t == 0:
                                        pe.wait_ge(l_ready, KH * b + j + 1 + 2)
                                    last = product(PS[:, 6 + t // 2, (t % 2) * D:(t % 2 + 1) * D],
                                                   [h[:, j, t * P:(t + 1) * P] for h in hid],
                                                   [w[:, j, :] for w in wps], j == 0, j == KH - 1)
                                if t % 2:
                                    last.then_inc(y_psum, 1)

                        pe.wait_ge(wr_split, 2)
                        transposes(0)
                        logits(0)
                        with pe.Fori(0, B - 1) as b:
                            up(b)
                            ranks(b)
                            transposes(b + 1)
                            down(b, range(TB // 2))
                            logits(b + 1)
                            down(b, range(TB // 2, TB))
                        up(B - 1)
                        ranks(B - 1)
                        down(B - 1, range(TB))

                    @block.scalar
                    def _(act):
                        def evac(b):
                            act.wait_ge(hT_psum, b + 1)
                            for k in range(KD):
                                nc.scalar.activation(xTp[0][:, k, :], PS[:, 4 + k, :], ACT.Copy).then_inc(hT_high, 1)

                        def gelus(b):
                            for j in range(KH):
                                act.wait_ge(h_psum, KH * b + j + 1)
                                nc.scalar.activation(hid[0][:, j, :], PS[:, j % 4, :], ACT.Gelu_apprx_tanh,
                                                     bias=bfs[:, j:j + 1])
                                act.wait_ge(l_ready, KH * b + j + 1)
                                nc.scalar.activation(act32[:, j % 2, :], PS[:, j % 4, :], ACT.Gelu_apprx_tanh,
                                                     bias=bfs[:, j:j + 1]).then_inc(h_ready, 1)
                                if j == 3:
                                    act.wait_ge(chosen, b + 1)
                                    nc.scalar.activation(m4[:, 3, :], m4[:, 2, :], ACT.Tanh,
                                                         scale=0.5).then_inc(gates_exp, 1)

                        act.wait_ge(w_in, W_IN)
                        act.sem_inc(h_ready, HELD)
                        evac(0)
                        with act.Fori(0, B // 2) as b:
                            gelus(b)
                            evac(b + 1)
                        act.wait_ge(raw_in, 32)
                        split_high(0)
                        with act.Fori(B // 2, B - 1) as b:
                            gelus(b)
                            evac(b + 1)
                        gelus(B - 1)

                    @block.gpsimd
                    def _(pool):
                        def rstds(b):
                            pool_wait(pool, hn_var, b + 1)
                            norm_rstd(pool, hn_rstd, 2 * b)

                        def copy_rows(b):
                            pool_wait(pool, hn_ready, b + 1)
                            if not isinstance(b, int) or b:
                                pool_wait(pool, scattered, 16 * 2 * TB * b)
                            nc.gpsimd.tensor_copy(rows[:, :, 0:D], hn[:]).then_inc(hn_copied, 1)
                            xs = X[:, bass.ds(TB * b, TB), :]
                            nc.gpsimd.tensor_tensor(xs, xs, bps[:].unsqueeze(1).to_broadcast([P, TB, D]),
                                                    ALU.add).then_inc(bias_added, 1)

                        def send_rows(b):
                            pool_wait(pool, slots_ready, b + 1)
                            nc.gpsimd.tensor_copy(rows[:, :, D:ROW], meta[:]).then_inc(rows_ready, 1)
                            nc.gpsimd.tensor_copy(slotc[:], slot[:]).then_inc(rows_ready, 1)
                            pool_wait(pool, rows_ready, 2 * b + 4)
                            pool_wait(pool, hn_copied, b + 1)
                            for t in range(TB):
                                for m in range(2):
                                    nc.gpsimd.indirect_dma_start(
                                        out=RG, out_offset=bass.IndirectOffsetOnAxis(ap=slotc[:, t, m:m + 1], axis=0),
                                        in_=rows[:, t, :], in_offset=None).then_inc(scattered, 16)

                        load_weights(pool, 0)
                        pool_wait(pool, w_in, W_IN)
                        nc.gpsimd.memset(pads[:], 0.0).then_inc(pads_zeroed, 1)
                        pool.sem_inc(rows_ready, 2)
                        rstds(0)
                        copy_rows(0)
                        with pool.Fori(0, B // 2 + 1) as b:
                            rstds(b + 1)
                            send_rows(b)
                            copy_rows(b + 1)
                        pool_wait(pool, e_high, 2)
                        low(nc.gpsimd, wfc[1][:, 0], fcraw[:], wfc[0][:, 0]).then_inc(e_low, 1)
                        low(nc.gpsimd, wpr[1][:, 0], prraw[:], wpr[0][:, 0]).then_inc(e_low, 1)
                        with pool.Fori(B // 2 + 1, B - 1) as b:
                            rstds(b + 1)
                            send_rows(b)
                            copy_rows(b + 1)
                        pool_wait(pool, e_low, 2)
                        load_weights(pool, 1)
                        send_rows(B - 1)
                        pool_wait(pool, scattered, 16 * 2 * TB * B)

                    @block.vector
                    def _(dve):
                        base = [0]
                        n = [0]
                        def link(ins):
                            n[0] += 1
                            ins.then_inc(s_chain, 1)
                            dve.wait_ge(s_chain, base[0] + n[0])

                        def tiles(b):
                            return [X[:, TB * b + t, :] for t in range(TB)]

                        def stats_part(b):
                            norm_stats(link, tiles(b)).then_inc(hn_var, 1)

                        def apply_part(b):
                            if not isinstance(b, int) or b:
                                dve.wait_ge(hT_psum, b)
                                dve.wait_ge(hn_copied, b)
                            dve.wait_ge(hn_rstd, 2 * b + 2)
                            norm_apply(tiles(b), [hn[:, t, :] for t in range(TB)]).then_inc(hn_ready, 1)

                        def first_of(score, top, choice):
                            link(nc.vector.tensor_reduce(top, score, op=ALU.max, axis=AX))
                            link(nc.vector.tensor_tensor(lg[:, 2, :, :], score,
                                                         top.unsqueeze(2).to_broadcast([P, TB, E]), ALU.is_equal))
                            link(nc.vector.tensor_tensor(lg[:, 2, :, :], lg[:, 2, :, :],
                                                         tiew.unsqueeze(1).to_broadcast([P, TB, E]), ALU.mult))
                            link(nc.vector.tensor_reduce(m4[:, 4, :], lg[:, 2, :, :], op=ALU.max, axis=AX))
                            link(nc.vector.tensor_tensor(choice, lg[:, 2, :, :],
                                                         m4[:, 4, :].unsqueeze(2).to_broadcast([P, TB, E]),
                                                         ALU.is_equal))

                        def choose(b):
                            dve.wait_ge(l_psum, b + 1)
                            nc.vector.tensor_copy(lg[:, 0, :, :].rearrange("p t e -> p (t e)"),
                                                  PS[:, 4, 0:TB * E]).then_inc(l_read, 1)
                            dve.wait_ge(l_read, b + 1)
                            first_of(lg[:, 0, :, :], m4[:, 0, :], oh[:, 0, :, :])
                            link(nc.vector.scalar_tensor_tensor(lg[:, 1, :, :], oh[:, 0, :, :], -BIG, lg[:, 0, :, :],
                                                                ALU.mult, ALU.add))
                            first_of(lg[:, 1, :, :], m4[:, 1, :], oh[:, 1, :, :])
                            link(nc.vector.tensor_tensor(m4[:, 2, :], m4[:, 0, :], m4[:, 1, :], ALU.subtract))
                            nc.vector.tensor_tensor(both[:], oh[:, 0, :, :], oh[:, 1, :, :],
                                                    ALU.add).then_inc(chosen, 1)

                        def lows(b, js):
                            for j in js:
                                dve.wait_ge(h_ready, KH * b + j + 1 + HELD)
                                low(nc.vector, hid[1][:, j, :], act32[:, j % 2, :], hid[0][:, j, :]).then_inc(l_ready, 1)

                        def x_low(b):
                            for k in range(KD):
                                dve.wait_ge(hT_high, KD * b + k + 1)
                                low(nc.vector, xTp[1][:, k, :], PS[:, 4 + k, :], xTp[0][:, k, :]).then_inc(hT_ready, 1)

                        CHOOSE = 12

                        pos = lg[:, 3, :, :]

                        def place_rows(b):
                            dve.wait_ge(r_psum, b + 1)
                            link(nc.vector.tensor_tensor(pos, PS[:, 5, 0:TB * E].rearrange("p (t e) -> p t e", e=E),
                                                         carry[:].unsqueeze(1).to_broadcast([P, TB, E]), ALU.add))
                            nc.vector.tensor_tensor(carry[:], carry[:], PS[:, 5, TB * E:(TB + 1) * E],
                                                    ALU.add).then_inc(r_read, 1)

                        def place(b):
                            dve.wait_ge(rows_ready, 2 * b + 2)
                            for m in range(2):
                                link(nc.vector.tensor_tensor(lg[:, 4 + m, :, :], pos, oh[:, m, :, :], ALU.mult))
                                link(nc.vector.tensor_reduce(m4[:, 5 + m, :], lg[:, 4 + m, :, :], op=ALU.add, axis=AX))
                                link(nc.vector.tensor_copy(slot[:, :, m], m4[:, 5 + m, :]))
                            dve.wait_ge(gates_exp, b + 1)
                            for m, sign in enumerate((0.5, -0.5)):
                                link(nc.vector.tensor_scalar(m4[:, 7, :], m4[:, 3, :], sign, 0.5, ALU.mult, ALU.add))
                                link(nc.vector.tensor_tensor(lg[:, 4 + m, :, :], oh[:, m, :, :],
                                                             m4[:, 7, :].unsqueeze(2).to_broadcast([P, TB, E]),
                                                             ALU.mult))
                            link(nc.vector.tensor_tensor(meta[:, :, 0:E], lg[:, 4, :, :], lg[:, 5, :, :], ALU.add))
                            nc.vector.tensor_copy(meta[:, :, E], tok[:]).then_inc(slots_ready, 1)
                            dve.wait_ge(slots_ready, b + 1)
                            link(nc.vector.tensor_scalar(tok[:], tok[:], float(L), None, ALU.add))

                        PLACE = 13

                        def residual(b, halves):
                            dve.wait_ge(bias_added, b + 1)
                            for i in halves:
                                dve.wait_ge(y_psum, 2 * b + i + 1)
                                xs = X[:, bass.ds(TB * b + 2 * i, 2), :].rearrange("p t d -> p (t d)")
                                nc.vector.tensor_tensor(xs, xs, PS[:, 6 + i, :], ALU.add).then_inc(x3_ready, 2)

                        dve.sem_inc(x3_ready, TB)
                        nc.vector.tensor_copy(carry[:], ebase)
                        for t in range(TB):
                            nc.vector.tensor_scalar(tok[:, t:t + 1], rowno[:, 0:1], float(t * P), None, ALU.add)
                        link(nc.vector.memset(meta[:], 0.0))
                        dve.sem_inc(l_ready, 2)
                        nc.vector.tensor_copy(triones[:, 0, :], tri[:])
                        nc.vector.tensor_copy(triones[:, 1, :], ones[:])
                        dve.wait_ge(w_in, W_IN)
                        nc.vector.tensor_copy(wrp[0][:], wr[:]).then_inc(wr_split, 1)
                        dve.wait_ge(wr_split, 1)
                        low(nc.vector, wrp[1][:], wr[:], wrp[0][:]).then_inc(wr_split, 1)
                        stats_part(0)
                        apply_part(0)
                        x_low(0)
                        choose(0)
                        with dve.Fori(0, B - 1) as b:
                            n[0] = 0
                            base[0] = (1 + CHOOSE + PLACE) * b + (2 + CHOOSE)
                            lows(b, range(0, 2))
                            stats_part(b + 1)
                            lows(b, range(2, 4))
                            apply_part(b + 1)
                            lows(b, range(4, KH))
                            place_rows(b)
                            x_low(b + 1)
                            place(b)
                            residual(b, range(1))
                            choose(b + 1)
                            residual(b, range(1, 2))
                            assert n[0] == 1 + CHOOSE + PLACE, n
                        n[0] = 0
                        base[0] = (1 + CHOOSE + PLACE) * (B - 1) + (2 + CHOOSE)
                        lows(B - 1, range(KH))
                        place_rows(B - 1)
                        place(B - 1)
                        dve.wait_ge(pads_zeroed, 1)
                        for h in range(2):
                            nc.vector.tensor_scalar(pads[:, h, TOK:TOK + 1], rowno[:, h:h + 1], float(N), None, ALU.add)
                        nc.vector.tensor_copy(ends[:], carry[:])
                        link(nc.vector.tensor_tensor(cnt[:, 0, :], carry[:], ebase, ALU.subtract))
                        for j in range(1, NBR - 1):
                            nc.vector.tensor_scalar(cmp_[:, :, j - 1], cnt[:, 0, :], float(BLK * j), None,
                                                    ALU.is_gt)
                        link(nc.vector.memset(cmp_[:, :, NBR - 2], 1.0))
                        link(nc.vector.tensor_reduce(cnt[:, 1, :], cmp_[:], op=ALU.add, axis=AX))
                        link(nc.vector.tensor_tensor_scan(cnt[:, 2, :], ones[:, 0:E], cnt[:, 1, :], 0.0,
                                                          ALU.mult, ALU.add))
                        link(nc.vector.tensor_tensor(cnt[:, 2, :], cnt[:, 2, :], cnt[:, 1, :], ALU.subtract))
                        link(nc.vector.tensor_copy(tbl[:, 0:E], cnt[:, 1, :]))
                        nc.vector.tensor_copy(tbl[:, E:2 * E], cnt[:, 2, :]).then_inc(carry_ready, 1)
                        residual(B - 1, range(2))
                        dve.wait_ge(x3_ready, TB * B + TB)

            if stop == 3:
                dump(nc, ctx, X, out, B, TB, P)
                return

            tm = Place(experts_at)
            xr = tm("xr", [P, 2, ROW])
            xTp = [tm("xTe" + n, [P, KD, BLK], F32R) for n in "hl"]
            act32 = tm("act32e", [P, 2, BLK])
            bpr = tm("bpr", [P, E, D])
            be = tm("be", [P, 2, KH])
            hid = [tm("hide" + n, [P, KH, BLK], F32R) for n in "hl"]
            meta = tm("metae", [P, 2, ROW - D])
            gate = tm("gate", [P, 2])
            toki = tm("toki", [P, 2], I32)
            y = tm("y", [P, 2, D])
            (x_in, x_psum, xT_ready, xr_free, h_psum, h_ready, y_psum, y_read, y_ready, gate_ready,
             added, y_sent, b_in, xT_high, l_ready, be_ready) = phase_sems(c, """d_x_in d_x_psum d_xT_ready d_xr_free d_h_psum
                d_h_ready d_y_psum d_y_read d_y_ready d_gate_ready d_added d_y_sent d_b_in
                d_xT_high d_l_ready d_be_ready""")
            rg = RG.rearrange("(n h p) c -> n p h c", h=2, p=P)

            def blocks_of(eng, e):
                return (eng.value_load(tbl[0:1, bass.ds(e, 1)], min_val=1, max_val=NBR - 1),
                        eng.value_load(tbl[0:1, bass.ds(E + e, 1)], min_val=0, max_val=2 * N // BLK + E))

            def every_block(eng, body, head=None):
                with eng.Fori(0, E // 2) as pair:
                    for par in range(2):
                        e = pair * 2 + par
                        if head:
                            head(pair, e, par)
                        count, before = blocks_of(eng, e)
                        with eng.Fori(0, count) as i:
                            body(before + i, e, par, i)

            with nc.Block() as block:
                @block.sync
                def _(sp):
                    def load(g, e, par, i):
                        sp.wait_ge(xr_free, g + 1)
                        sp.dma_start(xr[:].rearrange("p (a h) c -> p a h c", a=1),
                                     rg[bass.ds(e * NBR + i, 1)].rearrange("a p h c -> p a h c")).then_inc(x_in, 16)
                    for e in range(E):
                        sp.dma_start(bpr[:, e, :], d["bproj"][e:e + 1, :].to_broadcast([P, D])).then_inc(b_in, 16)
                    every_block(sp, load)
                    _, before = blocks_of(sp, E - 1)
                    count, _ = blocks_of(sp, E - 1)
                    load(before + count, E - 1, 1, 0)
                    sp.wait_ge(x_in, (before + count) * 16 + 16)
                    sp.sem_inc(sp_waits, 1)

                @block.tensor
                def _(pe):
                    def transposes(g):
                        pe.wait_ge(x_in, g * 16 + 16)
                        if not isinstance(g, int):
                            pe.wait_ge(xT_ready, g)
                        for k in range(KD):
                            for h in range(2):
                                last = nc.tensor.transpose(PS[:, 4, k * BLK + h * P:k * BLK + (h + 1) * P],
                                                           xr[:, h, k * P:(k + 1) * P], ident[:])
                        last.then_inc(x_psum, 1)

                    def one(g, e, par, i):
                        pe.wait_ge(xT_ready, g + 1)
                        for j in range(KH):
                            pe.wait_ge(h_ready, g * KH + j + 1)
                            for k in range(KD):
                                last = product(PS[:, j % 4, 0:BLK], [w[:, par, k, j * P:(j + 1) * P] for w in wfc],
                                               [x[:, k, :] for x in xTp], k == 0, k == KD - 1)
                            last.then_inc(h_psum, 1)
                        transposes(g + 1)
                        for h in range(2):
                            pe.wait_ge(y_read, g * 2 + h + 1)
                            for j in range(KH):
                                if h == 0:
                                    pe.wait_ge(l_ready, g * KH + j + 1 + 2)
                                last = product(PS[:, 5 + h, 0:D], [x[:, j, h * P:(h + 1) * P] for x in hid],
                                               [w[:, par, j, :] for w in wpr], j == 0, j == KH - 1)
                            last.then_inc(y_psum, 1)

                    transposes(0)
                    every_block(pe, one, lambda pair, e, par: pe.wait_ge(e_low, e * 2 + 2))

                @block.scalar
                def _(act):
                    act.sem_inc(h_ready, HELD)

                    def x_high(g):
                        act.wait_ge(x_psum, g + 1)
                        nc.scalar.activation(xTp[0][:].rearrange("p k n -> p (k n)"), PS[:, 4, :],
                                             ACT.Copy).then_inc(xT_high, 1)

                    def gelus(g, e, par, i):
                        for j in range(KH):
                            bias = be[:, par, j:j + 1]
                            act.wait_ge(h_psum, g * KH + j + 1)
                            nc.scalar.activation(hid[0][:, j, :], PS[:, j % 4, 0:BLK], ACT.Gelu_apprx_tanh, bias=bias)
                            act.wait_ge(l_ready, g * KH + j + 1)
                            nc.scalar.activation(act32[:, j % 2, :], PS[:, j % 4, 0:BLK], ACT.Gelu_apprx_tanh,
                                                 bias=bias).then_inc(h_ready, 1)
                        x_high(g + 1)
                        with act.If(i * E + e < E - 1):
                            act.wait_ge(raw_in, e * 32 + 64)
                            split_high(1 - par)

                    def head(pair, e, par):
                        nc.scalar.activation(be[:, par, :], bfc[:, bass.ds(e, 1), :].rearrange("p a j -> p (a j)"),
                                             ACT.Copy).then_inc(be_ready, 1)
                        act.wait_ge(be_ready, e + 1)

                    x_high(0)
                    every_block(act, gelus, head)

                @block.gpsimd
                def _(pool):
                    pool.sem_inc(y_sent, 1)

                    def send(g, e, par, i):
                        pool_wait(pool, y_ready, g * 2 + 2)
                        for h in range(2):
                            nc.gpsimd.indirect_dma_start(
                                out=out, out_offset=bass.IndirectOffsetOnAxis(ap=toki[:, h:h + 1], axis=0),
                                in_=y[:, h, :], in_offset=None, compute_op=ALU.add).then_inc(added, 16)
                        pool_wait(pool, added, g * 32 + 32)
                        pool.sem_inc(y_sent, 1)
                        with pool.If(i * E + e < E - 2):
                            pool_wait(pool, e_low, e * 2 + 4)
                            load_weights(pool, nc.s_assert_within(e + 2, 2, E - 1, skip_runtime_bounds_check_because="the If"))

                    every_block(pool, send)

                @block.vector
                def _(dve):
                    dve.sem_inc(y_read, 2)

                    def take(g):
                        dve.wait_ge(x_psum, g + 1)
                        dve.wait_ge(xT_high, g + 1)
                        low(nc.vector, xTp[1][:].rearrange("p k n -> p (k n)"), PS[:, 4, :],
                            xTp[0][:].rearrange("p k n -> p (k n)")).then_inc(xT_ready, 1)
                        nc.vector.tensor_copy(meta[:], xr[:, :, D:ROW]).then_inc(xr_free, 1)

                    def one(g, e, par, i):
                        for j in range(KH):
                            dve.wait_ge(h_ready, g * KH + j + 1 + HELD)
                            low(nc.vector, hid[1][:, j, :], act32[:, j % 2, :], hid[0][:, j, :]).then_inc(l_ready, 1)
                        dve.wait_ge(xr_free, g + 2)
                        dve.wait_ge(y_sent, g + 1)
                        nc.vector.tensor_copy(gate[:], meta[:, :, bass.ds(e, 1)].rearrange("p h a -> p (h a)"))
                        nc.vector.tensor_copy(toki[:], meta[:, :, E]).then_inc(gate_ready, 1)
                        dve.wait_ge(gate_ready, g + 1)
                        take(g + 1)
                        for h in range(2):
                            dve.wait_ge(y_psum, g * 2 + h + 1)
                            nc.vector.tensor_tensor(y[:, h, :], PS[:, 5 + h, 0:D],
                                                    bpr[:, bass.ds(e, 1), :].rearrange("p a d -> p (a d)"),
                                                    ALU.add).then_inc(y_read, 1)
                        for h in range(2):
                            dve.wait_ge(y_read, g * 2 + 3 + h)
                            nc.vector.tensor_scalar(y[:, h, :], y[:, h, :], gate[:, h:h + 1], None,
                                                    ALU.mult).then_inc(y_ready, 1)
                        with dve.If(i * E + e < E - 1):
                            dve.wait_ge(e_high, e * 2 + 4)
                            low(nc.vector, wfc[1][:, 1 - par], fcraw[:], wfc[0][:, 1 - par]).then_inc(e_low, 1)
                            low(nc.vector, wpr[1][:, 1 - par], prraw[:], wpr[0][:, 1 - par]).then_inc(e_low, 1)

                    dve.sem_inc(xr_free, 1)
                    dve.wait_ge(b_in, 16 * E)
                    dve.sem_inc(l_ready, 2)
                    take(0)
                    every_block(dve, one)


def dump(nc, ctx, X, out, B, TB, P):
    s = ctx.enter_context(nc.semaphore("dumped"))
    with nc.Block() as block:
        @block.sync
        def _(sp):
            for b in range(B):
                sp.dma_start(out[b * TB * P:(b + 1) * TB * P, :].rearrange("(t p) d -> p t d", p=P),
                             X[:, b * TB:(b + 1) * TB, :]).then_inc(s, 16)
            sp.wait_ge(s, 16 * B)


def kernel(x, ctx_1024, L0_attn_W_in, L0_attn_conv_w, L0_attn_conv_b, L0_attn_W_x, L0_attn_W_dt, L0_attn_b_dt,
           L0_attn_A_log, L0_attn_D_skip, L0_attn_W_out, L0_xattn_Wq, L0_xattn_bq, L0_xattn_Wk, L0_xattn_bk,
           L0_xattn_Wv, L0_xattn_bv, L0_xattn_Wo, L0_xattn_bo, L0_ffn_Wfc_s, L0_ffn_bfc_s, L0_ffn_Wproj_s,
           L0_ffn_bproj_s, L0_ffn_Wr, L0_ffn_Wfc, L0_ffn_bfc, L0_ffn_Wproj, L0_ffn_bproj):
    import numpy as np
    import concourse.bacc as bacc
    from concourse import mybir
    from concourse.bass_utils import run_bass_kernel_spmd

    nd = np.asarray
    P = 128
    Bb, L, D = nd(x).shape
    S = nd(ctx_1024).shape[1]
    E, _, HID = nd(L0_ffn_Wfc).shape
    ROOM = Bb * L + 2 * P
    EI = nd(L0_attn_W_out).shape[1]
    HH = 8

    small = np.zeros((P, 64), np.float32)
    small[:, 0:HH] = np.arange(P)[:, None] // 16 == np.arange(HH)[None, :]
    small[:, 8:8 + E] = E - np.arange(E)
    small[:, 16] = np.arange(P)
    small[:, 17] = np.arange(P) + P
    small[:, 24:24 + E] = np.arange(E) * ROOM
    small[:, 32:40] = 1e-5
    small[:, 40:48] = -0.5
    causal = np.where(np.arange(S)[None, :] > np.arange(P)[:, None], np.float32(-1e30), np.float32(0))
    arrays = {
        "x": nd(x),
        "ctxT": np.ascontiguousarray(nd(ctx_1024).reshape(Bb * S, D).T).reshape(D // P, P, Bb * S),
        "W_inT": nd(L0_attn_W_in)[EI:].T, "W_xT": nd(L0_attn_W_x).T, "W_dtT": nd(L0_attn_W_dt).T,
        "b_dt": nd(L0_attn_b_dt).reshape(-1, P).T, "D_skip": nd(L0_attn_D_skip).reshape(-1, P).T,
        "A_log": nd(L0_attn_A_log), "W_outT": nd(L0_attn_W_out).T,
        "Wq": nd(L0_xattn_Wq), "Wk": nd(L0_xattn_Wk), "Wv": nd(L0_xattn_Wv), "Wo": nd(L0_xattn_Wo),
        "bq": nd(L0_xattn_bq).reshape(-1, P).T, "bk": nd(L0_xattn_bk).reshape(-1, P).T,
        "bv": nd(L0_xattn_bv).reshape(1, -1), "bo": nd(L0_xattn_bo).reshape(1, -1),
        "Wfc_s": nd(L0_ffn_Wfc_s), "bfc_s": nd(L0_ffn_bfc_s).reshape(-1, P).T,
        "Wproj_s": nd(L0_ffn_Wproj_s), "bproj_s": nd(L0_ffn_bproj_s).reshape(1, -1),
        "Wr": nd(L0_ffn_Wr), "Wfc": nd(L0_ffn_Wfc), "bfc": nd(L0_ffn_bfc).reshape(E, -1, P).transpose(2, 0, 1),
        "Wproj": nd(L0_ffn_Wproj), "bproj": nd(L0_ffn_bproj),
        "ident": np.eye(P, dtype=np.float32),
        "tri": np.triu(np.ones((P, P), np.float32), 1),
        "small": small, "causal": np.tile(causal, (1, HH)),
        "steps": np.tile(np.arange(1, L, dtype=np.float32), (P, 1)),
    }
    nc = bacc.Bacc("TRN2", target_bir_lowering=False, num_devices=1)
    feeds, aps = {}, {}
    for name, a in arrays.items():
        a = np.ascontiguousarray(a)
        feeds["in_" + name] = a
        aps[name] = nc.dram_tensor("in_" + name, a.shape, mybir.dt.from_np(a.dtype), kind="ExternalInput").ap()
    aps["out"] = nc.dram_tensor("out_rows", (ROOM, D), mybir.dt.float32, kind="ExternalOutput").ap()
    build(nc, aps, STOP)
    r = run_bass_kernel_spmd(nc, [feeds], core_ids=[0])
    return r.results[0]["out_rows"][:Bb * L].reshape(Bb, L, D)


STOP = 9
```

```python
def build(nc, d):
    import concourse.bass as bass
    from concourse import mybir
    from contextlib import ExitStack

    BF16 = mybir.dt.bfloat16
    F32, F32R, I32 = mybir.dt.float32, mybir.dt.float32r, mybir.dt.int32
    ALU = mybir.AluOpType
    ACT = mybir.ActivationFunctionType
    AX = mybir.AxisListType.X

    P = 128
    B, L, D = d["x"].shape
    N = B * L
    TILES, TB = N // P, L // P
    KD = D // P
    S = d["ctxT"].shape[2] // B
    EI, NS = d["A_log"].shape
    KE = EI // P
    R = d["W_dtT"].shape[0]
    H = 16
    DK = D // H
    HH = H // KD
    NP = H // 2
    PW = 2 * DK + 2
    E = d["Wfc"].shape[0]
    HID = d["Wfc"].shape[2]
    KH = HID // P
    BLK = 2 * P
    ROOM = N + BLK
    NBR = ROOM // BLK
    ROW = 272
    GATE, TOK = D, D + E
    SCALE = DK ** -0.5
    BIG = 1e30

    out = d["out"]

    ctx = ExitStack()
    with ctx:
        class Place:
            def __init__(self, at):
                self.at = at

            def __call__(self, name, shape, dt=F32):
                held = 4
                for n in shape[1:]:
                    held *= n
                t = nc.alloc_sbuf_tensor_at(name, list(shape), dt, offset=self.at)
                self.at += -(-held // 64) * 64
                return t

        sb = Place(-(-nc.sbuf_base // 64) * 64)

        X = sb("X", [P, TILES, D])
        ident = sb("ident", [P, P])
        tri = sb("tri", [P, P])
        ones = sb("ones", [P, P])
        small = sb("small", [P, 64])
        headmask = small[:, 0:HH]
        tiew = small[:, 8:8 + E]
        rowno = small[:, 16:18]
        ebase = small[:, 24:24 + E]
        eps4, half4 = small[:, 32:32 + TB], small[:, 40:40 + TB]
        stats = sb("stats", [P, TB, 6])
        mv = sb("mv", [P, TB, 2])
        vare = sb("vare", [P, TB])
        rstd = sb("rstd", [P, TB])
        hn = sb("hn", [P, TB, D])
        PS = ctx.enter_context(nc.psum_tensor("PS", [P, 8, 512], F32))

        RG = nc.dram_tensor("routed_rows", [E * ROOM, ROW], F32, kind="Internal").ap()

        def phase_sems(c, names):
            return [c.enter_context(nc.semaphore(n)) for n in names.split()]

        pool_waits = ctx.enter_context(nc.semaphore("pool_waits"))
        sp_waits = ctx.enter_context(nc.semaphore("sp_waits"))
        pe_waits = ctx.enter_context(nc.semaphore("pe_waits"))
        bn_waits = ctx.enter_context(nc.semaphore("bn_waits"))

        def pool_wait(pool, sem, value):
            pool.wait_ge(sem, value)
            pool.sem_inc(pool_waits, 1)

        def norm_stats(link, tiles):
            for t, src in enumerate(tiles):
                last = nc.vector.bn_stats(stats[:, t, :], src)
            link(last)
            nc.vector.sem_inc(bn_waits, 1)
            for t in range(len(tiles)):
                last = nc.vector.bn_aggr(mv[:, t, :], stats[:, t, :])
            return last

        def norm_rstd(pool, done, before):
            nc.gpsimd.tensor_tensor(vare[:], mv[:, :, 1], eps4, ALU.add).then_inc(done, 1)
            pool_wait(pool, done, before + 1)
            nc.gpsimd.tensor_tensor(rstd[:], vare[:], half4, ALU.pow).then_inc(done, 1)

        def norm_apply(b, eng=nc.vector, part=range(TB)):
            for t in part:
                last = eng.tensor_scalar(hn[:, t, :], X[:, TB * b + t, :], mv[:, t, 0:1], rstd[:, t:t + 1],
                                         ALU.subtract, ALU.mult)
            return last

        def product(out, w, x, first=True, last=True):
            (wh, wl), (xh, xl) = w, x
            nc.tensor.matmul(out, wh, xh, start=first, stop=False)
            nc.tensor.matmul(out, wh, xl, start=False, stop=False)
            return nc.tensor.matmul(out, wl, xh, start=False, stop=last)

        def low(eng, out, whole, high):
            return eng.tensor_tensor(out, whole, high.bitcast(F32), ALU.subtract)

        SLOT = KE * NS // B
        PWB = 4

        prior = sb.at
        fcraw = sb("fcraw", [P, KD, HID])
        prraw = sb("prraw", [P, KH, D])
        wfs = [sb("wfs" + n, [P, KD, HID], F32R) for n in "hl"]
        wps = [sb("wps" + n, [P, KH, D], F32R) for n in "hl"]
        sz = Place(prior)("sz", [P, B, KE * L])
        ab = Place(max(sb.at, prior + 4 * B * KE * L))
        causal = ab("causal", [P, HH * S])
        causal16 = ab("causal16", [P, HH * S], BF16)
        ident16 = ab("ident16", [P, P], BF16)
        yD = ab("yD", [P, KE * L])
        hT_at = ab.at
        hT = ab("hT", [P, 2, KD, L])
        wq, wk, wv, wo = (ab(n, [P, KD, D]) for n in ("wq", "wk", "wv", "wo"))
        bq, bk = ab("bq", [P, KD]), ab("bk", [P, KD])
        bv = ab("bv", [1, D])
        bo = ab("bo", [P, D])
        ctx2 = ab("ctx2", [P, KD, B, 2, S])
        kT = ab("kT", [P, KD, B, S])
        vbd = ab("vbd", [P, B, NP * PW])

        with ExitStack() as c:
            tmp = Place(ab.at)
            win_at = tmp.at
            win = tmp("win", [P, KD, EI])
            wout_at = tmp.at
            wout = tmp("wout", [P, KE, D])
            kbd_at = tmp.at
            wx = tmp("wx", [P, KE, R + 2 * NS])
            wdt = tmp("wdt", [R, EI])
            bdt = tmp("bdt", [P, KE])
            dsk = tmp("dsk", [P, KE])
            alog = tmp("alog", [P, KE, NS])
            steps = tmp("steps", [P, L - 1])
            onesrow = tmp("onesrow", [P, L])
            dlt = tmp("dlt", [R, 1])
            bc = tmp("bc", [P, 2 * NS])
            dl = tmp("dl", [P, 8, KE])
            rate = tmp("rate", [P, KE, NS])
            coef = tmp("coef", [P, KE, NS])
            pw = tmp("pw", [P, PWB, L - 1])
            kern = tmp("kern", [P, KE, L])
            kbd = Place(kbd_at)("kbd", [P, B, KD, HH * S])
            gh = [Place(hT_at)("gh0", [P, KE * L], F32R), Place(kbd_at + 4 * B * KD * HH * S)("gh1", [P, KE * L], F32R)]
            gl = Place(prior)("gl", [P, B, KE * L], F32R)
            wouts = (Place(win_at)("wouth", [P, KE, D], F32R), Place(wout_at)("woutl", [P, KE, D], F32R))
            x_in = phase_sems(c, " ".join("x_in_%d" % b for b in range(B)))
            hn_ready = phase_sems(c, "hn_ready_by_dve hn_ready_by_pool")
            z_copied = phase_sems(c, "z_copied_by_act z_copied_by_dve")
            (consts_in, w_in, win_in, kv_in, late_in, small_mm, dve_done, act_done, pw_ready, pw_used, s_chain,
             hn_var, hn_rstd, hT_psum, hT_ready, z_psum, sz_ready, w_split, g_high, g_low, yD_ready, g_ready, o_psum,
             x1_ready, k_psum, kT_ready, v_psum, v_ready, vz, k_ready) = phase_sems(c, """consts_in w_in win_in kv_in
                late_in small_mm dve_done act_done pw_ready pw_used s_chain hn_var hn_rstd hT_psum hT_ready
                z_psum sz_ready w_split g_high g_low yD_ready g_ready o_psum x1_ready k_psum kT_ready v_psum
                v_ready vz k_ready""")
            W_IN, KV_IN, LATE_IN = 16 * 6, 16 * 8, 16 * 7
            with nc.Block() as block:
                @block.sync
                def _(sp):
                    def x_load(b):
                        sp.dma_start(X[:, b * TB:(b + 1) * TB, :],
                                     d["x"][b].rearrange("(t p) d -> p t d", p=P)).then_inc(x_in[b], 16)

                    for dst, src in ((wx[:], d["W_xT"].rearrange("(k p) r -> p k r", p=P)),
                                     (wdt[:], d["W_dtT"]), (bdt[:], d["b_dt"]), (dsk[:], d["D_skip"]),
                                     (alog[:], d["A_log"].rearrange("(k p) n -> p k n", p=P)),
                                     (steps[:], d["steps"])):
                        sp.dma_start(dst, src).then_inc(w_in, 16)
                    x_load(0)
                    for dst, src in ((ident[:], d["ident"]), (small[:], d["small"])):
                        sp.dma_start(dst, src).then_inc(consts_in, 16)
                    sp.dma_start(win[:], d["W_inT"].rearrange("(k p) e -> p k e", p=P)).then_inc(win_in, 16)
                    for b in range(1, 3):
                        x_load(b)
                    for w, n in ((wk, "Wk"), (wv, "Wv")):
                        sp.dma_start(w[:], d[n].rearrange("(k p) e -> p k e", p=P)).then_inc(kv_in, 16)
                    for k in range(KD):
                        for j in range(2):
                            sp.dma_start(ctx2[:, k, :, j, :],
                                         d["ctxT"][k].rearrange("p (b s) -> p b s", s=S)).then_inc(kv_in, 16)
                    sp.dma_start(bk[:], d["bk"]).then_inc(kv_in, 16)
                    sp.dma_start(bv[:], d["bv"]).then_inc(kv_in, 16)
                    for b in range(3, B):
                        x_load(b)
                    sp.dma_start(wout[:], d["W_outT"].rearrange("(k p) e -> p k e", p=P)).then_inc(late_in, 16)
                    for w, n in ((wq, "Wq"), (wo, "Wo")):
                        sp.dma_start(w[:], d[n].rearrange("(k p) e -> p k e", p=P)).then_inc(late_in, 16)
                    for dst, src in ((tri[:], d["tri"]), (causal[:], d["causal"]), (bq[:], d["bq"]),
                                     (bo[:], d["bo"].to_broadcast([P, D]))):
                        sp.dma_start(dst, src).then_inc(late_in, 16)
                    sp.wait_ge(late_in, LATE_IN)

                @block.tensor
                def _(pe):
                    pe.wait_ge(w_in, W_IN)
                    pe.wait_ge(dve_done, 1)
                    for k in range(KE):
                        nc.tensor.matmul(PS[0:R, 0, 0:1], wx[:, k, 0:R], ones[:, 0:1],
                                         start=k == 0, stop=k == KE - 1)
                    for k in range(KE):
                        last = nc.tensor.matmul(PS[:, 1, 0:2 * NS], ones[:, :], wx[:, k, R:R + 2 * NS],
                                                start=k == 0, stop=k == KE - 1)
                    last.then_inc(small_mm, 1)
                    pe.wait_ge(dve_done, 2)
                    for k in range(KE):
                        last = nc.tensor.matmul(PS[:, 2, k:k + 1], wdt[:, k * P:(k + 1) * P], dlt[:],
                                                start=True, stop=True)
                    last.then_inc(small_mm, 1)

                    def transposes(b):
                        for half in hn_ready:
                            pe.wait_ge(half, b + 1)
                        if b:
                            pe.wait_ge(hT_ready, KD * b)
                        for t in range(TB):
                            for k in range(KD):
                                last = nc.tensor.transpose(PS[:, 4 + k, t * P:(t + 1) * P],
                                                           hn[:, t, k * P:(k + 1) * P], ident[:])
                        last.then_inc(hT_psum, 1)

                    def z_part(b):
                        pe.wait_ge(hT_ready, KD * b + KD)
                        for e in range(KE):
                            if b:
                                if e < KE - 1:
                                    pe.wait_ge(z_copied[0], (KE - 1) * (b - 1) + e + 1)
                                else:
                                    pe.wait_ge(z_copied[1], b)
                            for k in range(KD):
                                last = nc.tensor.matmul(PS[:, e, :], win[:, k, e * P:(e + 1) * P],
                                                        hT[:, b % 2, k, :], start=k == 0, stop=k == KD - 1)
                            last.then_inc(z_psum, 1)

                    pe.wait_ge(consts_in, 32)
                    transposes(0)
                    pe.wait_ge(win_in, 16)
                    pe.wait_ge(dve_done, 3)
                    transposes(1)
                    for b in range(B):
                        z_part(b)
                        if b < B - 2:
                            transposes(b + 2)
                        if b == 1:
                            pe.wait_ge(kv_in, KV_IN)
                            for m in range(KD):
                                for k in range(KD):
                                    last = nc.tensor.matmul(PS[:, 6 + m, :], wk[:, k, m * P:(m + 1) * P],
                                                            ctx2[:, k, :, 0, :], start=k == 0, stop=k == KD - 1)
                                last.then_inc(k_psum, 1)
                    for b in range(B):
                        if b < 6:
                            pe.wait_ge(z_copied[0], (KE - 1) * (B - 1) + b // 2 + 1)
                        else:
                            pe.wait_ge(z_copied[1], B)
                        vs = PS[:, b // 2, (b % 2) * D:(b % 2 + 1) * D]
                        for k in range(KD):
                            nc.tensor.matmul(vs, ctx2[:, k, b, :, :], wv[:, k, :], start=k == 0, stop=False)
                        nc.tensor.matmul(vs, ones[0:1, :], bv[:], start=False, stop=True).then_inc(v_psum, 1)
                    pe.wait_ge(w_split, 2)
                    pe.wait_ge(kT_ready, KD)

                    def out_part(b):
                        pe.wait_ge(g_low, b + 1)
                        for t in range(TB):
                            if t % 2 == 0:
                                pe.wait_ge(x1_ready, 2 * b + t // 2 + 1)
                            for e in range(KE):
                                at = e * L + t * P
                                last = product(PS[:, 6 + t // 2, (t % 2) * D:(t % 2 + 1) * D],
                                               (gh[b % 2][:, at:at + P], gl[:, b, at:at + P]),
                                               [w[:, e, :] for w in wouts], e == 0, e == KE - 1)
                            if t % 2:
                                last.then_inc(o_psum, 1)
                    for b in range(B):
                        out_part(b)

                @block.vector
                def _(dve):
                    n = [0]
                    def link(ins):
                        n[0] += 1
                        ins.then_inc(s_chain, 1)
                        dve.wait_ge(s_chain, n[0])

                    def tiles(b):
                        return [X[:, TB * b + t, :] for t in range(TB)]

                    def stats_part(b):
                        dve.wait_ge(x_in[b], 16)
                        if b:
                            for half in hn_ready:
                                dve.wait_ge(half, b)
                        norm_stats(link, tiles(b)).then_inc(hn_var, 1)

                    def apply_part(b):
                        if b:
                            dve.wait_ge(hT_psum, b)
                        dve.wait_ge(hn_rstd, 2 * b + 2)
                        norm_apply(b, nc.vector, range(TB // 2)).then_inc(hn_ready[0], 1)

                    dve.sem_inc(x1_ready, 2)
                    nc.vector.memset(onesrow[:], 1.0)
                    link(nc.vector.memset(kern[:], 0.0))
                    nc.vector.memset(ones[:], 1.0).then_inc(dve_done, 1)
                    dve.wait_ge(small_mm, 1)
                    nc.vector.tensor_copy(dlt[:], PS[0:R, 0, 0:1]).then_inc(dve_done, 1)
                    link(nc.vector.tensor_copy(bc[:], PS[:, 1, 0:2 * NS]))
                    dve.wait_ge(small_mm, 2)
                    t_, na, ex, u, ln, dlt_ = (dl[:, i, :] for i in range(6))
                    link(nc.vector.tensor_tensor(t_, PS[:, 2, 0:KE], bdt[:], ALU.add))
                    link(nc.vector.tensor_scalar(na, t_, -1.0, None, ALU.mult))
                    link(nc.vector.tensor_tensor(na, na, t_, ALU.min))
                    nc.vector.tensor_scalar(dl[:, 6, :], t_, 0.0, None, ALU.max).then_inc(dve_done, 1)
                    stats_part(0)
                    dve.wait_ge(act_done, 1)
                    nc.vector.tensor_scalar(u, ex, 1.0, None, ALU.add).then_inc(dve_done, 1)
                    dve.wait_ge(act_done, 2)
                    nc.vector.tensor_scalar(alog[:], alog[:], 88.7, None, ALU.min).then_inc(dve_done, 1)
                    link(nc.vector.tensor_tensor(ln, ln, ex, ALU.mult))
                    link(nc.vector.tensor_scalar(dl[:, 7, :], u, -1.0, 1e-30, ALU.add, ALU.max))
                    link(nc.vector.reciprocal(dl[:, 7, :], dl[:, 7, :]))
                    link(nc.vector.tensor_tensor(ln, ln, dl[:, 7, :], ALU.mult))
                    link(nc.vector.tensor_scalar(na, u, 1.0, None, ALU.is_equal))
                    link(nc.vector.tensor_tensor(na, na, ex, ALU.mult))
                    link(nc.vector.tensor_tensor(ln, ln, na, ALU.add))
                    link(nc.vector.tensor_tensor(dlt_, ln, dl[:, 6, :], ALU.add))
                    dve.wait_ge(act_done, 3)
                    link(nc.vector.tensor_scalar(rate[:], rate[:], -2.0 ** -40, None, ALU.mult))
                    for k in range(KE):
                        last = nc.vector.tensor_scalar(rate[:, k, :], rate[:, k, :], dlt_[:, k:k + 1],
                                                       None, ALU.mult)
                    link(last)
                    nc.vector.tensor_scalar(rate[:], rate[:], -1e4 * 2.0 ** -40, 2.0 ** 40, ALU.max,
                                            ALU.mult).then_inc(dve_done, 1)
                    link(nc.vector.tensor_tensor(bc[:, 0:NS], bc[:, 0:NS], bc[:, NS:2 * NS], ALU.mult))
                    for k in range(KE):
                        last = nc.vector.tensor_scalar(coef[:, k, :], bc[:, 0:NS], dlt_[:, k:k + 1],
                                                       None, ALU.mult)
                    link(last)
                    link(nc.vector.reduce_sum(kern[:, :, 0], coef[:], axis=AX))
                    apply_part(0)
                    stats_part(1)
                    apply_part(1)
                    for i in range(KE * NS):
                        b, k, m = i // SLOT, i % KE, i // KE
                        if i == 0:
                            stats_part(2)
                        if i == 4 * SLOT:
                            dve.wait_ge(kv_in, KV_IN)
                            for m in range(KD):
                                dve.wait_ge(k_psum, m + 1)
                                nc.vector.tensor_scalar(kT[:, m, :, :].rearrange("p b s -> p (b s)"), PS[:, 6 + m, :],
                                                        bk[:, m:m + 1], None, ALU.add).then_inc(kT_ready, 1)
                        if i % SLOT == 5 and b < B - 3:
                            stats_part(b + 3)
                        if i % SLOT == 2 and b < B - 2:
                            apply_part(b + 2)
                        if i % SLOT == SLOT - 1:
                            dve.wait_ge(z_psum, KE * b + KE)
                            nc.vector.tensor_copy(sz[:, b, (KE - 1) * L:], PS[:, KE - 1, :]).then_inc(z_copied[1], 1)
                        dve.wait_ge(pw_ready, i + 1)
                        if i >= KE:
                            dve.wait_ge(pw_used, i - KE + 1)
                        nc.vector.scalar_tensor_tensor(
                            kern[:, k, 1:L], pw[:, i % PWB, :], coef[:, k, m:m + 1], kern[:, k, 1:L],
                            ALU.mult, ALU.add).then_inc(pw_used, 1)
                    for k in range(KE):
                        dve.wait_ge(pw_used, KE * (NS - 1) + k + 1)
                        nc.vector.tensor_tensor_scan(yD[:, k * L:(k + 1) * L], onesrow[:], kern[:, k, :],
                                                     dsk[:, k:k + 1], ALU.mult, ALU.add).then_inc(yD_ready, 1)

                    def residual(b):
                        for i in range(2):
                            dve.wait_ge(o_psum, 2 * b + i + 1)
                            xs = X[:, TB * b + 2 * i:TB * b + 2 * i + 2, :].rearrange("p t d -> p (t d)")
                            nc.vector.tensor_tensor(xs, xs, PS[:, 6 + i, :], ALU.add).then_inc(x1_ready, 1)

                    def gate(b):
                        dve.wait_ge(sz_ready, b + 1)
                        nc.vector.tensor_tensor(sz[:, b, :], sz[:, b, :], yD[:], ALU.mult).then_inc(g_ready, 1)

                    dve.wait_ge(late_in, LATE_IN)
                    nc.vector.tensor_copy(causal16[:], causal[:])
                    nc.vector.tensor_copy(ident16[:], ident[:])
                    dve.wait_ge(w_split, 1)
                    low(nc.vector, wouts[1][:], wout[:], wouts[0][:]).then_inc(w_split, 1)
                    dve.wait_ge(yD_ready, KE)
                    gate(0)
                    for b in range(B):
                        if b < B - 1:
                            gate(b + 1)
                        dve.wait_ge(g_high, b + 1)
                        low(nc.vector, gl[:, b, :], sz[:, b, :], gh[b % 2][:]).then_inc(g_low, 1)
                        if b:
                            residual(b - 1)
                        if b == B - 2:
                            dve.wait_ge(x1_ready, 2 + 2)
                            norm_stats(link, tiles(0)).then_inc(hn_var, 1)
                        if b == B - 1:
                            dve.wait_ge(hn_rstd, 2 * B + 2)
                            norm_apply(0)
                    residual(B - 1)
                    dve.wait_ge(x1_ready, 2 * B + 2)

                @block.scalar
                def _(act):
                    act.wait_ge(dve_done, 3)
                    nc.scalar.activation(dl[:, 2, :], dl[:, 1, :], ACT.Exp).then_inc(act_done, 1)
                    act.wait_ge(dve_done, 4)
                    nc.scalar.activation(dl[:, 4, :], dl[:, 3, :], ACT.Ln).then_inc(act_done, 1)
                    act.wait_ge(dve_done, 5)
                    nc.scalar.activation(rate[:], alog[:], ACT.Exp).then_inc(act_done, 1)

                    def evac(b):
                        act.wait_ge(hT_psum, b + 1)
                        if b >= 2:
                            act.wait_ge(z_psum, KE * (b - 1))
                        for k in range(KD):
                            nc.scalar.activation(hT[:, b % 2, k, :], PS[:, 4 + k, :], ACT.Copy).then_inc(hT_ready, 1)

                    COPY_AT = (3, 5, 6)
                    def z_copy(b, e):
                        act.wait_ge(z_psum, KE * b + e + 1)
                        nc.scalar.activation(sz[:, b, e * L:(e + 1) * L], PS[:, e, :],
                                             ACT.Copy).then_inc(z_copied[0], 1)

                    act.wait_ge(dve_done, 6)
                    for i in range(KE * NS):
                        b, k, m = i // SLOT, i % KE, i // KE
                        if i == 2:
                            evac(0)
                        if i == 6:
                            evac(1)
                        if i % SLOT == SLOT - 1 and b < B - 2:
                            evac(b + 2)
                        if i % SLOT in COPY_AT:
                            z_copy(b, COPY_AT.index(i % SLOT))
                        if i >= PWB:
                            act.wait_ge(pw_used, i - PWB + 1)
                        nc.scalar.activation(pw[:, i % PWB, :], steps[:], ACT.Exp,
                                             scale=rate[:, k, m:m + 1]).then_inc(pw_ready, 1)

                    def silu(b):
                        act.wait_ge(z_copied[0], (KE - 1) * (b + 1))
                        act.wait_ge(z_copied[1], b + 1)
                        nc.scalar.activation(sz[:, b, :], sz[:, b, :], ACT.Silu).then_inc(sz_ready, 1)

                    def high(b):
                        act.wait_ge(g_ready, b + 1)
                        if b >= 2:
                            act.wait_ge(o_psum, 2 * (b - 1))
                        nc.scalar.activation(gh[b % 2][:], sz[:, b, :], ACT.Copy).then_inc(g_high, 1)

                    silu(0)
                    silu(1)
                    act.wait_ge(z_psum, KE * B)
                    act.wait_ge(late_in, LATE_IN)
                    nc.scalar.activation(wouts[0][:], wout[:], ACT.Copy).then_inc(w_split, 1)
                    high(0)
                    act.wait_ge(vz, 3)
                    for b in range(B):
                        act.wait_ge(v_psum, 2 * (b // 2) + 2)
                        for h in range(2):
                            rows = slice(h * S, (h + 1) * S)
                            dst = vbd[rows, b, :].rearrange("p (j c) -> p j c", c=PW)[:, :, h * DK:(h + 1) * DK]
                            src = PS[rows, b // 2, (b % 2) * D:(b % 2 + 1) * D].rearrange("p (j c) -> p j c", c=2 * DK)
                            nc.scalar.activation(dst, src[:, :, h * DK:(h + 1) * DK],
                                                 ACT.Copy).then_inc(v_ready, 1)
                    for b in range(1, B):
                        if b < B - 1:
                            silu(b + 1)
                        high(b)

                @block.gpsimd
                def _(pool):
                    nc.gpsimd.memset(vbd[:], 0.0).then_inc(vz, 1)
                    pool_wait(pool, vz, 1)
                    for h in range(2):
                        v = vbd[h * S:(h + 1) * S, :, :].rearrange("p b (j c) -> p b j c", c=PW)
                        nc.gpsimd.memset(v[:, :, :, 2 * DK + h:2 * DK + h + 1], 1.0).then_inc(vz, 1)
                        pool_wait(pool, vz, 2 + h)
                    pool_wait(pool, consts_in, 32)
                    for b in range(B):
                        pool_wait(pool, hn_var, b + 1)
                        norm_rstd(pool, hn_rstd, 2 * b)
                        pool_wait(pool, hn_rstd, 2 * b + 2)
                        if b:
                            pool_wait(pool, hT_psum, b)
                        norm_apply(b, nc.gpsimd, range(TB // 2, TB)).then_inc(hn_ready[1], 1)
                    pool_wait(pool, yD_ready, KE)
                    for b in range(B):
                        for m in range(KD):
                            dst = kbd[:, b, m, :].rearrange("p (h s) -> p h s", s=S)
                            last = nc.gpsimd.tensor_tensor(
                                dst, kT[:, m, b, :].unsqueeze(1).to_broadcast([P, HH, S]),
                                headmask.unsqueeze(2).to_broadcast([P, HH, S]), ALU.mult)
                    last.then_inc(k_ready, 1)
                    pool_wait(pool, k_ready, 1)
                    pool_wait(pool, hn_var, B + 1)
                    norm_rstd(pool, hn_rstd, 2 * B)

        with ExitStack() as c:
            tmp = Place(kbd_at + 4 * B * KD * HH * S)
            gap = Place(sb.at)
            qT = gap("qT", [P, KD, L])
            pr = tmp("pr", [P, 2, H * S])
            prT = tmp("prT", [P, NP, P])
            mx = tmp("mx", [P, 2, H])
            den = tmp("den", [P, H])
            o = gap("o", [P, D])
            oTp = [gap("oT" + n, [P, KD, P], F32R) for n in "hl"]
            wqp = [gap("wq" + n, [P, KD, D], F32R) for n in "hl"]
            wop = [gap("wo" + n, [P, KD, D], F32R) for n in "hl"]
            hTp_at = Place(hT_at)
            hTp = [hTp_at("hTb" + n, [P, KD, L], F32R) for n in "hl"]
            (hn_var, hn_rstd, hn_ready, hT_psum, hT_ready, q_psum, qT_ready, bo_added,
             s_psum, s_max, s_shift, p_ready, pT_psum, pT_ready, o_psum, o_den, o_ready, oT_psum, oT_ready,
             y_psum, x2_ready, s_chain, ws_in, ws_high, ws_low, hT_high, oT_high, w_high,
             w_split) = phase_sems(c, """b_hn_var b_hn_rstd b_hn_ready b_hT_psum b_hT_ready b_q_psum b_qT_ready
                b_bo_added b_s_psum b_s_max b_s_shift b_p_ready b_pT_psum b_pT_ready b_o_psum b_o_den b_o_ready
                b_oT_psum b_oT_ready b_y_psum b_x2_ready b_chain b_ws_in b_ws_high
                b_ws_low b_hT_high b_oT_high b_w_high b_w_split""")
            with nc.Block() as block:
                @block.sync
                def _(sp):
                    sp.dma_start(fcraw[:], d["Wfc_s"].rearrange("(k p) e -> p k e", p=P)).then_inc(ws_in, 16)
                    sp.dma_start(prraw[:], d["Wproj_s"].rearrange("(k p) e -> p k e", p=P)).then_inc(ws_in, 16)

                @block.tensor
                def _(pe):
                    def transpose_x(j, t, bank=6):
                        pe.wait_ge(hn_ready, j + 1)
                        if not isinstance(j, int) or j >= TB:
                            pe.wait_ge(hT_ready, j)
                        for k in range(KD):
                            last = nc.tensor.transpose(PS[:, bank, k * P:(k + 1) * P],
                                                       hn[:, t, k * P:(k + 1) * P], ident[:])
                        last.then_inc(hT_psum, 1)

                    def project_q(b):
                        pe.wait_ge(hT_ready, TB * b + TB)
                        if not isinstance(b, int) or b:
                            pe.wait_ge(s_shift, KD * TB * b)
                        for m in range(KD):
                            for k in range(KD):
                                last = product(PS[:, m, :], [w[:, k, m * P:(m + 1) * P] for w in wqp],
                                               [x[:, k, :] for x in hTp], k == 0, k == KD - 1)
                            last.then_inc(q_psum, 1)

                    def scores(b, t):
                        i = TB * b + t
                        pe.wait_ge(qT_ready, KD * b + KD)
                        for m in range(KD):
                            if not isinstance(i, int) or i:
                                pe.wait_ge(s_shift, KD * (i - 1) + m + 1)
                            last = nc.tensor.matmul(PS[:, m, :], qT[:, m, t * P:(t + 1) * P],
                                                    kbd[:, bass.ds(b, 1), m, :].rearrange("p a n -> p (a n)"),
                                                    start=True, stop=t > 0)
                            if t == 0:
                                last = nc.tensor.matmul(PS[:, m, :], ident16[:], causal16[:], start=False,
                                                        stop=True)
                            last.then_inc(s_psum, 1)

                    def transpose_p(i, par):
                        pe.wait_ge(p_ready, i + 1)
                        if not isinstance(i, int) or i:
                            pe.wait_ge(pT_ready, i)
                        for j in range(NP):
                            last = nc.tensor.transpose(PS[:, 2 + j // 4, (j % 4) * P:(j % 4 + 1) * P],
                                                       pr[:, par, j * P:(j + 1) * P], ident[:])
                        last.then_inc(pT_psum, 1)

                    def weigh_values(i, b):
                        pe.wait_ge(pT_ready, i + 1)
                        if not isinstance(i, int) or i:
                            pe.wait_ge(o_ready, i)
                        for j in range(NP):
                            last = nc.tensor.matmul(
                                PS[:, 4, j * PW:(j + 1) * PW], prT[:, j, :],
                                vbd[:, bass.ds(b, 1), j * PW:(j + 1) * PW].rearrange("p a n -> p (a n)"),
                                start=True, stop=True)
                        last.then_inc(o_psum, 1)

                    def transpose_o(i):
                        pe.wait_ge(o_ready, i + 1)
                        if not isinstance(i, int) or i:
                            pe.wait_ge(oT_ready, i)
                        for k in range(KD):
                            last = nc.tensor.transpose(PS[:, 7, k * P:(k + 1) * P],
                                                       o[:, k * P:(k + 1) * P], ident[:])
                        last.then_inc(oT_psum, 1)

                    def project_o(i):
                        pe.wait_ge(oT_ready, i + 1)
                        if not isinstance(i, int) or i:
                            pe.wait_ge(x2_ready, i)
                        for k in range(KD):
                            last = product(PS[:, 5, 0:D], [x[:, k, :] for x in oTp],
                                           [w[:, k, :] for w in wop], k == 0, k == KD - 1)
                        last.then_inc(y_psum, 1)

                    def step(b, t, scored=True, following=True, lag2=True, lag3=True):
                        i = TB * b + t
                        if lag2:
                            transpose_p(i - 2, t % 2)
                        if scored:
                            scores(b, t)
                        if lag3:
                            transpose_o(i - 3)
                        if following:
                            transpose_x(i + TB, t)
                        if lag2:
                            weigh_values(i - 2, b if t >= 2 else b - 1)
                        if lag3:
                            project_o(i - 3)
                        if following and t == TB - 1:
                            project_q(b + 1)

                    for t in range(TB):
                        transpose_x(t, t, (6, 7, 5, 4)[t])
                    pe.wait_ge(w_split, 1)
                    project_q(0)
                    for t in range(TB):
                        if t == 3:
                            pe.wait_ge(w_split, 2)
                        step(0, t, lag2=t >= 2, lag3=t >= 3)
                    with pe.Fori(1, B - 1) as b:
                        for t in range(TB):
                            step(b, t)
                    for t in range(TB):
                        step(B - 1, t, following=False)
                    for t in range(3):
                        step(B, t, scored=False, following=False, lag2=t < 2)

                @block.scalar
                def _(act):
                    def evac_x(j, t, bank=6):
                        act.wait_ge(hT_psum, j + 1)
                        nc.scalar.activation(hTp[0][:, :, t * P:(t + 1) * P],
                                             PS[:, bank, 0:D].rearrange("p (k n) -> p k n", k=KD),
                                             ACT.Copy).then_inc(hT_high, 1)

                    def evac_q(b):
                        for m in range(KD):
                            act.wait_ge(q_psum, KD * b + m + 1)
                            nc.scalar.activation(qT[:, m, :], PS[:, m, :], ACT.Identity,
                                                 bias=bq[:, m:m + 1]).then_inc(qT_ready, 1)

                    def evac_p(i):
                        act.wait_ge(pT_psum, i + 1)
                        nc.scalar.activation(prT[:].rearrange("p j n -> p (j n)"),
                                             PS[:, 2:4, :].rearrange("p a n -> p (a n)"),
                                             ACT.Copy).then_inc(pT_ready, 1)

                    def evac_o(i):
                        act.wait_ge(oT_psum, i + 1)
                        nc.scalar.activation(oTp[0][:].rearrange("p k n -> p (k n)"), PS[:, 7, 0:D],
                                             ACT.Copy).then_inc(oT_high, 1)

                    def exps(i, par):
                        act.wait_ge(s_shift, KD * i + KD)
                        nc.scalar.activation(pr[:, par, :], pr[:, par, :], ACT.Exp,
                                             scale=SCALE).then_inc(p_ready, 1)

                    def step(b, t, scored=True, following=True, lag2=True, lag3=True):
                        i = TB * b + t
                        if lag2:
                            evac_p(i - 2)
                        if lag3:
                            evac_o(i - 3)
                        if following:
                            evac_x(i + TB, t)
                        if scored:
                            exps(i, t % 2)
                        if following and t == TB - 1:
                            evac_q(b + 1)

                    nc.scalar.activation(wqp[0][:], wq[:], ACT.Copy).then_inc(w_high, 1)
                    for t in range(TB):
                        evac_x(t, t, (6, 7, 5, 4)[t])
                    nc.scalar.activation(wop[0][:], wo[:], ACT.Copy).then_inc(w_high, 1)
                    evac_q(0)
                    for t in range(TB):
                        step(0, t, lag2=t >= 2, lag3=t >= 3)
                        if t == 0:
                            act.wait_ge(ws_in, 32)
                        to, whole = ((wfs, fcraw), (wps, prraw))[t // 2]
                        half = slice(t % 2 * (whole.shape[1] // 2), (t % 2 + 1) * (whole.shape[1] // 2))
                        nc.scalar.activation(to[0][:, half], whole[:, half], ACT.Copy).then_inc(ws_high, 1)
                    with act.Fori(1, B - 1) as b:
                        for t in range(TB):
                            step(b, t)
                    for t in range(TB):
                        step(B - 1, t, following=False)
                    for t in range(3):
                        step(B, t, scored=False, following=False, lag2=t < 2)

                @block.gpsimd
                def _(pool):
                    def rstds(i):
                        pool_wait(pool, hn_var, i + 1)
                        norm_rstd(pool, hn_rstd, 2 * i)

                    pool.sem_inc(hn_rstd, 2)
                    def add_bo(b):
                        pool_wait(pool, hn_ready, TB * b + TB)
                        xs = X[:, bass.ds(TB * b, TB), :]
                        nc.gpsimd.tensor_tensor(xs, xs, bo[:].unsqueeze(1).to_broadcast([P, TB, D]),
                                                ALU.add).then_inc(bo_added, 1)
                    add_bo(0)
                    rstds(1)
                    add_bo(1)
                    pool_wait(pool, ws_high, TB)
                    for b, parts, whole in ((2, wfs, fcraw), (3, wps, prraw)):
                        rstds(b)
                        add_bo(b)
                        low(nc.gpsimd, parts[1][:], whole[:], parts[0][:]).then_inc(ws_low, 1)
                    with pool.Fori(4, B) as b:
                        rstds(b)
                        add_bo(b)
                    rstds(B)

                @block.vector
                def _(dve):
                    base = [0]
                    n = [0]
                    def link(ins):
                        n[0] += 1
                        ins.then_inc(s_chain, 1)
                        dve.wait_ge(s_chain, base[0] + n[0])

                    def tile(j):
                        return X[:, bass.ds(j, 1), :].rearrange("p a d -> p (a d)")

                    def stats_part(b):
                        norm_stats(link, [tile(TB * b + t) for t in range(TB)]).then_inc(hn_var, 1)

                    def apply_part(b, t):
                        j = TB * b + t
                        if t == 0:
                            dve.wait_ge(hn_rstd, 2 * b + 2)
                        if not isinstance(j, int) or j >= TB:
                            dve.wait_ge(hT_psum, j - TB + 1)
                        nc.vector.tensor_scalar(hn[:, t, :], tile(j), mv[:, t, 0:1], rstd[:, t:t + 1],
                                                ALU.subtract, ALU.mult).then_inc(hn_ready, 1)

                    def x_low(j, t, bank=6):
                        dve.wait_ge(hT_high, j + 1)
                        low(nc.vector, hTp[1][:, :, t * P:(t + 1) * P],
                            PS[:, bank, 0:D].rearrange("p (k n) -> p k n", k=KD),
                            hTp[0][:, :, t * P:(t + 1) * P]).then_inc(hT_ready, 1)

                    def o_low(i):
                        dve.wait_ge(oT_high, i + 1)
                        low(nc.vector, oTp[1][:].rearrange("p k n -> p (k n)"), PS[:, 7, 0:D],
                            oTp[0][:].rearrange("p k n -> p (k n)")).then_inc(oT_ready, 1)

                    def maxima(i, par):
                        for m in range(KD):
                            dve.wait_ge(s_psum, KD * i + m + 1)
                            nc.vector.tensor_reduce(mx[:, par, m * HH:(m + 1) * HH],
                                                    PS[:, m, :].rearrange("p (h s) -> p h s", s=S),
                                                    op=ALU.max, axis=AX).then_inc(s_max, 1)

                    def shift(i, par):
                        if not isinstance(i, int) or i >= 2:
                            dve.wait_ge(pT_psum, i - 1)
                        for m in range(KD):
                            dve.wait_ge(s_max, KD * i + m + 1)
                            nc.vector.tensor_tensor(
                                pr[:, par, m * HH * S:(m + 1) * HH * S].rearrange("p (h s) -> p h s", s=S),
                                PS[:, m, :].rearrange("p (h s) -> p h s", s=S),
                                mx[:, par, m * HH:(m + 1) * HH].unsqueeze(2).to_broadcast([P, HH, S]),
                                ALU.subtract).then_inc(s_shift, 1)

                    def divide(i):
                        dve.wait_ge(o_psum, i + 1)
                        ps = PS[:, 4, 0:NP * PW].rearrange("p (j c) -> p j c", c=PW)
                        nc.vector.reciprocal(den[:].rearrange("p (j c) -> p j c", c=2),
                                             ps[:, :, 2 * DK:PW]).then_inc(o_den, 1)
                        dve.wait_ge(o_den, i + 1)
                        src = ps[:, :, 0:2 * DK].rearrange("p j (c e) -> p j c e", c=2)
                        nc.vector.tensor_tensor(
                            o[:].rearrange("p (j c e) -> p j c e", j=NP, c=2), src,
                            den[:].rearrange("p (j c) -> p j c", c=2).unsqueeze(3).to_broadcast([P, NP, 2, DK]),
                            ALU.mult).then_inc(o_ready, 1)

                    def residual(i, b):
                        dve.wait_ge(bo_added, b + 1)
                        dve.wait_ge(y_psum, i + 1)
                        nc.vector.tensor_tensor(tile(i), tile(i), PS[:, 5, 0:D], ALU.add).then_inc(x2_ready, 1)

                    def step(b, t, scored=True, following=True, lag3=True, lag4=True):
                        i = TB * b + t
                        if lag3:
                            divide(i - 3)
                        if lag4:
                            residual(i - 4, b - 1)
                        if following:
                            apply_part(b + 1, t)
                        if scored:
                            maxima(i, t % 2)
                        if lag3:
                            o_low(i - 3)
                        if scored:
                            shift(i, t % 2)
                        if following:
                            x_low(i + TB, t)

                    dve.sem_inc(hn_var, 1)
                    dve.sem_inc(hn_ready, TB)
                    for k, (whole, parts) in enumerate(((wq, wqp), (wo, wop))):
                        if k:
                            for t in range(TB):
                                x_low(t, t, (6, 7, 5, 4)[t])
                        dve.wait_ge(w_high, k + 1)
                        low(nc.vector, parts[1][:], whole[:], parts[0][:]).then_inc(w_split, 1)
                    stats_part(1)
                    for t in range(TB):
                        step(0, t, lag3=t >= 3, lag4=False)
                    with dve.Fori(1, B - 1) as b:
                        n[0] = 0
                        base[0] = b
                        dve.wait_ge(hn_ready, TB * b + TB)
                        stats_part(b + 1)
                        for t in range(TB):
                            step(b, t)
                    for t in range(TB):
                        step(B - 1, t, following=False)
                        if t == 0:
                            n[0] = 0
                            base[0] = B - 1
                            dve.wait_ge(hn_ready, TB * B)
                            dve.wait_ge(x2_ready, TB)
                            norm_stats(link, [X[:, u, :] for u in range(TB)]).then_inc(hn_var, 1)
                        if t == 2:
                            dve.wait_ge(hn_rstd, 2 * B + 2)
                            dve.wait_ge(hT_psum, TB * B)
                            norm_apply(0)
                    for t in range(TB):
                        step(B, t, scored=False, following=False, lag3=t < 3)
                    dve.wait_ge(x2_ready, N // P)

        with ExitStack() as c:
            tmp = Place(sb.at)
            wfc = [tmp("wfc" + n, [P, 2, KD, HID], F32R) for n in "hl"]
            wpr = [tmp("wpr" + n, [P, 2, KH, D], F32R) for n in "hl"]
            bfc = tmp("bfc", [P, E, KH])
            carry = tmp("carry", [P, E])
            (w_in, hn_var, hn_rstd, hn_ready, hT_psum, hT_ready, h_psum, h_ready, y_psum, x3_ready,
             l_psum, l_read, chosen, r_psum, r_read, gates_exp, slots_ready, rows_ready, hn_copied, scattered,
             bias_added, carry_ready, pads_stored, stored, s_chain, pads_zeroed, wr_split, hT_high,
             l_ready, raw_in, e_high, e_low, lT_psum, lT_ready, ends_ready, wr_in) = phase_sems(
                ctx, """c_w_in c_hn_var c_hn_rstd c_hn_ready c_hT_psum c_hT_ready c_h_psum c_h_ready c_y_psum
                c_x3_ready c_l_psum c_l_read c_chosen c_r_psum c_r_read c_gates_exp c_slots_ready c_rows_ready
                c_hn_copied c_scattered c_bias_added c_carry_ready c_pads_stored c_stored c_chain
                c_pads_zeroed c_wr_split c_hT_high c_l_ready c_raw_in c_e_high c_e_low c_lT_psum c_lT_ready
                c_ends_ready c_wr_in""")
            HELD = 4
            tbl = tmp("tbl", [P, 2 * E], I32)

            def load_weights(pool, e):
                pool.dma_start(fcraw[:], d["Wfc"][bass.ds(e, 1)].rearrange("a (k p) n -> p (a k) n",
                                                                           p=P)).then_inc(raw_in, 16)
                pool.dma_start(prraw[:], d["Wproj"][bass.ds(e, 1)].rearrange("a (k p) n -> p (a k) n",
                                                                             p=P)).then_inc(raw_in, 16)

            def split_high(par):
                nc.scalar.activation(wfc[0][:, par], fcraw[:], ACT.Copy).then_inc(e_high, 1)
                nc.scalar.activation(wpr[0][:, par], prraw[:], ACT.Copy).then_inc(e_high, 1)

            experts_at = tmp.at
            first_rows = Place(experts_at)
            xr = first_rows("xr", [P, 2, ROW])
            x_in, = phase_sems(ctx, "d_x_in")
            rg = RG.rearrange("(n h p) c -> n p h c", h=2, p=P)
            tm = Place(experts_at)
            wr = tm("wr", [P, KD, E])
            lT = tm("lT", [E, L])
            wrp = [tm("wr" + n, [P, KD, E], F32R) for n in "hl"]
            xTp = [tm("xT" + n, [P, KD, L], F32R) for n in "hl"]
            bfs = tm("bfs", [P, KH])
            bps = tm("bps", [P, D])
            act32 = tm("act32", [P, 2, L])
            hid = [tm("hid" + n, [P, KH, L], F32R) for n in "hl"]
            rows = tm("rows", [P, TB, ROW])
            pads = tm("pads", [P, 2, ROW])
            tok = tm("tok", [P, TB])
            lg = tm("lg", [P, 8, TB, E])
            oh = tm("oh", [P, 2, TB, E])
            both = tm("both", [P, TB, E], BF16)
            triones = tm("triones", [P, 2, P], BF16)
            m4 = tm("m4", [P, 8, TB])
            meta = tm("meta", [P, TB, ROW - D])
            slot = tm("slot", [P, TB, 2], I32)
            slotc = tm("slotc", [P, TB, 2], I32)
            ends = tm("ends", [P, E], I32)
            cnt = tm("cnt", [P, 4, E])
            cmp_ = tm("cmp", [P, E, NBR - 1])
            W_IN = 16 * 3
            with nc.Block() as block:
                @block.sync
                def _(sp):
                    sp.dma_start(wr[:], d["Wr"].rearrange("(k p) e -> p k e", p=P)).then_inc(wr_in, 16)
                    for dst, src in ((bfs[:], d["bfc_s"]), (bps[:], d["bproj_s"].to_broadcast([P, D])),
                                     (bfc[:], d["bfc"])):
                        sp.dma_start(dst, src).then_inc(w_in, 16)
                    ov = out.rearrange("(t p) d -> p t d", p=P)
                    with sp.Fori(0, B - 1) as b:
                        sp.wait_ge(x3_ready, TB * b + 2 * TB)
                        sp.dma_start(ov[:, bass.ds(TB * b, TB), :], X[:, bass.ds(TB * b, TB), :]).then_inc(stored, 16)
                    sp.wait_ge(pads_zeroed, 1)
                    sp.dma_start(out[N:N + BLK, :].rearrange("(h p) d -> p h d", p=P),
                                 pads[:, :, 0:D]).then_inc(stored, 16)
                    sp.wait_ge(ends_ready, 1)
                    ends_of = [sp.value_load(ends[0:1, e:e + 1], min_val=e * ROOM, max_val=e * ROOM + N)
                               for e in range(E)]
                    for end in ends_of:
                        sp.dma_start(RG[bass.ds(end, BLK), :].rearrange("(h p) c -> p h c", p=P),
                                     pads[:]).then_inc(pads_stored, 16)
                    sp.wait_ge(x3_ready, TB * (B - 1) + 2 * TB)
                    sp.dma_start(ov[:, TB * (B - 1):TB * B, :], X[:, TB * (B - 1):, :]).then_inc(stored, 16)
                    sp.wait_ge(pads_stored, 16 * E)
                    sp.wait_ge(scattered, 16 * 2 * TB * B)
                    sp.dma_start(xr[:], rg[0].rearrange("p h c -> p h c")).then_inc(x_in, 16)
                    sp.wait_ge(stored, 16 * B + 16)

                @block.tensor
                def _(pe):
                    def transposes(b):
                        pe.wait_ge(hn_ready, b + 1)
                        if not isinstance(b, int) or b:
                            pe.wait_ge(lT_ready, b)
                            pe.wait_ge(r_read, b)
                        for t in range(TB):
                            for k in range(KD):
                                last = nc.tensor.transpose(PS[:, 4 + k, t * P:(t + 1) * P],
                                                           hn[:, t, k * P:(k + 1) * P], ident[:])
                        last.then_inc(hT_psum, 1)

                    def up(b, js):
                        for j in js:
                            pe.wait_ge(h_ready, KH * b + j + 1)
                            js = slice(j * P, (j + 1) * P)
                            for k in range(KD):
                                last = product(PS[:, j % 4, :], [w[:, k, js] for w in wfs],
                                               [x[:, k, :] for x in xTp], k == 0, k == KD - 1)
                            last.then_inc(h_psum, 1)

                    def logits(b):
                        pe.wait_ge(hT_ready, KD * b + KD)
                        for k in range(KD):
                            last = product(PS[0:E, 4, :], [w[:, k, :] for w in wrp],
                                           [x[:, k, :] for x in xTp], k == 0, k == KD - 1)
                        last.then_inc(lT_psum, 1)

                    def transpose_logits(b):
                        pe.wait_ge(lT_ready, b + 1)
                        pe.sem_inc(pe_waits, 1)
                        for t in range(TB):
                            last = nc.tensor.transpose(PS[:, 5, t * E:(t + 1) * E], lT[0:E, t * P:(t + 1) * P],
                                                       ident[0:E, 0:E])
                        last.then_inc(l_psum, 1)

                    def ranks(b):
                        pe.wait_ge(chosen, b + 1)
                        for t in range(TB):
                            for s in range(t + 1):
                                last = nc.tensor.matmul(PS[:, 5, (TB + t) * E:(TB + t + 1) * E],
                                                        triones[:, 0 if s == t else 1, :], both[:, s, :],
                                                        start=s == 0, stop=s == t)
                        for s in range(TB):
                            last = nc.tensor.matmul(PS[:, 5, 2 * TB * E:(2 * TB + 1) * E], triones[:, 1, :], both[:, s, :],
                                                    start=s == 0, stop=s == TB - 1)
                        last.then_inc(r_psum, 1)

                    def down(b, tiles):
                        for t in tiles:
                            if t % 2 == 0:
                                pe.wait_ge(x3_ready, TB * b + t + 2)
                            for j in range(KH):
                                if t == 0:
                                    pe.wait_ge(l_ready, KH * b + j + 1 + 2)
                                last = product(PS[:, 6 + t // 2, (t % 2) * D:(t % 2 + 1) * D],
                                               [h[:, j, t * P:(t + 1) * P] for h in hid],
                                               [w[:, j, :] for w in wps], j == 0, j == KH - 1)
                            if t % 2:
                                last.then_inc(y_psum, 1)

                    transposes(0)
                    pe.wait_ge(hT_ready, KD)
                    up(0, range(2))
                    pe.wait_ge(wr_split, 2)
                    logits(0)
                    transpose_logits(0)
                    with pe.Fori(0, B - 1) as b:
                        ranks(b)
                        up(b, range(2, KH))
                        transposes(b + 1)
                        down(b, range(2))
                        logits(b + 1)
                        down(b, range(2, 3))
                        transpose_logits(b + 1)
                        down(b, range(3, TB))
                        up(b + 1, range(2))
                    ranks(B - 1)
                    up(B - 1, range(2, KH))
                    down(B - 1, range(TB))

                @block.scalar
                def _(act):
                    def evac(b):
                        act.wait_ge(hT_psum, b + 1)
                        for k in range(KD):
                            nc.scalar.activation(xTp[0][:, k, :], PS[:, 4 + k, :], ACT.Copy).then_inc(hT_high, 1)

                    def gelus(b):
                        for j in range(KH):
                            act.wait_ge(h_psum, KH * b + j + 1)
                            nc.scalar.activation(hid[0][:, j, :], PS[:, j % 4, :], ACT.Gelu_apprx_tanh,
                                                 bias=bfs[:, j:j + 1])
                            act.wait_ge(l_ready, KH * b + j + 1)
                            nc.scalar.activation(act32[:, j % 2, :], PS[:, j % 4, :], ACT.Gelu_apprx_tanh,
                                                 bias=bfs[:, j:j + 1]).then_inc(h_ready, 1)
                            if j == 3:
                                act.wait_ge(chosen, b + 1)
                                nc.scalar.activation(m4[:, 3, :], m4[:, 2, :], ACT.Tanh,
                                                     scale=0.5).then_inc(gates_exp, 1)
                                if not isinstance(b, int) or b:
                                    act.wait_ge(scattered, 16 * 2 * TB * b)
                                nc.scalar.activation(rows[:, :, 0:D], hn[:], ACT.Copy).then_inc(hn_copied, 1)

                    def evac_logits(b):
                        act.wait_ge(lT_psum, b + 1)
                        nc.scalar.activation(lT[0:E, :], PS[0:E, 4, :], ACT.Copy).then_inc(lT_ready, 1)

                    act.sem_inc(h_ready, HELD)
                    evac(0)
                    act.wait_ge(w_in, W_IN)
                    evac_logits(0)
                    gelus(0)
                    evac(1)
                    evac_logits(1)
                    with act.Fori(1, B // 2) as b:
                        gelus(b)
                        evac(b + 1)
                        evac_logits(b + 1)
                    act.wait_ge(raw_in, 32)
                    split_high(0)
                    with act.Fori(B // 2, B - 1) as b:
                        gelus(b)
                        evac(b + 1)
                        evac_logits(b + 1)
                    gelus(B - 1)

                @block.gpsimd
                def _(pool):
                    def rstds(b):
                        pool_wait(pool, hn_var, b + 1)
                        norm_rstd(pool, hn_rstd, 2 * b)

                    def add_bias(b):
                        pool_wait(pool, hn_ready, b + 1)
                        xs = X[:, bass.ds(TB * b, TB), :]
                        nc.gpsimd.tensor_tensor(xs, xs, bps[:].unsqueeze(1).to_broadcast([P, TB, D]),
                                                ALU.add).then_inc(bias_added, 1)

                    def send_rows(b):
                        pool_wait(pool, slots_ready, b + 1)
                        nc.gpsimd.tensor_copy(rows[:, :, D:ROW], meta[:]).then_inc(rows_ready, 1)
                        nc.gpsimd.tensor_copy(slotc[:], slot[:]).then_inc(rows_ready, 1)
                        pool_wait(pool, rows_ready, 2 * b + 4)
                        pool_wait(pool, hn_copied, b + 1)
                        for t in range(TB):
                            for m in range(2):
                                nc.gpsimd.indirect_dma_start(
                                    out=RG, out_offset=bass.IndirectOffsetOnAxis(ap=slotc[:, t, m:m + 1], axis=0),
                                    in_=rows[:, t, :], in_offset=None).then_inc(scattered, 16)

                    load_weights(pool, 0)
                    pool_wait(pool, w_in, W_IN)
                    nc.gpsimd.memset(pads[:], 0.0).then_inc(pads_zeroed, 1)
                    pool.sem_inc(rows_ready, 2)
                    pool.sem_inc(hn_rstd, 2)
                    add_bias(0)
                    with pool.Fori(0, B // 2 + 1) as b:
                        rstds(b + 1)
                        send_rows(b)
                        add_bias(b + 1)
                    pool_wait(pool, e_high, 2)
                    low(nc.gpsimd, wfc[1][:, 0], fcraw[:], wfc[0][:, 0]).then_inc(e_low, 1)
                    rstds(B // 2 + 2)
                    send_rows(B // 2 + 1)
                    add_bias(B // 2 + 2)
                    low(nc.gpsimd, wpr[1][:, 0], prraw[:], wpr[0][:, 0]).then_inc(e_low, 1)
                    with pool.Fori(B // 2 + 2, B - 1) as b:
                        rstds(b + 1)
                        send_rows(b)
                        add_bias(b + 1)
                    pool_wait(pool, e_low, 2)
                    load_weights(pool, 1)
                    send_rows(B - 1)
                    pool_wait(pool, scattered, 16 * 2 * TB * B)

                @block.vector
                def _(dve):
                    base = [0]
                    n = [0]
                    def link(ins):
                        n[0] += 1
                        ins.then_inc(s_chain, 1)
                        dve.wait_ge(s_chain, base[0] + n[0])

                    def tiles(b):
                        return [X[:, TB * b + t, :] for t in range(TB)]

                    def stats_part(b):
                        norm_stats(link, tiles(b)).then_inc(hn_var, 1)

                    def apply_part(b):
                        if not isinstance(b, int) or b:
                            dve.wait_ge(hT_psum, b)
                            dve.wait_ge(hn_copied, b)
                        dve.wait_ge(hn_rstd, 2 * b + 2)
                        norm_apply(b).then_inc(hn_ready, 1)

                    def first_of(score, top, choice):
                        link(nc.vector.tensor_reduce(top, score, op=ALU.max, axis=AX))
                        link(nc.vector.tensor_tensor(lg[:, 2, :, :], score,
                                                     top.unsqueeze(2).to_broadcast([P, TB, E]), ALU.is_equal))
                        link(nc.vector.tensor_tensor(lg[:, 2, :, :], lg[:, 2, :, :],
                                                     tiew.unsqueeze(1).to_broadcast([P, TB, E]), ALU.mult))
                        link(nc.vector.tensor_reduce(m4[:, 4, :], lg[:, 2, :, :], op=ALU.max, axis=AX))
                        link(nc.vector.tensor_tensor(choice, lg[:, 2, :, :],
                                                     m4[:, 4, :].unsqueeze(2).to_broadcast([P, TB, E]),
                                                     ALU.is_equal))

                    def choose(b):
                        dve.wait_ge(l_psum, b + 1)
                        nc.vector.tensor_copy(lg[:, 0, :, :].rearrange("p t e -> p (t e)"),
                                              PS[:, 5, 0:TB * E]).then_inc(l_read, 1)
                        dve.wait_ge(l_read, b + 1)
                        first_of(lg[:, 0, :, :], m4[:, 0, :], oh[:, 0, :, :])
                        link(nc.vector.scalar_tensor_tensor(lg[:, 1, :, :], oh[:, 0, :, :], -BIG, lg[:, 0, :, :],
                                                            ALU.mult, ALU.add))
                        first_of(lg[:, 1, :, :], m4[:, 1, :], oh[:, 1, :, :])
                        link(nc.vector.tensor_tensor(m4[:, 2, :], m4[:, 0, :], m4[:, 1, :], ALU.subtract))
                        nc.vector.tensor_tensor(both[:], oh[:, 0, :, :], oh[:, 1, :, :],
                                                ALU.add).then_inc(chosen, 1)

                    def lows(b, js):
                        for j in js:
                            dve.wait_ge(h_ready, KH * b + j + 1 + HELD)
                            low(nc.vector, hid[1][:, j, :], act32[:, j % 2, :], hid[0][:, j, :]).then_inc(l_ready, 1)

                    def x_low(b):
                        for k in range(KD):
                            dve.wait_ge(hT_high, KD * b + k + 1)
                            low(nc.vector, xTp[1][:, k, :], PS[:, 4 + k, :], xTp[0][:, k, :]).then_inc(hT_ready, 1)

                    CHOOSE = 12

                    pos = lg[:, 3, :, :]

                    def place_rows(b):
                        dve.wait_ge(r_psum, b + 1)
                        link(nc.vector.tensor_tensor(pos,
                                                     PS[:, 5, TB * E:2 * TB * E].rearrange("p (t e) -> p t e", e=E),
                                                     carry[:].unsqueeze(1).to_broadcast([P, TB, E]), ALU.add))
                        nc.vector.tensor_tensor(carry[:], carry[:], PS[:, 5, 2 * TB * E:(2 * TB + 1) * E],
                                                ALU.add).then_inc(r_read, 1)

                    def place(b):
                        dve.wait_ge(rows_ready, 2 * b + 2)
                        for m in range(2):
                            link(nc.vector.tensor_tensor(lg[:, 4 + m, :, :], pos, oh[:, m, :, :], ALU.mult))
                            link(nc.vector.tensor_reduce(m4[:, 5 + m, :], lg[:, 4 + m, :, :], op=ALU.add, axis=AX))
                            link(nc.vector.tensor_copy(slot[:, :, m], m4[:, 5 + m, :]))
                        dve.wait_ge(gates_exp, b + 1)
                        for m, sign in enumerate((0.5, -0.5)):
                            link(nc.vector.tensor_scalar(m4[:, 7, :], m4[:, 3, :], sign, 0.5, ALU.mult, ALU.add))
                            link(nc.vector.tensor_tensor(lg[:, 4 + m, :, :], oh[:, m, :, :],
                                                         m4[:, 7, :].unsqueeze(2).to_broadcast([P, TB, E]),
                                                         ALU.mult))
                        link(nc.vector.tensor_tensor(meta[:, :, 0:E], lg[:, 4, :, :], lg[:, 5, :, :], ALU.add))
                        nc.vector.tensor_copy(meta[:, :, E], tok[:]).then_inc(slots_ready, 1)
                        dve.wait_ge(slots_ready, b + 1)
                        link(nc.vector.tensor_scalar(tok[:], tok[:], float(L), None, ALU.add))

                    PLACE = 13

                    def residual(b, halves):
                        dve.wait_ge(bias_added, b + 1)
                        for i in halves:
                            dve.wait_ge(y_psum, 2 * b + i + 1)
                            xs = X[:, bass.ds(TB * b + 2 * i, 2), :].rearrange("p t d -> p (t d)")
                            nc.vector.tensor_tensor(xs, xs, PS[:, 6 + i, :], ALU.add).then_inc(x3_ready, 2)

                    dve.sem_inc(hn_var, 1)
                    dve.sem_inc(hn_ready, 1)
                    dve.sem_inc(x3_ready, TB)
                    nc.vector.tensor_copy(carry[:], ebase)
                    for t in range(TB):
                        nc.vector.tensor_scalar(tok[:, t:t + 1], rowno[:, 0:1], float(t * P), None, ALU.add)
                    link(nc.vector.memset(meta[:], 0.0))
                    dve.sem_inc(l_ready, 2)
                    nc.vector.tensor_copy(triones[:, 0, :], tri[:])
                    nc.vector.tensor_copy(triones[:, 1, :], ones[:])
                    x_low(0)
                    dve.wait_ge(wr_in, 16)
                    nc.vector.tensor_copy(wrp[0][:], wr[:]).then_inc(wr_split, 1)
                    dve.wait_ge(wr_split, 1)
                    low(nc.vector, wrp[1][:], wr[:], wrp[0][:]).then_inc(wr_split, 1)
                    choose(0)
                    with dve.Fori(0, B - 1) as b:
                        n[0] = 0
                        base[0] = (1 + CHOOSE + PLACE) * b + (1 + CHOOSE)
                        lows(b, range(0, 2))
                        stats_part(b + 1)
                        lows(b, range(2, 4))
                        place_rows(b)
                        apply_part(b + 1)
                        lows(b, range(4, KH))
                        x_low(b + 1)
                        place(b)
                        residual(b, range(1))
                        choose(b + 1)
                        residual(b, range(1, 2))
                        assert n[0] == 1 + CHOOSE + PLACE, n
                    n[0] = 0
                    base[0] = (1 + CHOOSE + PLACE) * (B - 1) + (1 + CHOOSE)
                    lows(B - 1, range(4))
                    place_rows(B - 1)
                    lows(B - 1, range(4, KH))
                    place(B - 1)
                    dve.wait_ge(pads_zeroed, 1)
                    for h in range(2):
                        nc.vector.tensor_scalar(pads[:, h, TOK:TOK + 1], rowno[:, h:h + 1], float(N), None, ALU.add)
                    nc.vector.tensor_copy(ends[:], carry[:]).then_inc(ends_ready, 1)
                    link(nc.vector.tensor_tensor(cnt[:, 0, :], carry[:], ebase, ALU.subtract))
                    for j in range(1, NBR - 1):
                        nc.vector.tensor_scalar(cmp_[:, :, j - 1], cnt[:, 0, :], float(BLK * j), None,
                                                ALU.is_gt)
                    link(nc.vector.memset(cmp_[:, :, NBR - 2], 1.0))
                    link(nc.vector.tensor_reduce(cnt[:, 1, :], cmp_[:], op=ALU.add, axis=AX))
                    link(nc.vector.tensor_tensor_scan(cnt[:, 2, :], ones[:, 0:E], cnt[:, 1, :], 0.0,
                                                      ALU.mult, ALU.add))
                    link(nc.vector.tensor_tensor(cnt[:, 2, :], cnt[:, 2, :], cnt[:, 1, :], ALU.subtract))
                    link(nc.vector.tensor_copy(tbl[:, 0:E], cnt[:, 1, :]))
                    nc.vector.tensor_copy(tbl[:, E:2 * E], cnt[:, 2, :]).then_inc(carry_ready, 1)
                    residual(B - 1, range(2))
                    dve.wait_ge(x3_ready, TB * B + TB)

            tm = Place(experts_at)
            tm.at = first_rows.at
            xTp = [tm("xTe" + n, [P, KD, BLK], F32R) for n in "hl"]
            act32 = tm("act32e", [P, 2, BLK])
            bpr = tm("bpr", [P, E, D])
            be = tm("be", [P, 2, KH])
            hid = [tm("hide" + n, [P, KH, BLK], F32R) for n in "hl"]
            meta = tm("metae", [P, 2, ROW - D])
            gate = tm("gate", [P, 2])
            toki = tm("toki", [P, 2], I32)
            y = tm("y", [P, 2, D])
            (x_psum, xT_ready, xr_free, h_psum, h_ready, y_psum, y_read, y_ready, gate_ready,
             added, y_sent, b_in, xT_high, l_ready, be_ready) = phase_sems(c, """d_x_psum d_xT_ready d_xr_free d_h_psum
                d_h_ready d_y_psum d_y_read d_y_ready d_gate_ready d_added d_y_sent d_b_in
                d_xT_high d_l_ready d_be_ready""")

            def blocks_of(eng, e):
                return (eng.value_load(tbl[0:1, bass.ds(e, 1)], min_val=1, max_val=NBR - 1),
                        eng.value_load(tbl[0:1, bass.ds(E + e, 1)], min_val=0, max_val=2 * N // BLK + E))

            def every_block(eng, body, head=None):
                with eng.Fori(0, E // 2) as pair:
                    for par in range(2):
                        e = pair * 2 + par
                        if head:
                            head(pair, e, par)
                        count, before = blocks_of(eng, e)
                        with eng.Fori(0, count) as i:
                            body(before + i, e, par, i)

            with nc.Block() as block:
                @block.sync
                def _(sp):
                    def load(g, e, par, i):
                        sp.wait_ge(xr_free, g + 1)
                        sp.dma_start(xr[:].rearrange("p (a h) c -> p a h c", a=1),
                                     rg[bass.ds(e * NBR + i, 1)].rearrange("a p h c -> p a h c")).then_inc(x_in, 16)
                    def load_next(g, e, par, i):
                        with sp.If(g > 0):
                            load(g, e, par, i)
                    every_block(sp, load_next)
                    _, before = blocks_of(sp, E - 1)
                    count, _ = blocks_of(sp, E - 1)
                    load(before + count, E - 1, 1, 0)
                    sp.wait_ge(x_in, (before + count) * 16 + 16)
                    sp.sem_inc(sp_waits, 1)

                @block.tensor
                def _(pe):
                    def transposes(g):
                        pe.wait_ge(x_in, g * 16 + 16)
                        if not isinstance(g, int):
                            pe.wait_ge(xT_ready, g)
                        for k in range(KD):
                            for h in range(2):
                                last = nc.tensor.transpose(PS[:, 4, k * BLK + h * P:k * BLK + (h + 1) * P],
                                                           xr[:, h, k * P:(k + 1) * P], ident[:])
                        last.then_inc(x_psum, 1)

                    def one(g, e, par, i):
                        pe.wait_ge(xT_ready, g + 1)
                        for j in range(KH):
                            pe.wait_ge(h_ready, g * KH + j + 1)
                            for k in range(KD):
                                last = product(PS[:, j % 4, 0:BLK], [w[:, par, k, j * P:(j + 1) * P] for w in wfc],
                                               [x[:, k, :] for x in xTp], k == 0, k == KD - 1)
                            last.then_inc(h_psum, 1)
                        transposes(g + 1)
                        for h in range(2):
                            pe.wait_ge(y_read, g * 2 + h + 1)
                            for j in range(KH):
                                if h == 0:
                                    pe.wait_ge(l_ready, g * KH + j + 1 + 2)
                                last = product(PS[:, 5 + h, 0:D], [x[:, j, h * P:(h + 1) * P] for x in hid],
                                               [w[:, par, j, :] for w in wpr], j == 0, j == KH - 1)
                            last.then_inc(y_psum, 1)

                    transposes(0)
                    every_block(pe, one, lambda pair, e, par: pe.wait_ge(e_low, e * 2 + 2))

                @block.scalar
                def _(act):
                    act.sem_inc(h_ready, HELD)

                    def x_high(g):
                        act.wait_ge(x_psum, g + 1)
                        nc.scalar.activation(xTp[0][:].rearrange("p k n -> p (k n)"), PS[:, 4, :],
                                             ACT.Copy).then_inc(xT_high, 1)

                    def gelus(g, e, par, i):
                        for j in range(KH):
                            bias = be[:, par, j:j + 1]
                            act.wait_ge(h_psum, g * KH + j + 1)
                            nc.scalar.activation(hid[0][:, j, :], PS[:, j % 4, 0:BLK], ACT.Gelu_apprx_tanh, bias=bias)
                            act.wait_ge(l_ready, g * KH + j + 1)
                            nc.scalar.activation(act32[:, j % 2, :], PS[:, j % 4, 0:BLK], ACT.Gelu_apprx_tanh,
                                                 bias=bias).then_inc(h_ready, 1)
                        x_high(g + 1)
                        with act.If(i * E + e < E - 1):
                            act.wait_ge(raw_in, e * 32 + 64)
                            split_high(1 - par)

                    def head(pair, e, par):
                        nc.scalar.activation(be[:, par, :], bfc[:, bass.ds(e, 1), :].rearrange("p a j -> p (a j)"),
                                             ACT.Copy).then_inc(be_ready, 1)
                        act.wait_ge(be_ready, e + 1)

                    x_high(0)
                    nc.scalar.dma_start(bpr[:].rearrange("p e d -> p (e d)"),
                                        d["bproj"].to_broadcast([P, E * D])).then_inc(b_in, 16)
                    every_block(act, gelus, head)

                @block.gpsimd
                def _(pool):
                    pool.sem_inc(y_sent, 1)

                    def send(g, e, par, i):
                        pool_wait(pool, y_ready, g * 2 + 2)
                        for h in range(2):
                            nc.gpsimd.indirect_dma_start(
                                out=out, out_offset=bass.IndirectOffsetOnAxis(ap=toki[:, h:h + 1], axis=0),
                                in_=y[:, h, :], in_offset=None, compute_op=ALU.add).then_inc(added, 16)
                        pool_wait(pool, added, g * 32 + 32)
                        pool.sem_inc(y_sent, 1)
                        with pool.If(i * E + e < E - 2):
                            pool_wait(pool, e_low, e * 2 + 4)
                            load_weights(pool, nc.s_assert_within(e + 2, 2, E - 1,
                                                                  skip_runtime_bounds_check_because="the If"))

                    every_block(pool, send)

                @block.vector
                def _(dve):
                    dve.sem_inc(y_read, 2)

                    def take(g):
                        dve.wait_ge(x_psum, g + 1)
                        dve.wait_ge(xT_high, g + 1)
                        low(nc.vector, xTp[1][:].rearrange("p k n -> p (k n)"), PS[:, 4, :],
                            xTp[0][:].rearrange("p k n -> p (k n)")).then_inc(xT_ready, 1)
                        nc.vector.tensor_copy(meta[:], xr[:, :, D:ROW]).then_inc(xr_free, 1)

                    def one(g, e, par, i):
                        for j in range(KH):
                            dve.wait_ge(h_ready, g * KH + j + 1 + HELD)
                            low(nc.vector, hid[1][:, j, :], act32[:, j % 2, :], hid[0][:, j, :]).then_inc(l_ready, 1)
                        dve.wait_ge(xr_free, g + 2)
                        dve.wait_ge(y_sent, g + 1)
                        nc.vector.tensor_copy(gate[:], meta[:, :, bass.ds(e, 1)].rearrange("p h a -> p (h a)"))
                        nc.vector.tensor_copy(toki[:], meta[:, :, E]).then_inc(gate_ready, 1)
                        dve.wait_ge(gate_ready, g + 1)
                        take(g + 1)
                        for h in range(2):
                            dve.wait_ge(y_psum, g * 2 + h + 1)
                            nc.vector.tensor_tensor(y[:, h, :], PS[:, 5 + h, 0:D],
                                                    bpr[:, bass.ds(e, 1), :].rearrange("p a d -> p (a d)"),
                                                    ALU.add).then_inc(y_read, 1)
                        for h in range(2):
                            dve.wait_ge(y_read, g * 2 + 3 + h)
                            nc.vector.tensor_scalar(y[:, h, :], y[:, h, :], gate[:, h:h + 1], None,
                                                    ALU.mult).then_inc(y_ready, 1)
                        with dve.If(i * E + e < E - 1):
                            dve.wait_ge(e_high, e * 2 + 4)
                            low(nc.vector, wfc[1][:, 1 - par], fcraw[:], wfc[0][:, 1 - par]).then_inc(e_low, 1)
                            low(nc.vector, wpr[1][:, 1 - par], prraw[:], wpr[0][:, 1 - par]).then_inc(e_low, 1)

                    dve.sem_inc(xr_free, 1)
                    dve.sem_inc(l_ready, 2)
                    take(0)
                    dve.wait_ge(b_in, 16)
                    every_block(dve, one)


def kernel(x, ctx_1024, L0_attn_W_in, L0_attn_conv_w, L0_attn_conv_b, L0_attn_W_x, L0_attn_W_dt, L0_attn_b_dt,
           L0_attn_A_log, L0_attn_D_skip, L0_attn_W_out, L0_xattn_Wq, L0_xattn_bq, L0_xattn_Wk, L0_xattn_bk,
           L0_xattn_Wv, L0_xattn_bv, L0_xattn_Wo, L0_xattn_bo, L0_ffn_Wfc_s, L0_ffn_bfc_s, L0_ffn_Wproj_s,
           L0_ffn_bproj_s, L0_ffn_Wr, L0_ffn_Wfc, L0_ffn_bfc, L0_ffn_Wproj, L0_ffn_bproj):
    import numpy as np
    import concourse.bacc as bacc
    from concourse import mybir
    from concourse.bass_utils import run_bass_kernel_spmd

    nd = np.asarray
    P = 128
    Bb, L, D = nd(x).shape
    S = nd(ctx_1024).shape[1]
    E, _, HID = nd(L0_ffn_Wfc).shape
    ROOM = Bb * L + 2 * P
    EI = nd(L0_attn_W_out).shape[1]
    HH = 8

    small = np.zeros((P, 64), np.float32)
    small[:, 0:HH] = np.arange(P)[:, None] // 16 == np.arange(HH)[None, :]
    small[:, 8:8 + E] = E - np.arange(E)
    small[:, 16] = np.arange(P)
    small[:, 17] = np.arange(P) + P
    small[:, 24:24 + E] = np.arange(E) * ROOM
    small[:, 32:40] = 1e-5
    small[:, 40:48] = -0.5
    causal = np.where(np.arange(S)[None, :] > np.arange(P)[:, None], np.float32(-1e30), np.float32(0))
    arrays = {
        "x": nd(x),
        "ctxT": np.ascontiguousarray(nd(ctx_1024).reshape(Bb * S, D).T).reshape(D // P, P, Bb * S),
        "W_inT": nd(L0_attn_W_in)[EI:].T, "W_xT": nd(L0_attn_W_x).T, "W_dtT": nd(L0_attn_W_dt).T,
        "b_dt": nd(L0_attn_b_dt).reshape(-1, P).T, "D_skip": nd(L0_attn_D_skip).reshape(-1, P).T,
        "A_log": nd(L0_attn_A_log), "W_outT": nd(L0_attn_W_out).T,
        "Wq": nd(L0_xattn_Wq), "Wk": nd(L0_xattn_Wk), "Wv": nd(L0_xattn_Wv), "Wo": nd(L0_xattn_Wo),
        "bq": nd(L0_xattn_bq).reshape(-1, P).T, "bk": nd(L0_xattn_bk).reshape(-1, P).T,
        "bv": nd(L0_xattn_bv).reshape(1, -1), "bo": nd(L0_xattn_bo).reshape(1, -1),
        "Wfc_s": nd(L0_ffn_Wfc_s), "bfc_s": nd(L0_ffn_bfc_s).reshape(-1, P).T,
        "Wproj_s": nd(L0_ffn_Wproj_s), "bproj_s": nd(L0_ffn_bproj_s).reshape(1, -1),
        "Wr": nd(L0_ffn_Wr), "Wfc": nd(L0_ffn_Wfc), "bfc": nd(L0_ffn_bfc).reshape(E, -1, P).transpose(2, 0, 1),
        "Wproj": nd(L0_ffn_Wproj), "bproj": nd(L0_ffn_bproj).reshape(1, -1),
        "ident": np.eye(P, dtype=np.float32),
        "tri": np.triu(np.ones((P, P), np.float32), 1),
        "small": small, "causal": np.tile(causal, (1, HH)),
        "steps": np.tile(np.arange(1, L, dtype=np.float32), (P, 1)),
    }
    nc = bacc.Bacc("TRN2", target_bir_lowering=False, num_devices=1)
    feeds, aps = {}, {}
    for name, a in arrays.items():
        a = np.ascontiguousarray(a)
        feeds["in_" + name] = a
        aps[name] = nc.dram_tensor("in_" + name, a.shape, mybir.dt.from_np(a.dtype), kind="ExternalInput").ap()
    aps["out"] = nc.dram_tensor("out_rows", (ROOM, D), mybir.dt.float32, kind="ExternalOutput").ap()
    build(nc, aps)
    r = run_bass_kernel_spmd(nc, [feeds], core_ids=[0])
    return r.results[0]["out_rows"][:Bb * L].reshape(Bb, L, D)
```
